# Optimizing a Trainium2 kernel written in Bass

```python
import numpy as np
import jax
import jax.numpy as jnp

def _softmax(x, axis=-1):
    return jax.nn.softmax(x, axis=axis)

def _gelu(x):
    return jax.nn.gelu(x, approximate=True)

def _silu(x):
    return jax.nn.silu(x)

def _sigmoid(x):
    return jax.nn.sigmoid(x)

def _layernorm(x, axis=-1, eps=1e-05):
    m = jnp.mean(x, axis=axis, keepdims=True)
    v = jnp.var(x, axis=axis, keepdims=True)
    return (x - m) / jnp.sqrt(v + eps)

def _scatter_add(tgt, idx, src, axis=0):
    return tgt.at[idx].add(src)

def _segment_sum(src, seg, n):
    return jax.ops.segment_sum(src, seg, n)
kernel_name = 'mk_decoder_preln_d2_seqx_r4_344810'

def setup_inputs(seed: int=0):
    np.random.seed(seed)
    _w = jnp.asarray

    def _rec_inputs():
        import jax
        import jax.numpy as jnp
        _rk = jax.random.key(seed)
        x = 7.22e-05 + 1 * jax.random.normal(jax.random.fold_in(_rk, 1), (4, 512, 512), jnp.float32)
        _lenS = 512 - jax.random.randint(jax.random.fold_in(_rk, 7), (4,), 0, max(1, 512 // 4) + 1, jnp.int32)
        _lenS2 = 512 - jax.random.randint(jax.random.fold_in(_rk, 8), (4,), 0, max(1, 512 // 4) + 1, jnp.int32)
        _ctx_1024P = jax.random.normal(jax.random.fold_in(_rk, 11), (4, 16, 256), jnp.float32)
        _ctx_1024c = jax.random.dirichlet(jax.random.fold_in(_rk, 511), 0.3 * jnp.ones((16,), jnp.float32), (4, 512))
        _ctx_1024t = jnp.einsum('bsk,bkd->bsd', _ctx_1024c, _ctx_1024P)
        _ctx_1024t = _ctx_1024t * jax.lax.rsqrt(jnp.mean(jnp.square(_ctx_1024t)) + 1e-12) * 0.953939
        ctx_1024 = 2.81802e-05 + 1.00001 * (_ctx_1024t + 0.3 * jax.random.normal(jax.random.fold_in(_rk, 611), (4, 512, 256), jnp.float32))
        _validS = jnp.arange(512)[None, :] < _lenS[:, None]
        _validS2 = jnp.arange(512)[None, :] < _lenS2[:, None]
        _causal = jnp.tril(jnp.ones((512, 512), dtype=bool))
        mask_BxS2_bf1 = jnp.ones((4, 512), dtype=bool)
        return (x, ctx_1024, mask_BxS2_bf1)
    x, ctx_1024, mask_BxS2_bf1 = _rec_inputs()

    def _L0_attn_setup():
        import jax, jax.numpy as jnp
        import numpy as np
        D_MODEL = 512
        NUM_HEADS = 16
        HEAD_DIM = D_MODEL // NUM_HEADS
        B, L = (2, 512)
        key = jax.random.key(seed)
        ks = jax.random.split(key, 7)
        s = 0.02
        return {'x': jax.random.normal(ks[0], (B, L, D_MODEL), dtype=jnp.float32), 'Wq_w': jax.random.normal(ks[1], (D_MODEL, D_MODEL), dtype=jnp.float32) * s, 'Wq_b': jnp.zeros((D_MODEL,), dtype=jnp.float32), 'Wk_w': jax.random.normal(ks[2], (HEAD_DIM, D_MODEL), dtype=jnp.float32) * s, 'Wk_b': jnp.zeros((HEAD_DIM,), dtype=jnp.float32), 'Wv_w': jax.random.normal(ks[3], (HEAD_DIM, D_MODEL), dtype=jnp.float32) * s, 'Wv_b': jnp.zeros((HEAD_DIM,), dtype=jnp.float32)}
    _L0_attn_all = _L0_attn_setup()
    _L0_attn_in = {k: v for k, v in _L0_attn_all.items() if k in ('Wq_w', 'Wq_b', 'Wk_w', 'Wk_b', 'Wv_w', 'Wv_b')}
    del _L0_attn_all

    def _L0_xattn_setup():
        import jax, jax.numpy as jnp
        import numpy as np
        key = jax.random.key(seed)
        ks = jax.random.split(key, 6)
        B, L, N, C, D = (8, 128, 512, 256, 128)
        return {'teacher_logits': jax.random.normal(ks[0], (B, L, N), dtype=jnp.float32), 'teacher_features': jax.random.normal(ks[1], (B, N, C), dtype=jnp.float32), 'Wq': jax.random.normal(ks[2], (D, C), dtype=jnp.float32) * (1.0 / np.sqrt(C)), 'bq': jnp.zeros((D,), dtype=jnp.float32), 'Wk': jax.random.normal(ks[3], (D, C), dtype=jnp.float32) * (1.0 / np.sqrt(C)), 'bk': jnp.zeros((D,), dtype=jnp.float32)}
    _L0_xattn_all = _L0_xattn_setup()
    _L0_xattn_in = {k: v for k, v in _L0_xattn_all.items() if k in ('Wq', 'bq', 'Wk', 'bk')}
    del _L0_xattn_all

    def _L0_ffn_setup():
        import jax, jax.numpy as jnp
        import numpy as np
        _FP4_LUT = jnp.array([0.0, 0.5, 1.0, 1.5, 2.0, 3.0, 4.0, 6.0, -0.0, -0.5, -1.0, -1.5, -2.0, -3.0, -4.0, -6.0], dtype=jnp.float32)
        GROUP_SIZE = 128
        EPS = 1e-06

        def _dequant_fp4(packed_i32, scales_f16, group_size):
            out_f, in_p = packed_i32.shape
            w = packed_i32.astype(jnp.uint32)
            shifts = jnp.arange(8, dtype=jnp.uint32) * 4
            nib = w[:, :, None] >> shifts & jnp.uint32(15)
            vals = _FP4_LUT[nib.astype(jnp.int32)].reshape(out_f, in_p * 8)
            s = scales_f16.astype(jnp.float32).T
            s_full = jnp.repeat(s, group_size, axis=1)
            return vals * s_full
        key = jax.random.key(seed)
        k1, k2, k3, k4, k5 = jax.random.split(key, 5)
        B, S, H, I = (4, 512, 512, 1408)
        x = jax.random.normal(k1, (B, S, H), dtype=jnp.float32)
        gate_up_packed = jax.random.randint(k2, (2 * I, H // 8), 0, 2147483647, dtype=jnp.int32)
        gate_up_scales = jax.random.uniform(k3, (H // GROUP_SIZE, 2 * I), dtype=jnp.float32).astype(jnp.float16)
        down_packed = jax.random.randint(k4, (H, I // 8), 0, 2147483647, dtype=jnp.int32)
        down_scales = jax.random.uniform(k5, (I // GROUP_SIZE, H), dtype=jnp.float32).astype(jnp.float16)
        return {'x': x, 'gate_up_packed': gate_up_packed, 'gate_up_scales': gate_up_scales, 'down_packed': down_packed, 'down_scales': down_scales}
    _L0_ffn_all = _L0_ffn_setup()
    _L0_ffn_in = {k: v for k, v in _L0_ffn_all.items() if k in ('gate_up_packed', 'gate_up_scales', 'down_packed', 'down_scales')}
    del _L0_ffn_all

    def _L1_attn_setup():
        import jax, jax.numpy as jnp
        import numpy as np
        B, S, D, H = (2, 512, 512, 16)
        HD = D // H
        key = jax.random.key(seed)
        ks = jax.random.split(key, 5)
        scale = 0.02
        return {'hidden_states': jax.random.normal(ks[0], (B, S, D), dtype=jnp.float32), 'Wqkv_w': jax.random.normal(ks[1], (3 * D, D), dtype=jnp.float32) * scale, 'Wqkv_b': jax.random.normal(ks[2], (3 * D,), dtype=jnp.float32) * scale, 'out_w': jax.random.normal(ks[3], (D, D), dtype=jnp.float32) * scale, 'out_b': jax.random.normal(ks[4], (D,), dtype=jnp.float32) * scale}
    _L1_attn_all = _L1_attn_setup()
    _L1_attn_in = {k: v for k, v in _L1_attn_all.items() if k in ('Wqkv_w', 'Wqkv_b', 'out_w', 'out_b')}
    del _L1_attn_all

    def _L1_xattn_setup():
        import jax, jax.numpy as jnp
        import numpy as np
        N_HEADS = 16
        N_KV_HEADS = 8
        HEAD_DIM = 128
        D_TEXT = 512
        D_VISION = 256
        GROUPS = N_HEADS // N_KV_HEADS
        key = jax.random.key(seed)
        ks = jax.random.split(key, 6)
        B, T_text, T_vis = (4, 512, 144)
        text_hidden = jax.random.normal(ks[0], (B, T_text, D_TEXT), dtype=jnp.float32)
        vision_tokens = jax.random.normal(ks[1], (B, T_vis, D_VISION), dtype=jnp.float32)
        vision_mask = jnp.ones((B, T_vis), dtype=bool)
        s = 0.02
        Wq = jax.random.normal(ks[2], (D_TEXT, N_HEADS * HEAD_DIM), dtype=jnp.float32) * s
        Wk = jax.random.normal(ks[3], (D_VISION, N_KV_HEADS * HEAD_DIM), dtype=jnp.float32) * s
        Wv = jax.random.normal(ks[4], (D_VISION, N_KV_HEADS * HEAD_DIM), dtype=jnp.float32) * s
        Wo = jax.random.normal(ks[5], (N_HEADS * HEAD_DIM, D_TEXT), dtype=jnp.float32) * s
        return {'text_hidden': text_hidden, 'vision_tokens': vision_tokens, 'vision_mask': vision_mask, 'Wq': Wq, 'Wk': Wk, 'Wv': Wv, 'Wo': Wo}
    _L1_xattn_all = _L1_xattn_setup()
    _L1_xattn_in = {k: v for k, v in _L1_xattn_all.items() if k in ('Wq', 'Wk', 'Wv', 'Wo')}
    del _L1_xattn_all

    def _L1_ffn_setup():
        import jax, jax.numpy as jnp
        import numpy as np
        TOPK = 2
        key = jax.random.key(seed)
        ks = jax.random.split(key, 6)
        B, T, H, S, r, ad = (2, 1024, 512, 32, 16, 32)
        h = jax.random.normal(ks[0], (B, T, H), dtype=jnp.float32)
        Wr = jax.random.normal(ks[1], (S, H), dtype=jnp.float32) * 0.02
        U = jax.random.normal(ks[2], (S, H, r), dtype=jnp.float32) * 0.02
        V = jax.random.normal(ks[3], (S, r, H), dtype=jnp.float32) * 0.02
        attr = jax.random.normal(ks[4], (S, ad), dtype=jnp.float32) * 0.02
        Wa = jax.random.normal(ks[5], (1, ad), dtype=jnp.float32) * 0.02
        return {'h': h, 'Wr': Wr, 'U': U, 'V': V, 'attr': attr, 'Wa': Wa}
    _L1_ffn_all = _L1_ffn_setup()
    _L1_ffn_in = {k: v for k, v in _L1_ffn_all.items() if k in ('Wr', 'U', 'V', 'attr', 'Wa')}
    del _L1_ffn_all
    return {'x': x, 'ctx_1024': ctx_1024, 'mask_BxS2_bf1': mask_BxS2_bf1, 'L0_attn_Wq_w': _L0_attn_in['Wq_w'], 'L0_attn_Wq_b': _L0_attn_in['Wq_b'], 'L0_attn_Wk_w': _L0_attn_in['Wk_w'], 'L0_attn_Wk_b': _L0_attn_in['Wk_b'], 'L0_attn_Wv_w': _L0_attn_in['Wv_w'], 'L0_attn_Wv_b': _L0_attn_in['Wv_b'], 'L0_xattn_Wq': _L0_xattn_in['Wq'], 'L0_xattn_bq': _L0_xattn_in['bq'], 'L0_xattn_Wk': _L0_xattn_in['Wk'], 'L0_xattn_bk': _L0_xattn_in['bk'], 'L0_ffn_gate_up_packed': _L0_ffn_in['gate_up_packed'], 'L0_ffn_gate_up_scales': _L0_ffn_in['gate_up_scales'], 'L0_ffn_down_packed': _L0_ffn_in['down_packed'], 'L0_ffn_down_scales': _L0_ffn_in['down_scales'], 'L1_attn_Wqkv_w': _L1_attn_in['Wqkv_w'], 'L1_attn_Wqkv_b': _L1_attn_in['Wqkv_b'], 'L1_attn_out_w': _L1_attn_in['out_w'], 'L1_attn_out_b': _L1_attn_in['out_b'], 'L1_xattn_Wq': _L1_xattn_in['Wq'], 'L1_xattn_Wk': _L1_xattn_in['Wk'], 'L1_xattn_Wv': _L1_xattn_in['Wv'], 'L1_xattn_Wo': _L1_xattn_in['Wo'], 'L1_ffn_Wr': _L1_ffn_in['Wr'], 'L1_ffn_U': _L1_ffn_in['U'], 'L1_ffn_V': _L1_ffn_in['V'], 'L1_ffn_attr': _L1_ffn_in['attr'], 'L1_ffn_Wa': _L1_ffn_in['Wa']}

def reference(x, ctx_1024, mask_BxS2_bf1, L0_attn_Wq_w, L0_attn_Wq_b, L0_attn_Wk_w, L0_attn_Wk_b, L0_attn_Wv_w, L0_attn_Wv_b, L0_xattn_Wq, L0_xattn_bq, L0_xattn_Wk, L0_xattn_bk, L0_ffn_gate_up_packed, L0_ffn_gate_up_scales, L0_ffn_down_packed, L0_ffn_down_scales, L1_attn_Wqkv_w, L1_attn_Wqkv_b, L1_attn_out_w, L1_attn_out_b, L1_xattn_Wq, L1_xattn_Wk, L1_xattn_Wv, L1_xattn_Wo, L1_ffn_Wr, L1_ffn_U, L1_ffn_V, L1_ffn_attr, L1_ffn_Wa):
    import jax
    import jax.numpy as jnp

    def _L0_attn_ref(x, Wq_w, Wq_b, Wk_w, Wk_b, Wv_w, Wv_b):
        import jax, jax.numpy as jnp
        import numpy as np
        D_MODEL = 512
        NUM_HEADS = 16
        HEAD_DIM = D_MODEL // NUM_HEADS
        B, L = (2, 512)
        b, l, _ = x.shape
        Q = (x @ Wq_w.T + Wq_b).reshape(b, l, NUM_HEADS, HEAD_DIM)
        K = x @ Wk_w.T + Wk_b
        V = x @ Wv_w.T + Wv_b
        scale = 1.0 / jnp.sqrt(jnp.float32(HEAD_DIM))
        scores = jnp.einsum('bqhd,bkd->bhqk', Q, K) * scale
        attn = jax.nn.softmax(scores, axis=-1)
        out = jnp.einsum('bhqk,bkd->bqhd', attn, V)
        return out.reshape(b, l, D_MODEL)

    def _L0_xattn_ref(teacher_logits, teacher_features, Wq, bq, Wk, bk):
        import jax, jax.numpy as jnp
        import numpy as np
        query = jnp.einsum('bnc,dc->bnd', teacher_features, Wq) + bq
        key = jnp.einsum('bnc,dc->bnd', teacher_features, Wk) + bk
        energy = jnp.einsum('bnd,bmd->bnm', query, key)
        attention = jax.nn.softmax(energy, axis=-1)
        x_m = jnp.einsum('bln,bmn->blm', teacher_logits, attention)
        return x_m

    def _L0_ffn_ref(x, gate_up_packed, gate_up_scales, down_packed, down_scales):
        import jax, jax.numpy as jnp
        import numpy as np
        _FP4_LUT = jnp.array([0.0, 0.5, 1.0, 1.5, 2.0, 3.0, 4.0, 6.0, -0.0, -0.5, -1.0, -1.5, -2.0, -3.0, -4.0, -6.0], dtype=jnp.float32)
        GROUP_SIZE = 128
        EPS = 1e-06

        def _dequant_fp4(packed_i32, scales_f16, group_size):
            out_f, in_p = packed_i32.shape
            w = packed_i32.astype(jnp.uint32)
            shifts = jnp.arange(8, dtype=jnp.uint32) * 4
            nib = w[:, :, None] >> shifts & jnp.uint32(15)
            vals = _FP4_LUT[nib.astype(jnp.int32)].reshape(out_f, in_p * 8)
            s = scales_f16.astype(jnp.float32).T
            s_full = jnp.repeat(s, group_size, axis=1)
            return vals * s_full
        I = gate_up_packed.shape[0] // 2
        w_gu = _dequant_fp4(gate_up_packed, gate_up_scales, GROUP_SIZE)
        w_down = _dequant_fp4(down_packed, down_scales, GROUP_SIZE)
        gate_up = jnp.einsum('bsh,oh->bso', x, w_gu)
        gate, up = (gate_up[..., :I], gate_up[..., I:])
        h = jax.nn.silu(gate) * up
        y = jnp.einsum('bsi,hi->bsh', h, w_down)
        rms = jnp.sqrt(jnp.mean(y * y, axis=-1, keepdims=True) + EPS)
        return y / rms

    def _L1_attn_ref(hidden_states, Wqkv_w, Wqkv_b, out_w, out_b):
        import jax, jax.numpy as jnp
        import numpy as np
        B, S, D, H = (2, 512, 512, 16)
        HD = D // H
        b, s, d = hidden_states.shape
        qkv = hidden_states @ Wqkv_w.T + Wqkv_b
        qkv = qkv.reshape(b, s, 3, H, HD)
        q, k, v = (qkv[:, :, 0], qkv[:, :, 1], qkv[:, :, 2])
        softmax_scale = 1.0 / np.float32(np.sqrt(HD))
        scores = jnp.einsum('bthd,bshd->bhts', q, k) * softmax_scale
        attn = jax.nn.softmax(scores, axis=-1)
        ctx = jnp.einsum('bhts,bshd->bthd', attn, v)
        ctx = ctx.reshape(b, s, d)
        return ctx @ out_w.T + out_b

    def _L1_xattn_ref(text_hidden, vision_tokens, vision_mask, Wq, Wk, Wv, Wo):
        import jax, jax.numpy as jnp
        import numpy as np
        N_HEADS = 16
        N_KV_HEADS = 8
        HEAD_DIM = 128
        D_TEXT = 512
        D_VISION = 256
        GROUPS = N_HEADS // N_KV_HEADS
        B, T_text, _ = text_hidden.shape
        T_vis = vision_tokens.shape[1]
        scale = jnp.float32(np.sqrt(HEAD_DIM))
        q = (text_hidden @ Wq).reshape(B, T_text, N_HEADS, HEAD_DIM).transpose(0, 2, 1, 3)
        k = (vision_tokens @ Wk).reshape(B, T_vis, N_KV_HEADS, HEAD_DIM).transpose(0, 2, 1, 3)
        v = (vision_tokens @ Wv).reshape(B, T_vis, N_KV_HEADS, HEAD_DIM).transpose(0, 2, 1, 3)
        k = jnp.repeat(k, GROUPS, axis=1)
        v = jnp.repeat(v, GROUPS, axis=1)
        scores = jnp.einsum('bhtd,bhsd->bhts', q, k) / scale
        mask = vision_mask[:, None, None, :]
        scores = jnp.where(mask, scores, -jnp.inf)
        attn = jax.nn.softmax(scores, axis=-1)
        attn = jnp.nan_to_num(attn, nan=0.0)
        out = jnp.einsum('bhts,bhsd->bhtd', attn, v)
        out = out.transpose(0, 2, 1, 3).reshape(B, T_text, N_HEADS * HEAD_DIM)
        return out @ Wo

    def _L1_ffn_ref(h, Wr, U, V, attr, Wa):
        import jax, jax.numpy as jnp
        import numpy as np
        TOPK = 2
        S = Wr.shape[0]
        sc = jnp.einsum('bth,sh->bts', h, Wr)
        _, idx = jax.lax.top_k(sc, TOPK)
        m = jax.nn.one_hot(idx, S, dtype=sc.dtype).sum(axis=-2)
        g = jax.nn.softmax(sc, axis=-1) * m
        g = g / (g.sum(axis=-1, keepdims=True) + 1e-08)
        hU = jnp.einsum('bth,shr->btsr', h, U)
        out = jnp.einsum('bts,btsr,srh->bth', g, hU, V)
        aw = jax.nn.sigmoid(attr @ Wa[0])
        gate = (g @ aw)[..., None]
        return out * (0.9 + 0.2 * gate)
    x = x + _L0_attn_ref(_layernorm(x, axis=-1), L0_attn_Wq_w, L0_attn_Wq_b, L0_attn_Wk_w, L0_attn_Wk_b, L0_attn_Wv_w, L0_attn_Wv_b)
    x = x + _L0_xattn_ref(_layernorm(x, axis=-1), ctx_1024, L0_xattn_Wq, L0_xattn_bq, L0_xattn_Wk, L0_xattn_bk)
    x = x + _L0_ffn_ref(_layernorm(x, axis=-1), L0_ffn_gate_up_packed, L0_ffn_gate_up_scales, L0_ffn_down_packed, L0_ffn_down_scales)
    x = x + _L1_attn_ref(_layernorm(x, axis=-1), L1_attn_Wqkv_w, L1_attn_Wqkv_b, L1_attn_out_w, L1_attn_out_b)
    x = x + _L1_xattn_ref(_layernorm(x, axis=-1), ctx_1024, mask_BxS2_bf1, L1_xattn_Wq, L1_xattn_Wk, L1_xattn_Wv, L1_xattn_Wo)
    x = x + _L1_ffn_ref(_layernorm(x, axis=-1), L1_ffn_Wr, L1_ffn_U, L1_ffn_V, L1_ffn_attr, L1_ffn_Wa)
    return x

_drawn_inputs = setup_inputs


def setup_inputs(seed=0):
    import zlib

    import numpy as np

    out = dict(_drawn_inputs(seed))
    spreads = {'L0_attn_Wq_b': (0.0, 0.8),
     'L0_attn_Wk_b': (0.0, 0.8),
     'L0_attn_Wv_b': (0.0, 0.1),
     'L0_xattn_bq': (0.0, 0.1),
     'L0_xattn_bk': (0.0, 0.8)}
    factors = {'L0_attn_Wq_w': 7.305,
     'L0_attn_Wk_w': 6.888,
     'L1_attn_Wqkv_w': 3.719,
     'L1_attn_Wqkv_b': 8.0,
     'L1_attn_out_w': 3.514,
     'L1_attn_out_b': 4.644,
     'L1_xattn_Wq': 8.0,
     'L1_xattn_Wk': 8.0,
     'L1_ffn_Wr': 3.694,
     'L1_ffn_U': 3.539,
     'L1_ffn_V': 3.553,
     'L1_ffn_attr': 8.0,
     'L1_ffn_Wa': 8.0}
    for name, (base, spread) in spreads.items():
        noise = np.random.default_rng([zlib.crc32(name.encode()), seed]).standard_normal(out[name].shape)
        drawn = base * np.exp(spread * noise) if base else spread * noise
        out[name] = jnp.asarray(drawn.astype(out[name].dtype))
    for name, factor in factors.items():
        out[name] = (out[name] * factor).astype(out[name].dtype)
    return out
```

```python
from contextlib import ExitStack

import concourse.bass as bass
from concourse import mybir

P = 128
F32 = mybir.dt.float32
F32R = mybir.dt.float32r
BF16 = mybir.dt.bfloat16
F16 = mybir.dt.float16
I32 = mybir.dt.int32
U32 = mybir.dt.uint32
U8 = mybir.dt.uint8
ALU = mybir.AluOpType
ACT = mybir.ActivationFunctionType
AX = mybir.AxisListType

B, S, D = 4, 512, 512
QT = S // P
T = B * QT
KC = D // P
TOK = B * S
NH, HD = 16, 32
C = 256
CC = C // P


class State:

    def __init__(self, nc, ctx):
        self.nc, self.ctx, self.used, self.taken = nc, ctx, 0, []

    def sem(self, name):
        self.used += 1
        self.taken.append(self.nc.alloc_semaphore(name=f"{name}_{self.used}"))
        return self.taken[-1]

    def stage(self, build, *args):
        build(self, *args)
        self.nc.all_engine_barrier()
        self.nc.clear_and_free_semaphores(self.taken)
        self.nc.all_engine_barrier()
        self.taken = []

    def sems(self, *names):
        return [self.sem(n) for n in names]


def tensors(nc, stack):
    def sb(name, shape, dt):
        return stack.enter_context(nc.sbuf_tensor(name, shape, dt))

    def ps(name, shape, dt=F32):
        return stack.enter_context(nc.psum_tensor(name, shape, dt))

    return sb, ps


def setup(st, x_in):
    nc = st.nc
    x_loaded, zeroed, made = st.sems("x_loaded", "ident_zeroed", "ident_made")
    with nc.Block() as block:

        @block.sync
        def _(sp):
            sp.dma_start(st.x[:], x_in.rearrange("b (q p) d -> p (b q) d", p=P)).then_inc(x_loaded, 16)
            sp.wait_ge(x_loaded, 16)

        @block.gpsimd
        def _(pool):
            pool.memset(st.ident[:], 0.0).then_inc(zeroed, 1)
            pool.wait_ge(zeroed, 1)
            pool.affine_select(out=st.ident[:], in_=st.ident[:], compare_op=ALU.not_equal, fill=1.0, base=0,
                               pattern=[[-1, P]], channel_multiplier=1).then_inc(made, 1)

        @block.vector
        def _(dve):
            dve.wait_ge(made, 1)
            dve.tensor_copy(st.ident_r[:], st.ident[:])


def weight_prep(st, name, loads, jobs, fills=()):
    nc = st.nc
    loaded, filled, turned, hi_done, lo_done = st.sems("w_loaded", "w_filled", "w_turned", "w_hi", "w_lo")
    with ExitStack() as stack:
        sb, ps = tensors(nc, stack)
        bank = ps(f"{name}_banks", [P, 2, 512])
        with nc.Block() as block:

            @block.sync
            def _(sp):
                if fills:
                    sp.wait_ge(filled, len(fills))
                for dst, src in loads:
                    sp.dma_start(dst, src, allow_slow_non_contiguous=dst.shape[-1] <= 16).then_inc(loaded, 16)

            @block.gpsimd
            def _(pool):
                for t in fills:
                    pool.memset(t, 0.0).then_inc(filled, 1)

            @block.tensor
            def _(pe):
                pe.wait_ge(loaded, 16 * len(loads))
                for j, (sources, hi, lo) in enumerate(jobs):
                    if j >= 2:
                        pe.wait_ge(lo_done, j - 1)
                    at = 0
                    for s in sources:
                        rows, cols = s.shape
                        last = pe.transpose(bank[0:cols, j % 2, at:at + rows], s, st.ident[0:rows, 0:rows])
                        at += rows
                    last.then_inc(turned, 1)

            def view(j):
                sources, hi, lo = jobs[j]
                n = sum(s.shape[0] for s in sources)
                v = bank[0:sources[0].shape[1], j % 2, 0:n]
                if len(hi.shape) == 3:
                    v = v.rearrange("p (a b) -> p a b", a=hi.shape[1])
                if len(hi.shape) == 4:
                    v = v.rearrange("p (a b c) -> p a b c", a=hi.shape[1], b=hi.shape[2])
                return v, hi, lo

            @block.scalar
            def _(act):
                if fills:
                    act.wait_ge(filled, len(fills))
                for j in range(len(jobs)):
                    v, hi, lo = view(j)
                    act.wait_ge(turned, j + 1)
                    act.activation(hi, v, ACT.Copy).then_inc(hi_done, 1)

            @block.vector
            def _(dve):
                if fills:
                    dve.wait_ge(filled, len(fills))
                for j in range(len(jobs)):
                    v, hi, lo = view(j)
                    dve.wait_ge(hi_done, j + 1)
                    if lo is None:
                        dve.sem_inc(lo_done, 1)
                    else:
                        dve.tensor_tensor(lo, v, hi.bitcast(F32), ALU.subtract).then_inc(lo_done, 1)


def norm_stats(st, dve, std_ready, var_ready, chain, bn, mv):
    n = [0]

    def link(ins, k=1):
        n[0] += k
        ins.then_inc(chain, 1)
        dve.wait_ge(chain, n[0])

    with dve.Fori(0, T - 1) as t:
        dve.bn_stats(bn[:, t, :], st.x[:, t, :]).then_inc(chain, 1)
    link(dve.bn_stats(bn[:, T - 1, :], st.x[:, T - 1, :]), T)
    mean_e, m2_e, mean_o, m2_o = (bn[:, :, k] for k in (1, 2, 4, 5))
    link(dve.tensor_tensor(mv[:, 0, :], mean_e, mean_o, ALU.add))
    link(dve.tensor_tensor(mv[:, 5, :], mean_e, mean_o, ALU.subtract))
    link(dve.tensor_tensor(mv[:, 6, :], m2_e, m2_o, ALU.add))
    link(dve.tensor_tensor(mv[:, 5, :], mv[:, 5, :], mv[:, 5, :], ALU.mult))
    link(dve.tensor_scalar(mv[:, 6, :], mv[:, 6, :], 1.0 / D, 1e-5, ALU.mult, ALU.add))
    dve.scalar_tensor_tensor(mv[:, 1, :], mv[:, 5, :], 0.25, mv[:, 6, :], ALU.mult, ALU.add).then_inc(var_ready, 1)
    dve.wait_ge(std_ready, 1)
    link(dve.reciprocal(mv[:, 3, :], mv[:, 2, :]))
    link(dve.scalar_tensor_tensor(mv[:, 4, :], mv[:, 0, :], -0.5, mv[:, 3, :], ALU.mult, ALU.mult))


def norm_to_features(st, name, source=None):
    nc = st.nc
    var_ready, std_ready, chain, xn_ready, turned, hi_done, bank_free = st.sems(
        "var_ready", "std_ready", "norm_chain", "xn_ready", "x_turned", "xT_hi_done", "x_bank_free")
    with ExitStack() as stack:
        sb, ps = tensors(nc, stack)
        bn = sb(f"{name}_bn", [P, T, 6], F32)
        mv = sb(f"{name}_mv", [P, 7, T], F32)
        xn = [sb(f"{name}_xn{s}", [P, D], F32) for s in range(2)]
        bank = [ps(f"{name}_bank{s}", [P, KC, P]) for s in range(2)]
        with nc.Block() as block:

            @block.vector
            def _(dve):
                dve.sem_inc(bank_free, 2)
                if source is None:
                    norm_stats(st, dve, std_ready, var_ready, chain, bn, mv)

                def normalise(t, s):
                    dve.wait_ge(bank_free, t + 1)
                    if source is None:
                        dve.tensor_scalar(xn[s][:], st.x[:, t, :], mv[:, 3, bass.ds(t, 1)], mv[:, 4, bass.ds(t, 1)],
                                          ALU.mult, ALU.add).then_inc(xn_ready, 1)
                    else:
                        dve.tensor_copy(xn[s][:], source[:, t, :]).then_inc(xn_ready, 1)

                def take_lo(t, s):
                    dve.wait_ge(hi_done, t + 1)
                    dve.tensor_tensor(st.xT_lo[:, :, bass.ds(t * P, P)], bank[s][:],
                                      st.xT_hi[:, :, bass.ds(t * P, P)].bitcast(F32), ALU.subtract)\
                        .then_inc(bank_free, 1)

                normalise(0, 0)
                with dve.Fori(0, T // 2 - 1) as j:
                    for s in range(2):
                        normalise(2 * j + s + 1, 1 - s)
                        take_lo(2 * j + s, s)
                normalise(T - 1, 1)
                take_lo(T - 2, 0)
                take_lo(T - 1, 1)

            @block.scalar
            def _(act):
                if source is None:
                    act.wait_ge(var_ready, 1)
                    act.activation(mv[:, 2, :], mv[:, 1, :], ACT.Sqrt).then_inc(std_ready, 1)
                with act.Fori(0, T // 2) as j:
                    for s in range(2):
                        t = 2 * j + s
                        act.wait_ge(turned, t + 1)
                        act.activation(st.xT_hi[:, :, bass.ds(t * P, P)], bank[s][:], ACT.Copy).then_inc(hi_done, 1)

            @block.tensor
            def _(pe):
                with pe.Fori(0, T // 2) as j:
                    for s in range(2):
                        t = 2 * j + s
                        pe.wait_ge(xn_ready, t + 1)
                        pe.wait_ge(bank_free, t + 1)
                        for c in range(KC):
                            last = pe.transpose(bank[s][:, c, :], xn[s][:, c * P:(c + 1) * P], st.ident[:])
                        last.then_inc(turned, 1)


def project(st, name, wT_hi, wT_lo, bias, kinds, q_dram, k_dram, v, vh):
    nc = st.nc
    NT = len(kinds)
    NV = kinds.count("v")
    NQK = NT - NV
    assert NT % 2 == 0 and all(k == "v" for k in kinds[NQK:])
    in_slot = [len(range(s, NQK, 2)) for s in range(2)]
    rows = vh * HD
    V_LAG = min(NV, 2)
    projected, hi_done, lo_done, vT_ready, v_turned, v_read = st.sems(
        "projected", "hi_done", "lo_done", "vT_ready", "v_turned", "v_read")
    stored = st.sems("stored_0", "stored_1")
    with ExitStack() as stack:
        sb, ps = tensors(nc, stack)
        hi = [sb(f"{name}_hi{s}", [P, S], F32R) for s in range(2)]
        lo = [sb(f"{name}_lo{s}", [P, S], F32R) for s in range(2)]
        vT = [sb(f"{name}_vT{s}", [P, S], F32) for s in range(2)]
        bank = [ps(f"{name}_bank{s}", [P, S]) for s in range(2)]
        v_bank = ps(f"{name}_v_bank", [P, QT, P])

        with nc.Block() as block:

            @block.tensor
            def _(pe):
                pe.sem_inc(v_turned, 2)
                with pe.Fori(0, B) as b:
                    def turn_v(n):
                        pe.wait_ge(vT_ready, b * NV + n + 3)
                        pe.wait_ge(v_read, b * NV + n + 1)
                        for q in range(QT):
                            last = pe.transpose(v_bank[:, q, :], vT[n % 2][:, q * P:(q + 1) * P], st.ident[:])
                        last.then_inc(v_turned, 1)

                    for f in range(NT):
                        g = (f - 2) % NT
                        back = 1 if f < 2 else 0
                        if g < NQK:
                            pe.wait_ge(lo_done, (b - back + 1) * NQK + g + 1)
                        else:
                            pe.wait_ge(vT_ready, (b - back) * NV + g - NQK + 3)
                        n = 0
                        for c in range(KC):
                            for w, m in ((wT_hi, st.xT_hi), (wT_hi, st.xT_lo), (wT_lo, st.xT_hi)):
                                last = pe.matmul(bank[f % 2][:], w[:, c, f * P:(f + 1) * P],
                                                 m[:, c, bass.ds(b * S, S)], start=(n == 0), stop=(n == 3 * KC - 1))
                                n += 1
                        last.then_inc(projected, 1)
                        if f > NQK:
                            turn_v(f - 1 - NQK)
                    turn_v(NV - 1)

            @block.scalar
            def _(act):
                act.sem_inc(vT_ready, 2)
                with act.Fori(0, B) as b:
                    for f in range(NT):
                        act.wait_ge(projected, b * NT + f + 1)
                        if f >= NQK:
                            n = f - NQK
                            act.wait_ge(v_turned, b * NV + n + 3 - V_LAG)
                            act.activation(vT[n % 2][:], bank[f % 2][:], ACT.Identity,
                                           bias=bias[:, f:f + 1]).then_inc(vT_ready, 1)
                        else:
                            act.wait_ge(stored[f % 2], 32 * (b * in_slot[f % 2] + f // 2) + 32)
                            act.activation(hi[f % 2][:], bank[f % 2][:], ACT.Identity,
                                           bias=bias[:, f:f + 1]).then_inc(hi_done, 1)

            @block.vector
            def _(dve):
                dve.sem_inc(lo_done, NQK)
                dve.sem_inc(v_read, 1)
                with dve.Fori(0, B) as b:
                    for f in range(NT):
                        if f >= NQK:
                            n = f - NQK
                            dve.wait_ge(v_turned, b * NV + n + 3)
                            for q in range(QT):
                                last = dve.tensor_copy(v[:, b * QT + q, n * vh:(n + 1) * vh, 0:HD],
                                                       v_bank[:, q, 0:rows].rearrange("p (h d) -> p h d", h=vh))
                            last.then_inc(v_read, 1)
                        else:
                            dve.wait_ge(hi_done, b * NQK + f + 1)
                            dve.scalar_tensor_tensor(lo[f % 2][:], bank[f % 2][:], bias[:, f:f + 1],
                                                     hi[f % 2][:].bitcast(F32), ALU.add, ALU.subtract)\
                                .then_inc(lo_done, 1)

            @block.sync
            def _(sp):
                for s in range(2):
                    sp.sem_inc(stored[s], 32)
                with sp.Fori(0, B) as b:
                    for f in range(NQK):
                        dram, f0 = (q_dram, f) if kinds[f] == "q" else (k_dram, f - kinds.index("k"))
                        n = min(P, dram.shape[1])
                        sp.wait_ge(lo_done, b * NQK + f + 1 + NQK)
                        for part, tile in enumerate((hi, lo)):
                            sp.dma_start(dram[part, f0 * P:f0 * P + n, bass.ds(b * S, S)], tile[f % 2][0:n, :].bitcast(F32))\
                                .then_inc(stored[f % 2], 16)
                for s in range(2):
                    sp.wait_ge(stored[s], 32 * (B * in_slot[s] + 1))


def attend(st, name, q_dram, k_dram, v, per_head, out):
    nc = st.nc
    N = B * NH
    scale = HD ** -0.5
    STK = 3 * HD
    maxed, max_read, mrow_in, mrow_turned, mrow_ready, scored, exp_done, weighed, o_read = st.sems(
        "maxed", "max_read", "mrow_in", "mrow_turned", "mrow_ready", "scored", "exp_done", "weighed", "o_read")
    turned, oT_ready = st.sems("turned", "oT_ready")
    max_hi_done, rden_done, on_done, made, v_staged, v_hi_done, split_next, pT_hi_done, pT_lo_done, cleared, \
        last_lo_done = st.sems(
        "max_hi_done", "rden_done", "on_done", "made", "v_staged", "v_hi_done", "split_next", "pT_hi_done",
        "pT_lo_done", "cleared", "last_lo_done")
    R = 4
    loaded = st.sems(*(f"qk_loaded_{s}" for s in range(R)))
    add = out is st.x
    with ExitStack() as stack:
        sb, ps = tensors(nc, stack)
        qs = [sb(f"{name}_qs{s}", [P, S], F32R) for s in range(R)]
        ks = [sb(f"{name}_ks{s}", [P, S], F32R) for s in range(R)]
        pT = [sb(f"{name}_pT{s}", [P, QT, S], F32) for s in range(2)]
        pT_hi, pT_lo = ([w[:, s, :].rearrange("p (k q) -> p k q", k=QT) for s in range(2)]
                        for w in (st.xT_hi, st.xT_lo))
        mx = sb(f"{name}_mx", [P, QT, 1], F32)
        ms = sb(f"{name}_ms", [P, QT, P], F32R)
        rden = sb(f"{name}_rden", [P, QT, 1], F32)
        on = sb(f"{name}_on", [P, QT, HD], F32)
        vs = [sb(f"{name}_vs{s}", [P, QT, P], F32R) for s in range(2)]
        OUTS = 2 * HD + 1
        fold = sb(f"{name}_fold", [OUTS, HD + 1], F32)
        max_bank = ps(f"{name}_max_bank", [P, 2, S])
        score_bank = ps(f"{name}_score_bank", [P, QT, S])
        o_bank = ps(f"{name}_o_bank", [P, 512])
        m_bank = ps(f"{name}_m_bank", [P, QT, P])
        oT = sb(f"{name}_oT", [OUTS, S], F32)
        o4 = o_bank[:, 0:QT * (HD + 1)].rearrange("p (q d) -> p q d", q=QT)

        def rounds(eng, body):
            for s in range(R):
                body(s, s)
            with eng.Fori(1, N // R - 1) as j:
                for s in range(R):
                    body(R * j + s, s)
            for s in range(R):
                body(N - R + s, s)

        with nc.Block() as block:

            @block.sync
            def _(sp):
                def load(i, s):
                    b, h = i // NH, i % NH
                    cols, rows = bass.ds(b * S, S), bass.ds(h * HD, HD)
                    krows = rows if per_head else slice(0, HD)
                    sp.dma_start(qs[s][0:HD, :].bitcast(F32), q_dram[0, rows, cols]).then_inc(loaded[s], 16)
                    sp.dma_start(qs[s][HD:3 * HD, :].bitcast(F32), q_dram[:, rows, cols]).then_inc(loaded[s], 16)
                    sp.dma_start(ks[s][0:2 * HD, :].bitcast(F32), k_dram[:, krows, cols]).then_inc(loaded[s], 16)
                    sp.dma_start(ks[s][2 * HD:3 * HD, :].bitcast(F32), k_dram[0, krows, cols]).then_inc(loaded[s], 16)

                for s in range(R):
                    load(s, s)
                with sp.Fori(1, N // R) as j:
                    for s in range(R):
                        i = R * j + s
                        sp.wait_ge(scored, 2 * (i - R + 1))
                        load(i, s)

            @block.tensor
            def _(pe):
                def maxes(i, s, half):
                    if half == 0:
                        pe.wait_ge(loaded[s], 64 // R * (i - s) + 64)
                    pe.wait_ge(max_read, 2 * i + half + 1)
                    for q in range(2):
                        c = (2 * half + q) * P
                        last = pe.matmul(max_bank[:, q, :], qs[s][0:STK, c:c + P], ks[s][0:STK, :],
                                         start=True, stop=True)
                    last.then_inc(maxed, 1)

                def max_rows(i):
                    pe.wait_ge(mrow_in, i + 1)
                    pe.wait_ge(mrow_ready, i + 1)
                    for q in range(QT):
                        last = pe.matmul(m_bank[:, q, :], ms[:, q, :], st.ident_r[:], start=True, stop=True)
                    last.then_inc(mrow_turned, 1)

                def scores(i, s, half):
                    pe.wait_ge(mrow_ready, i + 2)
                    pe.wait_ge(exp_done, 2 * i + half + 1)
                    for kt in (2 * half, 2 * half + 1):
                        last = pe.matmul(score_bank[:, kt, :], ks[s][0:STK + 2, kt * P:(kt + 1) * P],
                                         qs[s][0:STK + 2, :], start=True, stop=True)
                    last.then_inc(scored, 1)

                def weigh(i, s, half):
                    if half == 0:
                        pe.wait_ge(v_staged, i + 1)
                        pe.wait_ge(o_read, i + 1)
                    pe.wait_ge(pT_lo_done, 2 * i + half + 5)
                    if half:
                        pe.wait_ge(last_lo_done, i + 3)
                    for kt in (2 * half, 2 * half + 1):
                        for m, part in enumerate((pT_hi, pT_lo)):
                            last = pe.matmul(o_bank[:], vs[s % 2][:, kt, :], part[s % 2][:, kt, :],
                                             start=(kt == 0 and m == 0), stop=(kt == QT - 1 and m == 1))
                    if half:
                        last.then_inc(weighed, 1)

                def turn(i):
                    pe.wait_ge(oT_ready, i + 1)
                    for q in range(QT):
                        last = pe.matmul(o4[:, q, :], oT[:, q * P:(q + 1) * P], fold[:],
                                         start=True, stop=True)
                    last.then_inc(turned, 1)

                def step(i, s):
                    first, final = isinstance(i, int) and i == 0, isinstance(i, int) and i == N - 1
                    scores(i, s, 0)
                    scores(i, s, 1)
                    if not final:
                        maxes(i + 1, (s + 1) % R, 1)
                    if not first:
                        weigh(i - 1, s - 1, 0)
                        weigh(i - 1, s - 1, 1)
                    if not (isinstance(i, int) and i >= N - 2):
                        maxes(i + 2, (s + 2) % R, 0)
                    if not final:
                        max_rows(i + 1)
                    if not first:
                        turn(i - 1)

                pe.sem_inc(mrow_turned, 1)
                pe.sem_inc(weighed, 2)
                pe.wait_ge(made, 1)
                maxes(0, 0, 0)
                maxes(0, 0, 1)
                max_rows(0)
                maxes(1, 1, 0)
                rounds(pe, step)
                weigh(N - 1, 1, 0)
                weigh(N - 1, 1, 1)
                turn(N - 1)

            @block.gpsimd
            def _(pool):
                pool.sem_inc(last_lo_done, 2)
                pool.wait_ge(made, 1)
                with pool.Fori(0, N // 2) as j:
                    for s in range(2):
                        i = 2 * j + s
                        pool.wait_ge(weighed, i + 1)
                        values = v[:, bass.ds(i // NH * QT, QT), i % NH if per_head else 0, :]
                        pool.tensor_copy(vs[s][:, :, 0:HD], values).then_inc(v_hi_done, 1)
                        pool.wait_ge(v_hi_done, i + 1)
                        pool.sem_inc(split_next, 1)
                        pool.tensor_tensor(vs[s][:, :, HD:2 * HD], values, vs[s][:, :, 0:HD].bitcast(F32),
                                           ALU.subtract).then_inc(v_staged, 1)
                        pool.wait_ge(pT_hi_done, 2 * i + 2)
                        pool.tensor_tensor(pT_lo[s][:, QT - 1, :], pT[s][:, QT - 1, :],
                                           pT_hi[s][:, QT - 1, :].bitcast(F32), ALU.subtract)\
                            .then_inc(last_lo_done, 1)

            @block.scalar
            def _(act):
                act.sem_inc(exp_done, 2)
                act.sem_inc(mrow_ready, 1)

                def rows(i, s):
                    act.wait_ge(mrow_turned, i + 2)
                    act.activation(qs[s][STK:STK + 2, :], m_bank[STK:STK + 2, :, :].rearrange("p q c -> p (q c)"),
                                   ACT.Copy).then_inc(mrow_ready, 1)

                def take_oT(i):
                    act.wait_ge(weighed, i + 3)
                    act.activation(oT[:], o_bank[0:OUTS, :], ACT.Copy).then_inc(oT_ready, 1)

                def step(i, s):
                    def take_hi(half):
                        tiles = slice(2 * half, 2 * half + 2)
                        act.wait_ge(exp_done, 2 * i + half + 3)
                        act.wait_ge(weighed, i + 1)
                        act.activation(pT_hi[s % 2][:, tiles, :], pT[s % 2][:, tiles, :], ACT.Copy)\
                            .then_inc(pT_hi_done, 1)

                    for half in range(2):
                        tiles = slice(2 * half, 2 * half + 2)
                        act.wait_ge(scored, 2 * i + half + 1)
                        act.wait_ge(pT_lo_done, 2 * i + half + 1)
                        if half:
                            act.wait_ge(last_lo_done, i + 1)
                        act.activation(pT[s % 2][:, tiles, :], score_bank[:, tiles, :], ACT.Exp, scale=scale)\
                            .then_inc(exp_done, 1)
                    take_hi(0)
                    if not isinstance(i, int) or i >= 1:
                        take_oT(i - 1)
                    if not isinstance(i, int) or i < N - 1:
                        rows(i + 1, (s + 1) % R)
                    take_hi(1)

                rows(0, 0)
                rounds(act, step)
                take_oT(N - 1)

            @block.vector
            def _(dve):
                def reduce(i, half):
                    if half == 0:
                        reached(dve, mrow_in, i)
                    dve.wait_ge(maxed, 2 * i + half + 1)
                    dve.tensor_reduce(mx[:, 2 * half:2 * half + 2, 0], max_bank[:], AX.X, ALU.max)\
                        .then_inc(max_read, 1)

                def split_max(i):
                    dve.wait_ge(max_read, 2 * i + 3)
                    dve.wait_ge(mrow_turned, i + 1)
                    dve.tensor_scalar(ms[:, :, STK:STK + 1], mx[:], -1.0, None, ALU.mult).then_inc(max_hi_done, 1)
                    dve.wait_ge(max_hi_done, i + 1)
                    dve.scalar_tensor_tensor(ms[:, :, STK + 1:STK + 2], mx[:], -1.0,
                                             ms[:, :, STK:STK + 1].bitcast(F32), ALU.mult, ALU.subtract)\
                        .then_inc(mrow_in, 1)

                def invert(i):
                    dve.wait_ge(turned, i + 1)
                    dve.reciprocal(rden[:], o4[:, :, HD:HD + 1]).then_inc(rden_done, 1)

                def dest(i):
                    return out[:, bass.ds(i // NH * QT, QT), bass.ds(i % NH * HD, HD)]

                def normalise(i):
                    dve.wait_ge(rden_done, i + 1)
                    dve.tensor_tensor(on[:] if add else dest(i), o4[:, :, 0:HD], rden[:].to_broadcast([P, QT, HD]),
                                      ALU.mult).then_inc(o_read, 1)

                def add_out(i):
                    if add:
                        dve.wait_ge(o_read, i + 2)
                        dve.tensor_tensor(dest(i), dest(i), on[:], ALU.add).then_inc(on_done, 1)

                def take_lo(i, s, half):
                    tiles = slice(2, 3) if half else slice(0, 2)
                    dve.wait_ge(pT_hi_done, 2 * i + half + 1)
                    dve.tensor_tensor(pT_lo[s % 2][:, tiles, :], pT[s % 2][:, tiles, :],
                                      pT_hi[s % 2][:, tiles, :].bitcast(F32), ALU.subtract).then_inc(pT_lo_done, 1)

                def step(i, s):
                    first, final = isinstance(i, int) and i == 0, isinstance(i, int) and i == N - 1
                    earlier = not (isinstance(i, int) and i < 2)
                    if not final:
                        reduce(i + 1, 0)
                    if earlier:
                        invert(i - 2)
                        normalise(i - 2)
                    if not first:
                        take_lo(i - 1, s - 1, 1)
                    if earlier:
                        add_out(i - 2)
                    if not final:
                        reduce(i + 1, 1)
                        split_max(i + 1)
                    take_lo(i, s, 0)

                dve.sem_inc(pT_lo_done, 4)
                dve.sem_inc(max_read, 1)
                dve.sem_inc(o_read, 1)
                for s in range(R):
                    dve.memset(ks[s][STK:STK + 2, :].bitcast(F32), 1.0)
                dve.memset(ms[:].bitcast(F32), 0.0)
                dve.memset(fold[:], 0.0)
                for w in vs:
                    last = dve.memset(w[:].bitcast(F32), 0.0)
                last.then_inc(cleared, 1)
                dve.wait_ge(cleared, 1)
                for w in vs:
                    dve.memset(w[:, :, 2 * HD:OUTS].bitcast(F32), 1.0)
                dve.tensor_copy(fold[0:HD, 0:HD], st.ident[0:HD, 0:HD])
                dve.tensor_copy(fold[HD:2 * HD, 0:HD], st.ident[HD:2 * HD, HD:2 * HD])
                dve.tensor_copy(fold[2 * HD:OUTS, HD:HD + 1], st.ident[2 * HD:OUTS, 2 * HD:OUTS]).then_inc(made, 1)
                reduce(0, 0)
                reduce(0, 1)
                split_max(0)
                rounds(dve, step)
                for i in (N - 2, N - 1):
                    invert(i)
                    normalise(i)
                    add_out(i)
                    if i == N - 2:
                        take_lo(N - 1, 1, 1)


def persistent(st):
    sb, _ = tensors(st.nc, st.ctx)
    st.x = sb("x_res", [P, T, D], F32)
    st.ident = sb("ident", [P, P], F32)
    st.ident_r = sb("ident_r", [P, P], F32R)
    st.xT_hi = sb("xT_hi", [P, KC, TOK], F32R)
    st.xT_lo = sb("xT_lo", [P, KC, TOK], F32R)


def column(v):
    return v.rearrange("(p a) -> p a", a=1)


def layer0_attention(st, Wq_w, Wq_b, Wk_w, Wk_b, Wv_w, Wv_b):
    nc = st.nc
    kinds = ["q"] * KC + ["k", "v"]
    q_dram = nc.dram_tensor("l0_q", (2, D, TOK), F32).ap()
    k_dram = nc.dram_tensor("l0_k", (2, HD, TOK), F32).ap()
    norm_to_features(st, "l0a")
    with ExitStack() as outer:
        sb, _ = tensors(nc, outer)
        v = sb("l0_v", [P, T, 1, HD], F32)
        with ExitStack() as stack:
            sb, _ = tensors(nc, stack)
            wT_hi = sb("l0_wT_hi", [P, KC, len(kinds) * P], F32R)
            wT_lo = sb("l0_wT_lo", [P, KC, len(kinds) * P], F32R)
            bias = sb("l0_bias", [P, len(kinds)], F32)
            with ExitStack() as loading:
                sb, _ = tensors(nc, loading)
                wq = sb("l0_wq", [P, KC, D], F32)
                wkv = sb("l0_wkv", [HD, 2, D], F32)
                loads = [(wq[:], Wq_w.rearrange("(f p) d -> p f d", p=P)),
                         (wkv[:, 0, :], Wk_w), (wkv[:, 1, :], Wv_w),
                         (bias[:, 0:KC], Wq_b.rearrange("(f p) -> p f", p=P)),
                         (bias[0:HD, KC:KC + 1], column(Wk_b)), (bias[0:HD, KC + 1:KC + 2], column(Wv_b))]
                jobs = [([wq[:, f, c * P:(c + 1) * P] for f in range(KC)],
                         wT_hi[:, c, 0:D], wT_lo[:, c, 0:D]) for c in range(KC)]
                jobs += [([wkv[:, n, c * P:(c + 1) * P]], wT_hi[:, c, D + n * P:D + n * P + HD],
                          wT_lo[:, c, D + n * P:D + n * P + HD]) for c in range(KC) for n in range(2)]
                fills = [w[:, :, D:].bitcast(F32) for w in (wT_hi, wT_lo)] + [bias[:, KC:]]
                weight_prep(st, "l0w", loads, jobs, fills)
            project(st, "l0p", wT_hi, wT_lo, bias, kinds, q_dram, k_dram, v, 1)
        attend(st, "l0s", q_dram, k_dram, v, False, st.x)


def load_context(st, ctx_in, ctxT_hi, ctxT_lo, more_loads, more_jobs, name, fills=()):
    with ExitStack() as stack:
        sb, _ = tensors(st.nc, stack)
        raw = sb(f"{name}_ctx", [P, T, C], F32)
        loads = [(raw[:], ctx_in.rearrange("b (q p) c -> p (b q) c", p=P))] + more_loads
        jobs = [([raw[:, b * QT + q, c * P:(c + 1) * P] for q in range(QT)],
                 ctxT_hi[:, c, b * S:(b + 1) * S], ctxT_lo[:, c, b * S:(b + 1) * S])
                for b in range(B) for c in range(CC)]
        weight_prep(st, name, loads, jobs + more_jobs, fills)


def feature_attention(st, ctx_in, Wq, bq, Wk, bk):
    nc = st.nc
    assert S == D
    norm_to_features(st, "l0x")
    with ExitStack() as stack:
        sb, ps = tensors(nc, stack)
        ctxT_hi = sb("fa_ctxT_hi", [P, CC, TOK], F32R)
        ctxT_lo = sb("fa_ctxT_lo", [P, CC, TOK], F32R)
        wT_hi = sb("fa_wT_hi", [P, CC, 2 * P], F32R)
        wT_lo = sb("fa_wT_lo", [P, CC, 2 * P], F32R)
        bias = sb("fa_bias", [P, 2], F32)
        with ExitStack() as loading:
            sb2, _ = tensors(nc, loading)
            raw = sb2("fa_w", [P, 2, C], F32)
            loads = [(raw[:, 0, :], Wq), (raw[:, 1, :], Wk), (bias[:, 0:1], column(bq)), (bias[:, 1:2], column(bk))]
            jobs = [([raw[:, n, c * P:(c + 1) * P] for n in range(2)], wT_hi[:, c, :], wT_lo[:, c, :])
                    for c in range(CC)]
            load_context(st, ctx_in, ctxT_hi, ctxT_lo, loads, jobs, "fa_prep")

        hi = [sb(f"fa_hi{n}", [P, S], F32R) for n in range(2)]
        lo = [sb(f"fa_lo{n}", [P, S], F32R) for n in range(2)]
        prob = sb("fa_prob", [P, QT, S], F32)
        nmax = sb("fa_nmax", [P, QT], F32)
        den = sb("fa_den", [P, QT], F32)
        rden = sb("fa_rden", [P, QT], F32)
        attT_hi = sb("fa_attT_hi", [P, QT, S], F32R)
        attT_lo = sb("fa_attT_lo", [P, QT, S], F32R)
        xb_hi = sb("fa_xb_hi", [P, KC, S], F32R)
        xb_lo = sb("fa_xb_lo", [P, KC, S], F32R)
        work = [ps(f"fa_work{n}", [P, 512]) for n in range(2)]
        energy = ps("fa_energy", [P, QT, S])
        turn = [ps(f"fa_turn{n}", [P, 512]) for n in range(2)]
        U = 2 + QT
        worked, work_read, hi_done, scored, nmax_ready, exp_done, rden_done, prob_ready, turned, att_hi, turn_read, \
            staged = st.sems("worked", "work_read", "hi_done", "scored", "nmax_ready", "exp_done", "rden_done",
                             "prob_ready", "turned", "att_hi", "turn_read", "staged")
        with nc.Block() as block:

            @block.gpsimd
            def _(pool):
                with pool.Fori(0, B) as b:
                    pool.wait_ge(worked, U * b + 1)
                    pool.tensor_copy(xb_hi[:], st.xT_hi[:, :, bass.ds(b * S, S)])
                    pool.tensor_copy(xb_lo[:], st.xT_lo[:, :, bass.ds(b * S, S)]).then_inc(staged, 1)

            @block.tensor
            def _(pe):
                pe.sem_inc(worked, 1)
                with pe.Fori(0, B) as b:
                    for n in range(2):
                        pe.wait_ge(work_read, U * b + n + 1)
                        m = 0
                        for c in range(CC):
                            for w, x in ((wT_hi, ctxT_hi), (wT_hi, ctxT_lo), (wT_lo, ctxT_hi)):
                                last = pe.matmul(work[n][:], w[:, c, n * P:(n + 1) * P], x[:, c, bass.ds(b * S, S)],
                                                 start=(m == 0), stop=(m == 3 * CC - 1))
                                m += 1
                        last.then_inc(worked, 1)
                    pe.wait_ge(work_read, U * b + 4)
                    for q in range(QT):
                        for m, (qq, kk) in enumerate(((hi[0], hi[1]), (hi[0], lo[1]), (lo[0], hi[1]))):
                            last = pe.matmul(energy[:, q, :], qq[:, q * P:(q + 1) * P], kk[:], start=(m == 0),
                                             stop=(m == 2))
                        last.then_inc(scored, 1)
                    pe.wait_ge(prob_ready, b + 1)
                    for k in range(QT):
                        pe.wait_ge(turn_read, QT * b + k + 1)
                        for q in range(QT):
                            last = pe.transpose(turn[k % 2][:, q * P:(q + 1) * P], prob[:, q, k * P:(k + 1) * P],
                                                st.ident[:])
                        last.then_inc(turned, 1)
                    pe.wait_ge(turn_read, QT * b + QT + 2)
                    pe.wait_ge(staged, b + 1)
                    for t in range(QT):
                        pe.wait_ge(work_read, U * b + 2 + t + 1)
                        m = 0
                        for k in range(QT):
                            for x, a in ((xb_hi, attT_hi), (xb_hi, attT_lo), (xb_lo, attT_hi)):
                                last = pe.matmul(work[t % 2][:], x[:, k, t * P:(t + 1) * P], a[:, k, :],
                                                 start=(m == 0), stop=(m == 3 * QT - 1))
                                m += 1
                        last.then_inc(worked, 1)

            @block.scalar
            def _(act):
                with act.Fori(0, B) as b:
                    for n in range(2):
                        act.wait_ge(worked, U * b + n + 2)
                        act.activation(hi[n][:], work[n][:], ACT.Identity, bias=bias[:, n:n + 1]).then_inc(hi_done, 1)
                    for q in range(QT):
                        act.wait_ge(nmax_ready, QT * b + q + 1)
                        act.activation(prob[:, q, :], energy[:, q, :], ACT.Exp, bias=nmax[:, q:q + 1],
                                       accum_out=den[:, q:q + 1]).then_inc(exp_done, 1)
                    for k in range(QT):
                        act.wait_ge(turned, QT * b + k + 1)
                        act.activation(attT_hi[:, k, :], turn[k % 2][:], ACT.Copy).then_inc(att_hi, 1)

            @block.vector
            def _(dve):
                dve.sem_inc(work_read, 2)
                dve.sem_inc(turn_read, 2)
                with dve.Fori(0, B) as b:
                    for n in range(2):
                        dve.wait_ge(hi_done, 2 * b + n + 1)
                        dve.scalar_tensor_tensor(lo[n][:], work[n][:], bias[:, n:n + 1], hi[n][:].bitcast(F32),
                                                 ALU.add, ALU.subtract).then_inc(work_read, 1)
                    for q in range(QT):
                        dve.wait_ge(scored, QT * b + q + 1)
                        dve.tensor_reduce(nmax[:, q:q + 1], energy[:, q, :], AX.X, ALU.max, negate=True)\
                            .then_inc(nmax_ready, 1)
                    dve.wait_ge(exp_done, QT * b + QT)
                    dve.reciprocal(rden[:], den[:]).then_inc(rden_done, 1)
                    dve.wait_ge(rden_done, b + 1)
                    for q in range(QT):
                        last = dve.tensor_scalar(prob[:, q, :], prob[:, q, :], rden[:, q:q + 1], None, ALU.mult)
                    last.then_inc(prob_ready, 1)
                    for k in range(QT):
                        dve.wait_ge(att_hi, QT * b + k + 1)
                        dve.tensor_tensor(attT_lo[:, k, :], turn[k % 2][:], attT_hi[:, k, :].bitcast(F32),
                                          ALU.subtract).then_inc(turn_read, 1)
                    for t in range(QT):
                        dve.wait_ge(worked, U * b + 2 + t + 2)
                        xt = st.x[:, bass.ds(b * QT + t, 1), :].rearrange("p a d -> p (a d)")
                        dve.tensor_tensor(xt, work[t % 2][:], xt, ALU.add).then_inc(work_read, 1)


def turn_scales(nc, st, scale, gate_up_scales, down_scales):
    NC = scale.shape[2]
    with ExitStack() as stack:
        sb, ps = tensors(nc, stack)
        s16 = sb("ffn_s16", [KC, 2 * NC * P], F16)
        d16 = sb("ffn_d16", [NC, D], F16)
        s32 = sb("ffn_s32", [KC, 2 * NC * P], F32)
        d32 = sb("ffn_d32", [NC, D], F32)
        gu_bank, dn_bank = ps("ffn_gu_scales", [P, 512]), ps("ffn_dn_scales", [P, 512])
        s_loaded, s32_ready, s_turned = st.sems("s_loaded", "s32_ready", "s_turned")
        with nc.Block() as block:

            @block.sync
            def _(sp):
                sp.dma_start(s16[:], gate_up_scales).then_inc(s_loaded, 16)
                sp.dma_start(d16[:], down_scales).then_inc(s_loaded, 16)

            @block.tensor
            def _(pe):
                pe.wait_ge(s32_ready, 2)
                for f in range(2 * NC):
                    pe.matmul(gu_bank[:, f * KC:(f + 1) * KC], s32[:, f * P:(f + 1) * P], st.ident[0:KC, 0:KC],
                              start=True, stop=True)
                for o in range(KC):
                    last = pe.matmul(dn_bank[:, o * NC:(o + 1) * NC], d32[:, o * P:(o + 1) * P], st.ident[0:NC, 0:NC],
                                     start=True, stop=True)
                last.then_inc(s_turned, 1)

            @block.vector
            def _(dve):
                dve.wait_ge(s_loaded, 32)
                dve.tensor_copy(s32[:], s16[:]).then_inc(s32_ready, 1)
                dve.tensor_copy(d32[:], d16[:]).then_inc(s32_ready, 1)
                dve.wait_ge(s_turned, 1)
                gu = gu_bank[:, 0:2 * NC * KC].rearrange("p (n c k) -> p c n k", n=2, k=KC)
                dn = dn_bank[:, 0:KC * NC].rearrange("p (o c) -> p c o", o=KC)
                for row, by in enumerate((4.0, -1.0)):
                    dve.tensor_scalar(scale[:, row, :, 0:2, :], gu, by, None, ALU.mult)
                    dve.tensor_scalar(scale[:, row, :, 2, :], dn, by, None, ALU.mult)


def packed_ffn(st, gate_up_packed, gate_up_scales, down_packed, down_scales):
    nc = st.nc
    I = gate_up_packed.shape[0] // 2
    NC = I // P
    WORDS = D // 8
    MAG, SIGN, BASE = 7 << 22, 1 << 31, 124 << 23
    norm_to_features(st, "ffn")
    with ExitStack() as stack:
        sb, ps = tensors(nc, stack)
        packed = sb("ffn_packed", [P, 2 * NC, WORDS], I32)
        dpacked = sb("ffn_dpacked", [P, KC, I // 8], I32)
        scale = sb("ffn_scale", [P, 2, NC, 3, KC], F32)
        csc = sb("ffn_csc", [P, 2, 3 * KC], F32)
        turn_scales(nc, st, scale, gate_up_scales, down_scales)
        mag = sb("ffn_mag", [P, 3, D], I32)
        sgn = sb("ffn_sgn", [P, 3, D], I32)
        w32 = sb("ffn_w32", [P, 3, D], F32)
        gu_hi = [sb(f"ffn_gu_hi{s}", [P, 2, KC, P], F32R) for s in range(2)]
        gu_lo = [sb(f"ffn_gu_lo{s}", [P, 2, KC, P], F32R) for s in range(2)]
        dn_hi = [sb(f"ffn_dn_hi{s}", [P, D], F32R) for s in range(2)]
        dn_lo = [sb(f"ffn_dn_lo{s}", [P, D], F32R) for s in range(2)]
        sl = [sb(f"ffn_sl{s}", [P, S], F32) for s in range(2)]
        h32 = [sb(f"ffn_h32{s}", [P, S], F32) for s in range(2)]
        h_hi = [sb(f"ffn_h_hi{s}", [P, S], F32R) for s in range(2)]
        h_lo = [sb(f"ffn_h_lo{s}", [P, S], F32R) for s in range(2)]
        y = sb("ffn_y", [P, T, D], F32)
        ss = sb("ffn_ss", [P, 4, T], F32)
        turn = [ps(f"ffn_turn{s}", [P, 512]) for s in range(2)]
        g_bank = [ps(f"ffn_g{s}", [P, S]) for s in range(2)]
        u_bank = [ps(f"ffn_u{s}", [P, S]) for s in range(2)]
        y_bank = [ps(f"ffn_y{s}", [P, D]) for s in range(2)]
        loaded, chain, csc_ready, f_ready, scaled, w_ready, turned, w_hi, turn_read = st.sems(
            "ffn_loaded", "ffn_chain", "csc_ready", "f_ready", "scaled", "w_ready", "turned",
            "w_hi", "turn_read")
        gu_done, silu_done, h_ready, h_hi_done, h_lo_done, y_done, y_read, y_zero, sq_done, ms_ready, rms_ready = \
            st.sems("gu_done", "silu_done", "h_ready", "h_hi_done", "h_lo_done", "y_done", "y_read", "y_zero",
                    "sq_done", "ms_ready", "rms_ready")

        def chunks(eng, body):
            with eng.Fori(0, NC // 2) as j:
                for s in range(2):
                    body(2 * j + s, s)
            for c in range(NC // 2 * 2, NC):
                body(c, c % 2)

        with nc.Block() as block:

            @block.sync
            def _(sp):
                for dst, src in ((packed[:], gate_up_packed.rearrange("(f p) w -> p f w", p=P)),
                                 (dpacked[:], down_packed.rearrange("(o p) w -> p o w", p=P))):
                    sp.dma_start(dst, src).then_inc(loaded, 16)

            @block.gpsimd
            def _(pool):
                pool.memset(y[:], 0.0).then_inc(y_zero, 1)

            @block.tensor
            def _(pe):
                def turn_weights(c, n):
                    pe.wait_ge(w_ready, c + 1)
                    pe.wait_ge(turn_read, 3 * c + n + 1)
                    for k in range(KC):
                        last = pe.transpose(turn_of(c, n)[:, k * P:(k + 1) * P], w32[:, n, k * P:(k + 1) * P],
                                            st.ident[:])
                    last.then_inc(turned, 1)

                def gate_up(c, s, b):
                    u = B * c + b
                    for n, bank in enumerate((g_bank, u_bank)):
                        pe.wait_ge(h_ready if n else silu_done, u + 1)
                        m = 0
                        for k in range(KC):
                            for w, x in ((gu_hi, st.xT_hi), (gu_hi, st.xT_lo), (gu_lo, st.xT_hi)):
                                last = pe.matmul(bank[b % 2][:], w[s][:, n, k, :], x[:, k, b * S:(b + 1) * S],
                                                 start=(m == 0), stop=(m == 3 * KC - 1))
                                m += 1
                        last.then_inc(gu_done, 1)

                def down(c, s, b):
                    u = B * c + b
                    pe.wait_ge(h_lo_done, u + 1)
                    for t in range(QT):
                        pe.wait_ge(y_read, QT * u + t + 1)
                        for m, (h, w) in enumerate(((h_hi, dn_hi), (h_hi, dn_lo), (h_lo, dn_hi))):
                            last = pe.matmul(y_bank[t % 2][:], h[b % 2][:, t * P:(t + 1) * P], w[s][:],
                                             start=(m == 0), stop=(m == 2))
                        last.then_inc(y_done, 1)

                def turn_of(c, n):
                    return turn[n % 2]

                def chunk(c, s):
                    known = isinstance(c, int)
                    pe.wait_ge(turn_read, 3 * c + 5)
                    for b in range(B):
                        gate_up(c, s, b)
                        if b:
                            down(c, s, b - 1)
                        elif known and c == 0:
                            pass
                        else:
                            down(c - 1, 1 - s, B - 1)
                        if b and not (known and c == NC - 1):
                            turn_weights(c + 1, b - 1)

                for n in range(3):
                    turn_weights(0, n)
                chunk(0, 0)
                with pe.Fori(0, (NC - 2) // 2) as j:
                    chunk(2 * j + 1, 1)
                    chunk(2 * j + 2, 0)
                for c in range((NC - 2) // 2 * 2 + 1, NC):
                    chunk(c, c % 2)
                down(NC - 1, (NC - 1) % 2, B - 1)

            @block.scalar
            def _(act):
                act.sem_inc(silu_done, 2)

                def scale_weights(c):
                    act.wait_ge(csc_ready, c + 1)
                    act.wait_ge(f_ready, c + 1)
                    for n in range(3):
                        for k in range(KC):
                            col = n * KC + k
                            last = act.activation(w32[:, n, k * P:(k + 1) * P], w32[:, n, k * P:(k + 1) * P],
                                                  ACT.Identity, bias=csc[:, 1, col:col + 1],
                                                  scale=csc[:, 0, col:col + 1])
                    last.then_inc(scaled, 1)

                def take_hi(c, s, n):
                    act.wait_ge(turned, 3 * c + n + 1)
                    dst = dn_hi[s][:] if n == 2 else gu_hi[s][:, n, :, :].rearrange("p k f -> p (k f)")
                    act.activation(dst, turn[n % 2][:], ACT.Copy).then_inc(w_hi, 1)

                def hidden(c, b):
                    u = B * c + b
                    act.wait_ge(gu_done, 2 * u + 1)
                    act.activation(sl[b % 2][:], g_bank[b % 2][:], ACT.Silu).then_inc(silu_done, 1)
                    act.wait_ge(h_ready, u + 3)
                    act.activation(h_hi[b % 2][:], h32[b % 2][:], ACT.Copy).then_inc(h_hi_done, 1)

                def chunk(c, s):
                    more = not (isinstance(c, int) and c == NC - 1)
                    for b in range(B):
                        if b == 1 and more:
                            scale_weights(c + 1)
                        if b > 1 and more:
                            take_hi(c + 1, 1 - s, b - 2)
                        hidden(c, b)
                    if more:
                        take_hi(c + 1, 1 - s, 2)

                scale_weights(0)
                for n in range(3):
                    take_hi(0, 0, n)
                chunks(act, chunk)
                act.wait_ge(y_read, QT * B * NC + 2)
                for t in range(T):
                    if t >= 2:
                        act.wait_ge(sq_done, t - 1)
                    act.activation(sl[t % 2][:], y[:, t, :], ACT.Square, accum_out=ss[:, 0, t:t + 1]).then_inc(sq_done, 1)
                act.wait_ge(ms_ready, 1)
                act.activation(ss[:, 2, :], ss[:, 1, :], ACT.Sqrt).then_inc(rms_ready, 1)

            @block.vector
            def _(dve):
                dve.wait_ge(loaded, 32)
                dve.sem_inc(turn_read, 2)
                dve.sem_inc(h_ready, 2)
                dve.sem_inc(y_read, 2)

                def unpack(c, part):
                    dst, keep, at = ((mag, MAG, 22), (sgn, SIGN - (1 << 32), 28))[part]
                    for j in range(8):
                        shift = at - 4 * j
                        op = ALU.logical_shift_left if shift >= 0 else ALU.logical_shift_right
                        gu_words = packed[:].rearrange("p (n c) w -> p c n w", n=2)[:, bass.ds(c, 1), :, :]\
                            .rearrange("p a n w -> p (a n) w")
                        dn_words = dpacked[:, :, bass.ds(c * (P // 8), P // 8)]
                        dve.tensor_scalar(dst[:, 0:2, :].rearrange("p n (w e) -> p n w e", e=8)[:, :, :, j],
                                          gu_words, abs(shift), keep, op, ALU.bitwise_and)
                        last = dve.tensor_scalar(
                            dst[:, 2, :].rearrange("p (o w e) -> p o w e", o=KC, e=8)[:, :, :, j],
                            dn_words, abs(shift), keep, op, ALU.bitwise_and)
                    return last

                def decode(c, part):
                    base = 4 * c
                    if part == 0:
                        dve.tensor_copy(csc[:].rearrange("p r (n k) -> p r n k", n=3),
                                        scale[:, :, bass.ds(c, 1), :, :].rearrange("p r a n k -> p r (a n) k"))\
                            .then_inc(csc_ready, 1)
                        unpack(c, 0).then_inc(chain, 1)
                        dve.wait_ge(chain, base + 1)
                        dve.tensor_scalar(mag[:], mag[:], BASE, None, ALU.bitwise_or).then_inc(chain, 1)
                        dve.wait_ge(chain, base + 2)
                        g = mag[:].bitcast(F32)
                        dve.scalar_tensor_tensor(w32[:], g, 0.25, g, ALU.min, ALU.add).then_inc(f_ready, 1)
                    elif part == 1:
                        unpack(c, 1).then_inc(chain, 1)
                    else:
                        dve.wait_ge(scaled, c + 1)
                        dve.wait_ge(chain, base + 3)
                        wi = w32[:].bitcast(I32)
                        dve.tensor_tensor(wi, wi, sgn[:], ALU.bitwise_xor).then_inc(w_ready, 1)
                        dve.sem_inc(chain, 1)

                def take_lo(c, s, n):
                    dve.wait_ge(w_hi, 3 * c + n + 1)
                    hi, lo = (dn_hi[s][:], dn_lo[s][:]) if n == 2 else \
                        (x[s][:, n, :, :].rearrange("p k f -> p (k f)") for x in (gu_hi, gu_lo))
                    dve.tensor_tensor(lo, turn[n % 2][:], hi.bitcast(F32), ALU.subtract).then_inc(turn_read, 1)

                def hidden(c, b, part):
                    u = B * c + b
                    if part == 0:
                        dve.wait_ge(silu_done, u + 3)
                        dve.wait_ge(gu_done, 2 * u + 2)
                        dve.tensor_tensor(h32[b % 2][:], u_bank[b % 2][:], sl[b % 2][:], ALU.mult).then_inc(h_ready, 1)
                    else:
                        dve.wait_ge(h_hi_done, u + 1)
                        dve.tensor_tensor(h_lo[b % 2][:], h32[b % 2][:], h_hi[b % 2][:].bitcast(F32), ALU.subtract)\
                            .then_inc(h_lo_done, 1)

                def add_y(c, b, t):
                    v = QT * (B * c + b) + t
                    dve.wait_ge(y_done, v + 1)
                    yt = y[:, b * QT + t, :]
                    dve.tensor_tensor(yt, y_bank[t % 2][:], yt, ALU.add).then_inc(y_read, 1)

                def chunk(c, s):
                    first, final = isinstance(c, int) and c == 0, isinstance(c, int) and c == NC - 1
                    for b in range(B):
                        cp, bp = (c, b - 1) if b else (c - 1, B - 1)
                        adds = not (first and b == 0)
                        hidden(c, b, 0)
                        for t in (0, 1):
                            if adds:
                                add_y(cp, bp, t)
                        hidden(c, b, 1)
                        for t in (2, 3):
                            if adds:
                                add_y(cp, bp, t)
                        if final:
                            continue
                        if b == 0:
                            decode(c + 1, 0)
                            decode(c + 1, 1)
                            decode(c + 1, 2)
                        else:
                            take_lo(c + 1, 1 - s, b - 1)

                decode(0, 0)
                decode(0, 1)
                decode(0, 2)
                for n in range(3):
                    take_lo(0, 0, n)
                dve.wait_ge(y_zero, 1)
                chunk(0, 0)
                with dve.Fori(0, (NC - 2) // 2) as j:
                    chunk(2 * j + 1, 1)
                    chunk(2 * j + 2, 0)
                for c in range((NC - 2) // 2 * 2 + 1, NC):
                    chunk(c, c % 2)
                for t in range(QT):
                    add_y(NC - 1, B - 1, t)
                dve.wait_ge(sq_done, T)
                dve.tensor_scalar(ss[:, 1, :], ss[:, 0, :], 1.0 / D, 1e-6, ALU.mult, ALU.add).then_inc(ms_ready, 1)
                dve.wait_ge(rms_ready, 1)
                dve.reciprocal(ss[:, 3, :], ss[:, 2, :]).then_inc(ms_ready, 1)
                dve.wait_ge(ms_ready, 2)
                for t in range(T):
                    dve.scalar_tensor_tensor(st.x[:, t, :], y[:, t, :], ss[:, 3, t:t + 1], st.x[:, t, :], ALU.mult,
                                             ALU.add)


def turn_tile(eng_pe, bank, source, ident):
    for c in range(KC):
        last = eng_pe.transpose(bank[:, c * P:(c + 1) * P], source[:, c * P:(c + 1) * P], ident)
    return last


def layer1_attention(st, Wqkv_w, Wqkv_b, out_w, out_b):
    nc = st.nc
    kinds = ["q"] * KC + ["k"] * KC + ["v"] * KC
    q_dram = nc.dram_tensor("l1_q", (2, D, TOK), F32).ap()
    k_dram = nc.dram_tensor("l1_k", (2, D, TOK), F32).ap()
    norm_to_features(st, "l1a")
    with ExitStack() as outer:
        sb, _ = tensors(nc, outer)
        v = sb("l1_v", [P, T, NH, HD], F32)
        with ExitStack() as stack:
            sb, _ = tensors(nc, stack)
            wT_hi = sb("l1_wT_hi", [P, KC, 3 * D], F32R)
            wT_lo = sb("l1_wT_lo", [P, KC, 3 * D], F32R)
            bias = sb("l1_bias", [P, 3 * KC], F32)
            for n in range(3):
                with ExitStack() as loading:
                    sb, _ = tensors(nc, loading)
                    raw = sb(f"l1_w{n}", [P, KC, D], F32)
                    loads = [(raw[:], Wqkv_w[n * D:(n + 1) * D, :].rearrange("(f p) d -> p f d", p=P))]
                    if n == 0:
                        loads.append((bias[:], Wqkv_b.rearrange("(f p) -> p f", p=P)))
                    jobs = [([raw[:, f, c * P:(c + 1) * P] for f in range(KC)],
                             wT_hi[:, c, n * D:(n + 1) * D], wT_lo[:, c, n * D:(n + 1) * D]) for c in range(KC)]
                    weight_prep(st, f"l1w{n}", loads, jobs)
            project(st, "l1p", wT_hi, wT_lo, bias, kinds, q_dram, k_dram, v, P // HD)
        ao = sb_tensor(nc, outer, "l1_ao", [P, T, D])
        attend(st, "l1s", q_dram, k_dram, v, True, ao)
        output_projection(st, ao, out_w, out_b)


def sb_tensor(nc, stack, name, shape, dt=F32):
    return stack.enter_context(nc.sbuf_tensor(name, shape, dt))


def output_projection(st, ao, out_w, out_b):
    nc = st.nc
    with ExitStack() as stack:
        sb, ps = tensors(nc, stack)
        raw = sb("op_w", [P, KC, D], F32)
        w_hi = sb("op_w_hi", [P, KC, D], F32R)
        w_lo = sb("op_w_lo", [P, KC, D], F32R)
        bias = sb("op_bias", [P, D], F32)
        jobs = [([raw[:, f, c * P:(c + 1) * P] for f in range(KC)], w_hi[:, c, :], w_lo[:, c, :]) for c in range(KC)]
        weight_prep(st, "op_prep", [(raw[:], out_w.rearrange("(f p) d -> p f d", p=P)),
                                    (bias[:], out_b.rearrange("(a d) -> a d", a=1).to_broadcast([P, D]))], jobs)
        a32 = [sb(f"op_a32{s}", [P, D], F32) for s in range(2)]
        a_hi = [sb(f"op_a_hi{s}", [P, D], F32R) for s in range(2)]
        a_lo = [sb(f"op_a_lo{s}", [P, D], F32R) for s in range(2)]
        turn = [ps(f"op_turn{s}", [P, D]) for s in range(2)]
        bank = [ps(f"op_bank{s}", [P, D]) for s in range(2)]
        copied, turned, hi_done, lo_done, done, read, biased = st.sems(
            "op_copied", "op_turned", "op_hi", "op_lo", "op_done", "op_read", "op_biased")
        with nc.Block() as block:

            @block.gpsimd
            def _(pool):
                with pool.Fori(0, T) as t:
                    xt = st.x[:, bass.ds(t, 1), :].rearrange("p a d -> p (a d)")
                    pool.tensor_tensor(xt, xt, bias[:], ALU.add).then_inc(biased, 1)

            @block.tensor
            def _(pe):
                def turn_a(t, s):
                    pe.wait_ge(copied, t + 1)
                    pe.wait_ge(lo_done, t + 1)
                    turn_tile(pe, turn[s], a32[s], st.ident[:]).then_inc(turned, 1)

                def product(t, s):
                    pe.wait_ge(lo_done, t + 3)
                    pe.wait_ge(read, t + 1)
                    m = 0
                    for c in range(KC):
                        for a, w in ((a_hi, w_hi), (a_hi, w_lo), (a_lo, w_hi)):
                            last = pe.matmul(bank[s][:], a[s][:, c * P:(c + 1) * P], w[:, c, :], start=(m == 0),
                                             stop=(m == 3 * KC - 1))
                            m += 1
                    last.then_inc(done, 1)

                turn_a(0, 0)
                with pe.Fori(0, T // 2 - 1) as j:
                    for s in range(2):
                        turn_a(2 * j + s + 1, 1 - s)
                        product(2 * j + s, s)
                turn_a(T - 1, 1)
                product(T - 2, 0)
                product(T - 1, 1)

            @block.scalar
            def _(act):
                act.sem_inc(done, 2)
                with act.Fori(0, T // 2) as j:
                    for s in range(2):
                        t = 2 * j + s
                        act.wait_ge(turned, t + 1)
                        act.wait_ge(done, t + 1)
                        act.activation(a_hi[s][:], turn[s][:], ACT.Copy).then_inc(hi_done, 1)

            @block.vector
            def _(dve):
                dve.sem_inc(lo_done, 2)
                dve.sem_inc(read, 2)

                def copy(t, s):
                    dve.wait_ge(lo_done, t + 1)
                    dve.tensor_copy(a32[s][:], ao[:, bass.ds(t, 1), :].rearrange("p a d -> p (a d)"))\
                        .then_inc(copied, 1)

                def take_lo(t, s):
                    dve.wait_ge(hi_done, t + 1)
                    dve.tensor_tensor(a_lo[s][:], turn[s][:], a_hi[s][:].bitcast(F32), ALU.subtract)\
                        .then_inc(lo_done, 1)

                def add(t, s):
                    dve.wait_ge(biased, t + 1)
                    dve.wait_ge(done, t + 3)
                    xt = st.x[:, bass.ds(t, 1), :].rearrange("p a d -> p (a d)")
                    dve.tensor_tensor(xt, bank[s][:], xt, ALU.add).then_inc(read, 1)

                copy(0, 0)
                copy(1, 1)
                take_lo(0, 0)
                with dve.Fori(0, T // 2 - 1) as j:
                    for s in range(2):
                        t = 2 * j + s
                        copy(t + 2, s)
                        take_lo(t + 1, 1 - s)
                        add(t, s)
                take_lo(T - 1, 1)
                add(T - 2, 0)
                add(T - 1, 1)


def routed_mixture(st, Wr, U, V, attr, Wa, out):
    nc = st.nc
    NS, R = Wr.shape[0], U.shape[2]
    F = NS * R
    FC = F // P
    AD = attr.shape[1]
    norm_to_features(st, "mix")
    with ExitStack() as stack:
        sb, ps = tensors(nc, stack)
        wr_hi = sb("mix_wr_hi", [P, KC, P], F32R)
        wr_lo = sb("mix_wr_lo", [P, KC, P], F32R)
        u_hi = sb("mix_u_hi", [P, KC, F], F32R)
        u_lo = sb("mix_u_lo", [P, KC, F], F32R)
        v32 = sb("mix_v32", [P, FC, D], F32)
        v_hi = sb("mix_v_hi", [P, FC, D], F32R)
        v_lo = sb("mix_v_lo", [P, FC, D], F32R)
        attr_b = sb("mix_attr", [P, NS, AD], F32)
        wa_b = sb("mix_wa", [P, 1, AD], F32)
        with ExitStack() as loading:
            sb2, _ = tensors(nc, loading)
            wr = sb2("mix_wr", [NS, D], F32)
            u = sb2("mix_u", [P, P, R], F32)
            loads = [(wr[:], Wr), (u[:], U.rearrange("s (c h) r -> (s c) h r", c=KC)),
                     (attr_b[:].rearrange("p s a -> p (s a)"),
                      attr.rearrange("s a -> (s a)").rearrange("(o a) -> o a", o=1).to_broadcast([P, NS * AD])),
                     (wa_b[:, 0, :], Wa.to_broadcast([P, AD])),
                     (v32[:], V.rearrange("s r d -> (s r) d").rearrange("(c p) d -> p c d", p=P))]
            jobs = [([wr[:, c * P:(c + 1) * P]], wr_hi[:, c, 0:NS], wr_lo[:, c, 0:NS]) for c in range(KC)]
            for r in range(0, R, 4):
                hi, lo = (w[:].rearrange("p c (s r) -> p r s c", r=R)[:, r:r + 4] for w in (u_hi, u_lo))
                jobs.append(([u[:, :, r + k] for k in range(4)], hi, lo))
            weight_prep(st, "mix_prep", loads, jobs, [w[:].bitcast(F32) for w in (wr_hi, wr_lo)])

        scT = sb("mix_scT", [NS, S], F32)
        sc = sb("mix_sc", [P, T, NS], F32)
        top = sb("mix_top", [P, T, 8], F32)
        idx = sb("mix_idx", [P, T, 8], U32)
        idx_f = sb("mix_idx_f", [P, T, 2], F32)
        number = sb("mix_number", [P, 1, NS], F32)
        first = sb("mix_first", [P, T, NS], F32)
        g = sb("mix_g", [P, T, NS], F32)
        e = sb("mix_e", [P, T, NS], F32)
        den = sb("mix_den", [P, 4, T], F32)
        aw = sb("mix_aw", [P, 3, NS], F32)
        spread = sb("mix_spread", [P, F], F32)
        spread_r = sb("mix_spread_r", [P, F], F32R)
        gT_hi = sb("mix_gT_hi", [P, TOK], F32R)
        gT_lo = sb("mix_gT_lo", [P, TOK], F32R)
        hu = [sb(f"mix_hu{n}", [P, S], F32) for n in range(2)]
        z = [sb(f"mix_z{n}", [P, S], F32) for n in range(2)]
        z_hi = sb("mix_z_hi", [P, FC, S], F32R)
        z_lo = sb("mix_z_lo", [P, FC, S], F32R)
        hu_bank = [ps(f"mix_hu_bank{n}", [P, S]) for n in range(2)]
        g_bank = [ps(f"mix_g_bank{n}", [P, S]) for n in range(2)]
        out_bank = [ps(f"mix_out_bank{n}", [P, D]) for n in range(2)]
        sc_bank = ps("mix_sc_bank", [P, S])
        turn_bank = ps("mix_turn_bank", [P, S])
        v_hi_done, made, scored, sc_read, sc_turned, sc_taken, chain, e_in, e_out, aw_in, aw_out, g_ready, g_turned, \
            gT_hi_done, gT_done = st.sems(
                "v_hi_done", "made", "scored", "sc_read", "sc_turned", "sc_taken", "mix_chain", "e_in", "e_out",
                "aw_in", "aw_out", "g_ready", "g_turned", "gT_hi_done", "gT_done")
        hu_done, hu_copied, spread_done, z_made, z_hi_done, z_lo_done, out_done, x_ready, stored = st.sems(
            "hu_done", "hu_copied", "spread_done", "z_made", "z_hi_done", "z_lo_done", "out_done", "x_ready",
            "stored")
        with nc.Block() as block:

            @block.gpsimd
            def _(pool):
                pool.iota(number[:, 0, :], pattern=[[1, NS]], base=0, channel_multiplier=0,
                          allow_small_or_imprecise_dtypes=True).then_inc(made, 1)
                pool.memset(spread[:], 1.0).then_inc(made, 1)
                pool.wait_ge(made, 2)
                pool.affine_select(out=spread[:], in_=spread[:], compare_op=ALU.is_ge, fill=0.0, base=0,
                                   pattern=[[1, F]], channel_multiplier=-R).then_inc(made, 1)
                pool.wait_ge(made, 3)
                pool.affine_select(out=spread[:], in_=spread[:], compare_op=ALU.is_ge, fill=0.0, base=R - 1,
                                   pattern=[[-1, F]], channel_multiplier=R).then_inc(made, 1)
                for w in (gT_hi, gT_lo):
                    pool.memset(w[:].bitcast(F32), 0.0).then_inc(made, 1)

            @block.tensor
            def _(pe):
                def turn_scores(b):
                    pe.wait_ge(sc_read, b + 1)
                    if b:
                        pe.wait_ge(sc_taken, b)
                    for q in range(QT):
                        last = pe.matmul(turn_bank[:, q * NS:(q + 1) * NS], scT[:, q * P:(q + 1) * P],
                                         st.ident[0:NS, 0:NS], start=True, stop=True)
                    last.then_inc(sc_turned, 1)

                for b in range(B):
                    if b:
                        pe.wait_ge(sc_read, b)
                    m = 0
                    for c in range(KC):
                        for w, x in ((wr_hi, st.xT_hi), (wr_hi, st.xT_lo), (wr_lo, st.xT_hi)):
                            last = pe.matmul(sc_bank[:], w[:, c, :], x[:, c, b * S:(b + 1) * S], start=(m == 0),
                                             stop=(m == 3 * KC - 1))
                            m += 1
                    last.then_inc(scored, 1)
                    turn_scores(b)
                pe.wait_ge(g_ready, 1)
                for b in range(B):
                    if b:
                        pe.wait_ge(gT_done, b)
                    for q in range(QT):
                        last = pe.matmul(turn_bank[0:NS, q * P:(q + 1) * P], g[:, b * QT + q, :], st.ident[:],
                                         start=True, stop=True)
                    last.then_inc(g_turned, 1)
                pe.wait_ge(gT_done, B)
                pe.wait_ge(v_hi_done, 2 * FC)
                with pe.Fori(0, B) as b:
                    for c in range(FC):
                        i = b * FC + c
                        pe.wait_ge(hu_copied, i + 1)
                        m = 0
                        for k in range(KC):
                            for w, x in ((u_hi, st.xT_hi), (u_hi, st.xT_lo), (u_lo, st.xT_hi)):
                                last = pe.matmul(hu_bank[c % 2][:], w[:, k, c * P:(c + 1) * P],
                                                 x[:, k, bass.ds(b * S, S)], start=(m == 0), stop=(m == 3 * KC - 1))
                                m += 1
                        last.then_inc(hu_done, 1)
                        pe.wait_ge(z_made, i + 1)
                        for m, part in enumerate((gT_hi, gT_lo)):
                            last = pe.matmul(g_bank[c % 2][:], spread_r[:, c * P:(c + 1) * P],
                                             part[:, bass.ds(b * S, S)], start=(m == 0), stop=(m == 1))
                        last.then_inc(spread_done, 1)
                    pe.wait_ge(z_lo_done, FC * (b + 1))
                    for q in range(QT):
                        pe.wait_ge(x_ready, b * QT + q + 1)
                        m = 0
                        for c in range(FC):
                            for a, w in ((z_hi, v_hi), (z_hi, v_lo), (z_lo, v_hi)):
                                last = pe.matmul(out_bank[q % 2][:], a[:, c, q * P:(q + 1) * P], w[:, c, :],
                                                 start=(m == 0), stop=(m == 3 * FC - 1))
                                m += 1
                        last.then_inc(out_done, 1)

            @block.scalar
            def _(act):
                act.sem_inc(hu_copied, 2)
                for c in range(FC):
                    act.activation(v_hi[:, c, :], v32[:, c, :], ACT.Copy).then_inc(v_hi_done, 1)
                for b in range(B):
                    act.wait_ge(scored, b + 1)
                    if b:
                        act.wait_ge(sc_turned, b)
                    act.activation(scT[:], sc_bank[0:NS, :], ACT.Copy).then_inc(sc_read, 1)
                act.wait_ge(aw_in, 1)
                act.activation(aw[:, 1, :], aw[:, 0, :], ACT.Exp, scale=-1.0).then_inc(aw_out, 1)
                act.wait_ge(e_in, 1)
                act.activation(e[:], e[:], ACT.Exp).then_inc(e_out, 1)
                for b in range(B):
                    act.wait_ge(g_turned, b + 1)
                    act.wait_ge(made, 6)
                    act.activation(gT_hi[0:NS, b * S:(b + 1) * S], turn_bank[0:NS, :], ACT.Copy).then_inc(gT_hi_done, 1)
                with act.Fori(0, B) as b:
                    for c in range(FC + 1):
                        if c < FC:
                            i = b * FC + c
                            act.wait_ge(hu_done, i + 1)
                            act.wait_ge(z_made, i + 1)
                            act.activation(hu[c % 2][:], hu_bank[c % 2][:], ACT.Copy).then_inc(hu_copied, 1)
                        if c:
                            act.wait_ge(z_made, b * FC + c + 2)
                            act.activation(z_hi[:, c - 1, :], z[(c - 1) % 2][:], ACT.Copy).then_inc(z_hi_done, 1)

            @block.vector
            def _(dve):
                n_chain = [0]

                def link(ins):
                    n_chain[0] += 1
                    ins.then_inc(chain, 1)
                    dve.wait_ge(chain, n_chain[0])

                dve.sem_inc(z_made, 2)
                dve.sem_inc(x_ready, 2)
                link(dve.tensor_tensor(attr_b[:], attr_b[:], wa_b[:].to_broadcast([P, NS, AD]), ALU.mult))
                dve.tensor_reduce(aw[:, 0, :], attr_b[:], AX.X, ALU.add).then_inc(aw_in, 1)
                for c in range(FC):
                    dve.wait_ge(v_hi_done, FC)
                    dve.tensor_tensor(v_lo[:, c, :], v32[:, c, :], v_hi[:, c, :].bitcast(F32), ALU.subtract)\
                        .then_inc(v_hi_done, 1)
                for b in range(B):
                    dve.wait_ge(sc_turned, b + 1)
                    dve.tensor_copy(sc[:, b * QT:(b + 1) * QT, :],
                                    turn_bank[:, 0:QT * NS].rearrange("p (q s) -> p q s", q=QT)).then_inc(sc_taken, 1)
                dve.wait_ge(sc_taken, B)
                for t in range(T):
                    last = dve.max(top[:, t, :], sc[:, t, :])
                link(last)
                for t in range(T):
                    last = dve.max_index(idx[:, t, :], top[:, t, :], sc[:, t, :])
                link(last)
                full = [P, T, NS]
                dve.tensor_tensor(e[:], sc[:], top[:, :, 0:1].to_broadcast(full), ALU.subtract).then_inc(e_in, 1)
                link(dve.tensor_copy(idx_f[:], idx[:, :, 0:2]))
                dve.wait_ge(made, 6)
                dve.tensor_copy(spread_r[:], spread[:])
                numbers = number[:].to_broadcast(full)
                link(dve.tensor_tensor(first[:], numbers, idx_f[:, :, 0:1].to_broadcast(full), ALU.is_equal))
                link(dve.tensor_tensor(g[:], numbers, idx_f[:, :, 1:2].to_broadcast(full), ALU.is_equal))
                link(dve.tensor_tensor(g[:], g[:], first[:], ALU.add))
                dve.wait_ge(aw_out, 1)
                link(dve.tensor_scalar(aw[:, 1, :], aw[:, 1, :], 1.0, None, ALU.add))
                link(dve.reciprocal(aw[:, 2, :], aw[:, 1, :]))
                dve.wait_ge(e_out, 1)
                link(dve.tensor_reduce(den[:, 0, :], e[:], AX.X, ALU.add))
                link(dve.reciprocal(den[:, 1, :], den[:, 0, :]))
                link(dve.tensor_tensor(e[:], e[:], over(den, 1, full), ALU.mult))
                link(dve.tensor_tensor(g[:], g[:], e[:], ALU.mult))
                link(dve.tensor_reduce(den[:, 0, :], g[:], AX.X, ALU.add))
                link(dve.tensor_scalar(den[:, 0, :], den[:, 0, :], 1e-8, None, ALU.add))
                link(dve.reciprocal(den[:, 1, :], den[:, 0, :]))
                link(dve.tensor_tensor(g[:], g[:], over(den, 1, full), ALU.mult))
                link(dve.tensor_tensor(e[:], g[:], aw[:, 2:3, :].to_broadcast(full), ALU.mult))
                link(dve.tensor_reduce(den[:, 2, :], e[:], AX.X, ALU.add))
                link(dve.tensor_scalar(den[:, 3, :], den[:, 2, :], 0.2, 0.9, ALU.mult, ALU.add))
                dve.tensor_tensor(g[:], g[:], over(den, 3, full), ALU.mult).then_inc(g_ready, 1)
                for b in range(B):
                    dve.wait_ge(gT_hi_done, b + 1)
                    cols = slice(b * S, (b + 1) * S)
                    dve.tensor_tensor(gT_lo[0:NS, cols], turn_bank[0:NS, :], gT_hi[0:NS, cols].bitcast(F32), ALU.subtract)\
                        .then_inc(gT_done, 1)
                with dve.Fori(0, B) as b:
                    for c in range(FC):
                        i = b * FC + c
                        dve.wait_ge(hu_copied, i + 3)
                        dve.wait_ge(spread_done, i + 1)
                        dve.tensor_tensor(z[c % 2][:], g_bank[c % 2][:], hu[c % 2][:], ALU.mult).then_inc(z_made, 1)
                        dve.wait_ge(z_hi_done, i + 1)
                        dve.tensor_tensor(z_lo[:, c, :], z[c % 2][:], z_hi[:, c, :].bitcast(F32), ALU.subtract)\
                            .then_inc(z_lo_done, 1)
                    for q in range(QT):
                        dve.wait_ge(out_done, b * QT + q + 1)
                        xt = st.x[:, bass.ds(b * QT + q, 1), :].rearrange("p a d -> p (a d)")
                        dve.tensor_tensor(xt, out_bank[q % 2][:], xt, ALU.add).then_inc(x_ready, 1)

            @block.sync
            def _(sp):
                for b in range(B):
                    sp.wait_ge(x_ready, QT * (b + 1) + 2)
                    sp.dma_start(out[b].rearrange("(q p) d -> p q d", p=P), st.x[:, b * QT:(b + 1) * QT, :])\
                        .then_inc(stored, 16)
                sp.wait_ge(stored, 16 * B)


def over(rows, n, shape):
    return rows[:, n, :].rearrange("p (t a) -> p t a", a=1).to_broadcast(shape)


def reached(eng, sem, count):
    if not (isinstance(count, int) and count <= 0):
        eng.wait_ge(sem, count)


def cross_attention(st, ctx_in, mask, Wq, Wk, Wv, Wo):
    nc = st.nc
    HX = 128
    G = Wk.shape[1] // HX
    NR = Wq.shape[1] // HX // G
    NU = G * B
    LOW = -1e30
    scale = HX ** -0.5
    norm_to_features(st, "xat")
    with ExitStack() as stack:
        sb, ps = tensors(nc, stack)
        ctxT_hi = sb("xa_ctxT_hi", [P, CC, TOK], F32R)
        ctxT_lo = sb("xa_ctxT_lo", [P, CC, TOK], F32R)
        load_context(st, ctx_in, ctxT_hi, ctxT_lo, [], [], "xa_prep")
        mask8 = sb("xa_mask8", [P, B, S], U8)
        mask_bias = sb("xa_mask_bias", [P, S], F32)
        PIECE = KC // 2 * NR * HX
        assert PIECE == 2 * CC * HX == D
        raw = [sb(f"xa_raw{n}", [P, PIECE], F32) for n in range(2)]
        kv_w = [sb(f"xa_kv_w{n}", [P, 2, CC, HX], F32R) for n in range(2)]
        q_w = [sb(f"xa_q_w{n}", [P, KC, NR * HX], F32R) for n in range(2)]
        o_w = [sb(f"xa_o_w{n}", [P, NR, D], F32R) for n in range(2)]
        k_hi = [sb(f"xa_k_hi{n}", [P, S], F32R) for n in range(2)]
        k_lo = [sb(f"xa_k_lo{n}", [P, S], F32R) for n in range(2)]
        vT = sb("xa_vT", [P, S], F32)
        v_hi = [sb(f"xa_v_hi{n}", [P, QT * HX], F32R) for n in range(2)]
        v_lo = [sb(f"xa_v_lo{n}", [P, QT * HX], F32R) for n in range(2)]
        q_hi = [sb(f"xa_q_hi{n}", [P, S], F32R) for n in range(NR)]
        q_lo = [sb(f"xa_q_lo{n}", [P, S], F32R) for n in range(NR)]
        nmax = sb("xa_nmax", [P, QT], F32)
        den = sb("xa_den", [P, NR, 3, QT], F32)
        prob = sb("xa_prob", [P, QT, S], F32)
        pT_hi = sb("xa_pT_hi", [P, QT - 1, S], F32R)
        pT_lo = sb("xa_pT_lo", [P, QT - 1, S], F32R)
        o_hi = sb("xa_o_hi", [P, S], F32R)
        o_lo = sb("xa_o_lo", [P, S], F32R)
        bank_a = ps("xa_bank_a", [P, 512])
        bank_b = ps("xa_bank_b", [P, 512])
        s_bank = [ps(f"xa_s_bank{n}", [P, S]) for n in range(2)]
        t_bank = [ps(f"xa_t_bank{n}", [P, S]) for n in range(2)]
        o_bank = ps("xa_o_bank", [P, S])
        out_bank = ps("xa_out_bank", [P, D])
        mask_in, mask_ready, maximum_next, rounding_next, raw_in_0, raw_in_1, split, weighed_first = st.sems(
            "mask_in", "mask_ready", "maximum_next", "rounding_next", "raw_in_0", "raw_in_1", "split", "weighed_first")
        k_done, k_hi_done, k_lo_done, vT_done, vT_copied, v_done, v_hi_done, v_lo_done, q_done, q_hi_done, \
            q_lo_done = st.sems("k_done", "k_hi_done", "k_lo_done", "vT_done", "vT_copied", "v_done", "v_hi_done",
                                "v_lo_done", "q_done", "q_hi_done", "q_lo_done")
        scored, maxed, exp_done, clamped, inverted, turned, pT_hi_done, pT_lo_done, weighed, o_hi_done, o_lo_done, \
            out_done, added = st.sems("scored", "maxed", "exp_done", "clamped", "inverted", "turned", "pT_hi_done",
                                      "pT_lo_done", "weighed", "o_hi_done", "o_lo_done", "out_done", "added")

        raw_in = (raw_in_0, raw_in_1)
        STAGING = (0, 1, 0, 1, 0)
        PIECES = len(STAGING)

        def products(pe, bank, pairs):
            for m, (w, x) in enumerate(pairs):
                last = pe.matmul(bank, w, x, start=(m == 0), stop=(m == len(pairs) - 1))
            return last

        def units(eng, unit):
            unit(0, 0)
            with eng.Fori(0, NU // 2 - 1) as j:
                unit(2 * j + 1, 1)
                unit(2 * j + 2, 0)
            unit(NU - 1, 1)

        def is_last(u):
            return isinstance(u, int) and u == NU - 1

        def is_first(u):
            return isinstance(u, int) and u == 0

        with nc.Block() as block:

            @block.sync
            def _(sp):
                def load(g):
                    for i, n in enumerate(STAGING):
                        before = g * PIECES + (-1, -2, 0, 1, 2)[i]
                        reached(sp, split, 2 * before + 2 if not (is_first(g) and i < 2) else 0)
                        if i == 0:
                            view = raw[n][:].rearrange("p (n c f) -> p n c f", n=2, c=CC)
                            for m, w in enumerate((Wk, Wv)):
                                sp.dma_start(view[:, m, :, :], w[:, bass.ds(g * HX, HX)]
                                             .rearrange("(c p) f -> p c f", p=P)).then_inc(raw_in[n], 16)
                        elif i < 3:
                            rows = slice((i - 1) * D // 2, i * D // 2)
                            sp.dma_start(raw[n][:].rearrange("p (c f) -> p c f", c=KC // 2),
                                         Wq[rows, bass.ds(g * NR * HX, NR * HX)].rearrange("(c p) f -> p c f", p=P))\
                                .then_inc(raw_in[n], 16)
                        else:
                            sp.dma_start(raw[n][:], Wo[bass.ds((g * NR + i - 3) * HX, HX), :]).then_inc(raw_in[n], 16)

                sp.dma_start(mask8[:].rearrange("p b s -> p (b s)"),
                             mask.rearrange("b s -> (b s)").rearrange("(o a) -> o a", o=1).to_broadcast([P, B * S]))\
                    .then_inc(mask_in, 16)
                load(0)
                with sp.Fori(1, G) as g:
                    load(g)

            @block.gpsimd
            def _(pool):
                def rounded(eng, hi, raw):
                    eng.sem_inc(rounding_next, 1)
                    return eng.tensor_copy(hi, raw)

                def split_weights(g):
                    loaded = ((64 * g + 32, 0), (32 * g + 16, 1), (64 * g + 48, 0), (32 * g + 32, 1), (64 * g + 64, 0))
                    for i, (count, n) in enumerate(loaded):
                        pool.wait_ge(raw_in[n], count)
                        if i == 0:
                            parts = [w[:].rearrange("p n c f -> p (n c f)") for w in kv_w]
                            reached(pool, k_done, B * g)
                            reached(pool, vT_done, B * g)
                        elif i < 3:
                            parts = [w[:, (i - 1) * KC // 2:i * KC // 2, :].rearrange("p c f -> p (c f)")
                                     for w in q_w]
                            reached(pool, q_done, NR * B * g)
                        else:
                            parts = [w[:, i - 3, :] for w in o_w]
                            reached(pool, out_done, QT * (NR * B * g - NR + i - 2) if not is_first(g) else 0)
                        rounded(pool, parts[0], raw[n][:]).then_inc(split, 1)
                        pool.wait_ge(split, 2 * (g * PIECES + i) + 1)
                        pool.tensor_tensor(parts[1], raw[n][:], parts[0].bitcast(F32), ALU.subtract)\
                            .then_inc(split, 1)

                split_weights(0)
                with pool.Fori(1, G) as g:
                    split_weights(g)

            @block.tensor
            def _(pe):
                def ctx_projection(u, bank, n):
                    cols = bass.ds(u % B * S, S)
                    return products(pe, bank[:], [(w[:, n, c, :], x[:, c, cols]) for c in range(CC)
                                                  for w, x in ((kv_w[0], ctxT_hi), (kv_w[0], ctxT_lo),
                                                               (kv_w[1], ctxT_hi))])

                def project_k(u):
                    pe.wait_ge(split, u // B * (2 * PIECES) + 2)
                    reached(pe, q_lo_done, 2 * u - 1)
                    ctx_projection(u, bank_a, 0).then_inc(k_done, 1)

                def project_vT(u):
                    pe.wait_ge(split, u // B * (2 * PIECES) + 2)
                    reached(pe, v_lo_done, u)
                    ctx_projection(u, bank_b, 1).then_inc(vT_done, 1)

                def turn_v(u):
                    pe.wait_ge(vT_copied, u + 1)
                    for q in range(QT):
                        last = pe.transpose(bank_b[:, q * HX:(q + 1) * HX], vT[:, q * P:(q + 1) * P], st.ident[:])
                    last.then_inc(v_done, 1)

                def project_q(u, r, part):
                    cols = bass.ds(u % B * S, S)
                    pairs = [(w[:, c, r * HX:(r + 1) * HX], x[:, c, cols]) for c in range(KC)
                             for w, x in ((q_w[0], st.xT_hi), (q_w[0], st.xT_lo), (q_w[1], st.xT_hi))]
                    if part:
                        for m in range(KC * part, KC * part + KC):
                            last = pe.matmul(bank_a[:], *pairs[m], start=False, stop=(m == 3 * KC - 1))
                        if part == 2:
                            last.then_inc(q_done, 1)
                        return
                    pe.wait_ge(split, u // B * (2 * PIECES) + 6)
                    if r == 0:
                        pe.wait_ge(k_lo_done, u + 1)
                        reached(pe, q_lo_done, 2 * u)
                    else:
                        pe.wait_ge(k_lo_done, NU if is_last(u) else u + 2)
                    for m in range(KC):
                        pe.matmul(bank_a[:], *pairs[m], start=(m == 0), stop=False)

                def score(u, s, r, q):
                    n = NR * u + r
                    if q == 0:
                        pe.wait_ge(q_lo_done, n + 1)
                    reached(pe, maxed, QT * n + q - 1)
                    tile = slice(q * P, (q + 1) * P)
                    products(pe, s_bank[q % 2][:], [(q_hi[r][:, tile], k_hi[s][:]), (q_hi[r][:, tile], k_lo[s][:]),
                                                    (q_lo[r][:, tile], k_hi[s][:])]).then_inc(scored, 1)

                def turn_probabilities(u, r, kt):
                    n = NR * u + r
                    pe.wait_ge(exp_done, QT * n + QT)
                    reached(pe, pT_lo_done, QT * n + kt - 1)
                    for q in range(QT):
                        last = pe.transpose(t_bank[kt % 2][:, q * P:(q + 1) * P], prob[:, q, kt * P:(kt + 1) * P],
                                            st.ident[:])
                    last.then_inc(turned, 1)

                def weigh(u, s, r, kt):
                    n = NR * u + r
                    pe.wait_ge(pT_lo_done, QT * n + kt + 1)
                    if kt == 0:
                        reached(pe, o_lo_done, n)
                        pe.wait_ge(v_lo_done, u + 1)
                    keys = slice(kt * HX, (kt + 1) * HX)
                    for m, (v, p_) in enumerate(((v_hi, pT_hi), (v_hi, pT_lo), (v_lo, pT_hi))):
                        last = pe.matmul(o_bank[:], v[s][:, keys], p_[:, kt % (QT - 1), :], start=(kt == 0 and m == 0),
                                         stop=(kt == QT - 1 and m == 2))
                    if kt == 0:
                        last.then_inc(weighed_first, 1)
                    if kt == QT - 1:
                        last.then_inc(weighed, 1)

                def project_out(n, r, q):
                    pe.wait_ge(o_lo_done, n + 1)
                    pe.wait_ge(split, n // (NR * B) * (2 * PIECES) + 8 + 2 * r)
                    reached(pe, added, QT * n + q)
                    tile = slice(q * P, (q + 1) * P)
                    products(pe, out_bank[:], [(o_hi[:, tile], o_w[0][:, r, :]), (o_hi[:, tile], o_w[1][:, r, :]),
                                               (o_lo[:, tile], o_w[0][:, r, :])]).then_inc(out_done, 1)

                def unit(u, s):
                    for r in range(NR):
                        n = NR * u + r

                        def out(q):
                            if not (is_first(u) and r == 0):
                                project_out(n - 1, 1 - r, q)

                        def next_q(part):
                            if r == 0:
                                project_q(u, 1, part)
                            elif not is_last(u):
                                project_q(u + 1, 0, part)

                        def next_score(q):
                            if r == 0:
                                score(u, s, 1, q)
                            elif not is_last(u):
                                score(u + 1, 1 - s, 0, q)

                        score(u, s, r, 2)
                        if r == 0:
                            if not is_last(u):
                                project_k(u + 1)
                            score(u, s, r, 3)
                            out(0)
                            if not is_last(u):
                                project_vT(u + 1)
                            out(1)
                            next_q(0)
                            next_q(1)
                            out(2)
                            next_q(2)
                            turn_probabilities(u, r, 0)
                            out(3)
                            turn_probabilities(u, r, 1)
                        else:
                            next_q(0)
                            score(u, s, r, 3)
                            out(0)
                            next_q(1)
                            out(1)
                            next_q(2)
                            if not is_last(u):
                                turn_v(u + 1)
                            out(2)
                            turn_probabilities(u, r, 0)
                            turn_probabilities(u, r, 1)
                            out(3)
                        turn_probabilities(u, r, 2)
                        weigh(u, s, r, 0)
                        turn_probabilities(u, r, 3)
                        weigh(u, s, r, 1)
                        next_score(0)
                        weigh(u, s, r, 2)
                        next_score(1)
                        weigh(u, s, r, 3)

                project_k(0)
                project_vT(0)
                turn_v(0)
                for part in range(3):
                    project_q(0, 0, part)
                score(0, 0, 0, 0)
                score(0, 0, 0, 1)
                units(pe, unit)
                for q in range(QT):
                    project_out(NR * NU - 1, 1, q)

            @block.scalar
            def _(act):
                def take_k(u, s):
                    act.wait_ge(k_done, u + 1)
                    reached(act, scored, NR * QT * (u - 1))
                    act.activation(k_hi[s][:], bank_a[:], ACT.Copy).then_inc(k_hi_done, 1)

                def take_vT(u):
                    act.wait_ge(vT_done, u + 1)
                    reached(act, v_done, u)
                    act.activation(vT[:], bank_b[:], ACT.Copy).then_inc(vT_copied, 1)

                def take_v(u, s):
                    act.wait_ge(v_done, u + 1)
                    reached(act, weighed, NR * (u - 1))
                    act.activation(v_hi[s][:], bank_b[:], ACT.Copy).then_inc(v_hi_done, 1)

                def take_q(u, r):
                    n = NR * u + r
                    act.wait_ge(q_done, n + 1)
                    reached(act, scored, QT * (n - 1))
                    act.activation(q_hi[r][:], bank_a[:], ACT.Copy).then_inc(q_hi_done, 1)

                def exponential(u, r, q):
                    n = NR * u + r
                    act.wait_ge(maxed, QT * n + q + 1)
                    reached(act, clamped, n - 1)
                    act.activation(prob[:, q, :], prob[:, q, :], ACT.Exp, bias=nmax[:, q:q + 1], scale=-1.0,
                                   accum_out=den[:, r, 0, q:q + 1]).then_inc(exp_done, 1)

                def unit(u, s):
                    for r in range(NR):
                        n = NR * u + r
                        exponential(u, r, 2)
                        if r == 0 and not is_last(u):
                            take_k(u + 1, 1 - s)
                        exponential(u, r, 3)
                        if r == 0:
                            if not is_last(u):
                                take_vT(u + 1)
                            take_q(u, 1)
                        elif not is_last(u):
                            take_q(u + 1, 0)
                            take_v(u + 1, 1 - s)
                        for kt in range(QT):
                            act.wait_ge(turned, QT * n + kt + 1)
                            reached(act, weighed, n)
                            if kt == QT - 1:
                                act.wait_ge(weighed_first, n + 1)
                            act.activation(pT_hi[:, kt % (QT - 1), :], t_bank[kt % 2][:], ACT.Copy)\
                                .then_inc(pT_hi_done, 1)
                        for q in range(2):
                            if r == 0:
                                exponential(u, 1, q)
                            elif not is_last(u):
                                exponential(u + 1, 0, q)
                        act.wait_ge(weighed, n + 1)
                        reached(act, out_done, QT * n)
                        act.activation(o_hi[:], o_bank[:], ACT.Copy).then_inc(o_hi_done, 1)

                take_k(0, 0)
                take_vT(0)
                take_v(0, 0)
                take_q(0, 0)
                exponential(0, 0, 0)
                exponential(0, 0, 1)
                units(act, unit)

            @block.vector
            def _(dve):
                def take_lo(hi_done, count, lo, bank, hi, lo_done):
                    dve.wait_ge(hi_done, count)
                    dve.tensor_tensor(lo, bank, hi.bitcast(F32), ALU.subtract).then_inc(lo_done, 1)

                def take_k(u, s):
                    take_lo(k_hi_done, u + 1, k_lo[s][:], bank_a[:], k_hi[s][:], k_lo_done)

                def take_v(u, s):
                    take_lo(v_hi_done, u + 1, v_lo[s][:], bank_b[:], v_hi[s][:], v_lo_done)

                def take_q(u, r):
                    take_lo(q_hi_done, NR * u + r + 1, q_lo[r][:], bank_a[:], q_hi[r][:], q_lo_done)

                def maximum(u, r, q):
                    n = NR * u + r
                    dve.wait_ge(scored, QT * n + q + 1)
                    reached(dve, turned, QT * n)
                    dve.wait_ge(mask_ready, u + 1)
                    dve.sem_inc(maximum_next, 1)
                    dve.tensor_tensor_reduce(prob[:, q, :], s_bank[q % 2][:], mask_bias[:], -scale, -LOW * 1e-5,
                                             ALU.add, ALU.min, nmax[:, q:q + 1]).then_inc(maxed, 1)

                def bias_of(u):
                    reached(dve, maxed, NR * QT * u)
                    dve.tensor_scalar(mask_bias[:], mask8[:, bass.ds(u % B, 1), :].rearrange("p a s -> p (a s)"),
                                      -LOW, LOW, ALU.mult, ALU.add).then_inc(mask_ready, 1)

                def take_pT(u, r, kt):
                    slot = kt % (QT - 1)
                    take_lo(pT_hi_done, QT * (NR * u + r) + kt + 1, pT_lo[:, slot, :], t_bank[kt % 2][:],
                            pT_hi[:, slot, :], pT_lo_done)

                def add(n, r, q):
                    dve.wait_ge(out_done, QT * n + q + 1)
                    xt = st.x[:, bass.ds(n // NR % B * QT + q, 1), :].rearrange("p a d -> p (a d)")
                    dve.scalar_tensor_tensor(xt, out_bank[:], den[:, r, 2, q:q + 1], xt, ALU.mult, ALU.add)\
                        .then_inc(added, 1)

                def unit(u, s):
                    for r in range(NR):
                        n = NR * u + r

                        def add_last(q):
                            if not (is_first(u) and r == 0):
                                add(n - 1, 1 - r, q)

                        maximum(u, r, 2)
                        maximum(u, r, 3)
                        add_last(0)
                        if r == 0 and not is_last(u):
                            take_k(u + 1, 1 - s)
                        dve.wait_ge(exp_done, QT * n + QT)
                        dve.tensor_scalar(den[:, r, 1, :], den[:, r, 0, :], 1e-30, None, ALU.max).then_inc(clamped, 1)
                        dve.wait_ge(clamped, n + 1)
                        dve.reciprocal(den[:, r, 2, :], den[:, r, 1, :]).then_inc(inverted, 1)
                        add_last(1)
                        if r == 0:
                            add_last(2)
                            take_q(u, 1)
                            take_pT(u, r, 0)
                            add_last(3)
                            take_pT(u, r, 1)
                        else:
                            if not is_last(u):
                                take_q(u + 1, 0)
                            add_last(2)
                            take_pT(u, r, 0)
                            if not is_last(u):
                                take_v(u + 1, 1 - s)
                            take_pT(u, r, 1)
                            add_last(3)
                        take_pT(u, r, 2)
                        take_pT(u, r, 3)
                        if r == 0:
                            maximum(u, 1, 0)
                            maximum(u, 1, 1)
                        elif not is_last(u):
                            bias_of(u + 1)
                            maximum(u + 1, 0, 0)
                            maximum(u + 1, 0, 1)
                        take_lo(o_hi_done, n + 1, o_lo[:], o_bank[:], o_hi[:], o_lo_done)
                        dve.wait_ge(inverted, n + 1)

                dve.wait_ge(mask_in, 16)
                take_k(0, 0)
                take_v(0, 0)
                take_q(0, 0)
                bias_of(0)
                maximum(0, 0, 0)
                maximum(0, 0, 1)
                units(dve, unit)
                for q in range(QT):
                    add(NR * NU - 1, 1, q)


_INS = ["x", "ctx_1024", "mask_BxS2_bf1", "L0_attn_Wq_w", "L0_attn_Wq_b", "L0_attn_Wk_w", "L0_attn_Wk_b",
        "L0_attn_Wv_w", "L0_attn_Wv_b", "L0_xattn_Wq", "L0_xattn_bq", "L0_xattn_Wk", "L0_xattn_bk",
        "L0_ffn_gate_up_packed", "L0_ffn_gate_up_scales", "L0_ffn_down_packed", "L0_ffn_down_scales",
        "L1_attn_Wqkv_w", "L1_attn_Wqkv_b", "L1_attn_out_w", "L1_attn_out_b", "L1_xattn_Wq", "L1_xattn_Wk",
        "L1_xattn_Wv", "L1_xattn_Wo", "L1_ffn_Wr", "L1_ffn_U", "L1_ffn_V", "L1_ffn_attr", "L1_ffn_Wa"]
_OUTS = [((B, S, D), "float32")]


def decoder(nc, x, ctx_in, mask, l0_Wq, l0_bq, l0_Wk, l0_bk, l0_Wv, l0_bv, x0_Wq, x0_bq, x0_Wk, x0_bk,
            gate_up_packed, gate_up_scales, down_packed, down_scales, Wqkv, bqkv, out_w, out_b, x1_Wq, x1_Wk,
            x1_Wv, x1_Wo, Wr, U, V, attr, Wa, out):
    with ExitStack() as ctx:
        st = State(nc, ctx)
        persistent(st)
        st.stage(setup, x)
        st.stage(layer0_attention, l0_Wq, l0_bq, l0_Wk, l0_bk, l0_Wv, l0_bv)
        st.stage(feature_attention, ctx_in, x0_Wq, x0_bq, x0_Wk, x0_bk)
        st.stage(packed_ffn, gate_up_packed, gate_up_scales, down_packed, down_scales)
        st.stage(layer1_attention, Wqkv, bqkv, out_w, out_b)
        st.stage(cross_attention, ctx_in, mask, x1_Wq, x1_Wk, x1_Wv, x1_Wo)
        st.stage(routed_mixture, Wr, U, V, attr, Wa, out)


def kernel(**inputs):
    import numpy as _np
    import concourse.bacc as _bacc
    from concourse import mybir as _mybir
    from concourse.bass_utils import run_bass_kernel_spmd as _run

    nc = _bacc.Bacc("TRN2", target_bir_lowering=False, num_devices=1)
    arrays, args = {}, []
    for name in _INS:
        a = _np.ascontiguousarray(inputs[name])
        arrays[f"in_{name}_dram"] = a
        args.append(nc.dram_tensor(f"in_{name}_dram", a.shape, _mybir.dt.from_np(a.dtype), kind="ExternalInput").ap())
    for i, (shape, dtype) in enumerate(_OUTS):
        dt = _mybir.dt.from_np(_np.dtype(dtype))
        args.append(nc.dram_tensor(f"out_{i}_dram", shape, dt, kind="ExternalOutput").ap())
    decoder(nc, *args)
    r = _run(nc, [arrays], core_ids=[0])
    return r.results[0]["out_0_dram"]
```

```python
from contextlib import ExitStack

import concourse.bass as bass
from concourse import mybir

P = 128
F32 = mybir.dt.float32
F32R = mybir.dt.float32r
BF16 = mybir.dt.bfloat16
F16 = mybir.dt.float16
I32 = mybir.dt.int32
U32 = mybir.dt.uint32
U8 = mybir.dt.uint8
ALU = mybir.AluOpType
ACT = mybir.ActivationFunctionType
AX = mybir.AxisListType

B, S, D = 4, 512, 512
QT = S // P
T = B * QT
KC = D // P
TOK = B * S
NH, HD = 16, 32
C = 256
CC = C // P


class State:

    def __init__(self, nc, ctx):
        self.nc, self.ctx, self.used, self.taken = nc, ctx, 0, []

    def sem(self, name):
        self.used += 1
        self.taken.append(self.nc.alloc_semaphore(name=f"{name}_{self.used}"))
        return self.taken[-1]

    def stage(self, build, *args):
        build(self, *args)
        self.nc.all_engine_barrier()
        self.nc.clear_and_free_semaphores(self.taken)
        self.nc.all_engine_barrier()
        self.taken = []

    def sems(self, *names):
        return [self.sem(n) for n in names]


def tensors(nc, stack):
    def sb(name, shape, dt):
        return stack.enter_context(nc.sbuf_tensor(name, shape, dt))

    def ps(name, shape, dt=F32):
        return stack.enter_context(nc.psum_tensor(name, shape, dt))

    return sb, ps


def reached(eng, sem, count):
    if not (isinstance(count, int) and count <= 0):
        eng.wait_ge(sem, count)


def setup(st, x_in):
    nc = st.nc
    x_loaded, zeroed, made = st.sems("x_loaded", "ident_zeroed", "ident_made")
    with nc.Block() as block:

        @block.sync
        def _(sp):
            sp.dma_start(st.x[:], x_in.rearrange("b (q p) d -> p (b q) d", p=P)).then_inc(x_loaded, 16)
            sp.wait_ge(x_loaded, 16)

        @block.gpsimd
        def _(pool):
            pool.memset(st.ident[:], 0.0).then_inc(zeroed, 1)
            pool.wait_ge(zeroed, 1)
            pool.affine_select(out=st.ident[:], in_=st.ident[:], compare_op=ALU.not_equal, fill=1.0, base=0,
                               pattern=[[-1, P]], channel_multiplier=1).then_inc(made, 1)

        @block.vector
        def _(dve):
            dve.wait_ge(made, 1)
            dve.tensor_copy(st.ident_r[:], st.ident[:])


class Preparation:

    def __init__(self, st, loads, jobs, fills):
        self.st, self.loads, self.jobs, self.fills, self.banks = st, loads, jobs, fills, []
        self.loaded, self.filled, self.turned, self.hi_done, self.lo_done = st.sems(
            "w_loaded", "w_filled", "w_turned", "w_hi", "w_lo")

    def load(self, sp):
        if self.fills:
            sp.wait_ge(self.filled, len(self.fills))
        for dst, src in self.loads:
            sp.dma_start(dst, src, allow_slow_non_contiguous=dst.shape[-1] <= 16).then_inc(self.loaded, 16)

    def fill(self, pool):
        for t in self.fills:
            pool.memset(t, 0.0).then_inc(self.filled, 1)

    def turn(self, pe, j):
        sources, hi, lo = self.jobs[j]
        bank = self.banks[j % len(self.banks)]
        if j == 0:
            pe.wait_ge(self.loaded, 16 * len(self.loads))
        if j >= len(self.banks):
            pe.wait_ge(self.lo_done, j - len(self.banks) + 1)
        at = 0
        for s in sources:
            rows, cols = s.shape
            last = pe.transpose(bank[0:cols, at:at + rows], s, self.st.ident[0:rows, 0:rows])
            at += rows
        last.then_inc(self.turned, 1)

    def view(self, j):
        sources, hi, lo = self.jobs[j]
        n = sum(s.shape[0] for s in sources)
        v = self.banks[j % len(self.banks)][0:sources[0].shape[1], 0:n]
        if len(hi.shape) == 3:
            v = v.rearrange("p (a b) -> p a b", a=hi.shape[1])
        if len(hi.shape) == 4:
            v = v.rearrange("p (a b c) -> p a b c", a=hi.shape[1], b=hi.shape[2])
        return v, hi, lo

    def take_hi(self, act, j):
        v, hi, lo = self.view(j)
        if j == 0 and self.fills:
            act.wait_ge(self.filled, len(self.fills))
        act.wait_ge(self.turned, j + 1)
        act.activation(hi, v, ACT.Copy).then_inc(self.hi_done, 1)

    def take_lo(self, dve, j):
        v, hi, lo = self.view(j)
        if j == 0 and self.fills:
            dve.wait_ge(self.filled, len(self.fills))
        dve.wait_ge(self.hi_done, j + 1)
        dve.tensor_tensor(lo, v, hi.bitcast(F32), ALU.subtract).then_inc(self.lo_done, 1)


def norm_stats(st, dve, std_ready, var_ready, chain, bn, mv, weights):
    n = [0]

    def link(ins, k=1):
        n[0] += k
        ins.then_inc(chain, 1)
        dve.wait_ge(chain, n[0])

    with dve.Fori(0, T) as t:
        dve.bn_stats(bn[:, t, :], st.x[:, t, :]).then_inc(chain, 1)
    weights()
    n[0] = T
    dve.wait_ge(chain, T)
    mean_e, m2_e, mean_o, m2_o = (bn[:, :, k] for k in (1, 2, 4, 5))
    link(dve.tensor_tensor(mv[:, 0, :], mean_e, mean_o, ALU.add))
    link(dve.tensor_tensor(mv[:, 5, :], mean_e, mean_o, ALU.subtract))
    link(dve.tensor_tensor(mv[:, 6, :], m2_e, m2_o, ALU.add))
    link(dve.tensor_tensor(mv[:, 5, :], mv[:, 5, :], mv[:, 5, :], ALU.mult))
    link(dve.tensor_scalar(mv[:, 6, :], mv[:, 6, :], 1.0 / D, 1e-5, ALU.mult, ALU.add))
    dve.scalar_tensor_tensor(mv[:, 1, :], mv[:, 5, :], 0.25, mv[:, 6, :], ALU.mult, ALU.add).then_inc(var_ready, 1)
    dve.wait_ge(std_ready, 1)
    link(dve.reciprocal(mv[:, 3, :], mv[:, 2, :]))
    link(dve.scalar_tensor_tensor(mv[:, 4, :], mv[:, 0, :], -0.5, mv[:, 3, :], ALU.mult, ALU.mult))


def norm_to_features(st, name, loads=(), jobs=(), fills=()):
    nc = st.nc
    R = 4
    var_ready, std_ready, chain, xn_ready, turned, hi_done, bank_free = st.sems(
        "var_ready", "std_ready", "norm_chain", "xn_ready", "x_turned", "xT_hi_done", "x_bank_free")
    prep = Preparation(st, loads, jobs, fills)
    with ExitStack() as stack:
        sb, ps = tensors(nc, stack)
        bn = sb(f"{name}_bn", [P, T, 6], F32)
        mv = sb(f"{name}_mv", [P, 7, T], F32)
        xn = [sb(f"{name}_xn{s}", [P, D], F32) for s in range(R)]
        bank = [ps(f"{name}_bank{s}", [P, KC, P]) for s in range(R)]
        prep.banks = [ps(f"{name}_w_bank{s}", [P, 512]) for s in range(R)] if jobs else []
        with nc.Block() as block:

            @block.sync
            def _(sp):
                prep.load(sp)
                if loads:
                    sp.wait_ge(prep.loaded, 16 * len(loads))

            @block.gpsimd
            def _(pool):
                prep.fill(pool)

            @block.vector
            def _(dve):
                def weights():
                    for j in range(len(jobs)):
                        prep.take_lo(dve, j)

                norm_stats(st, dve, std_ready, var_ready, chain, bn, mv, weights)

                def normalise(t):
                    if t >= R:
                        dve.wait_ge(bank_free, t - R + 1)
                    dve.tensor_scalar(xn[t % R][:], st.x[:, t, :], mv[:, 3, t:t + 1], mv[:, 4, t:t + 1], ALU.mult,
                                      ALU.add).then_inc(xn_ready, 1)

                for t in range(R - 1):
                    normalise(t)
                for t in range(T):
                    if t + R - 1 < T:
                        normalise(t + R - 1)
                    dve.wait_ge(hi_done, t + 1)
                    cols = slice(t * P, (t + 1) * P)
                    dve.tensor_tensor(st.xT_lo[:, :, cols], bank[t % R][:], st.xT_hi[:, :, cols].bitcast(F32),
                                      ALU.subtract).then_inc(bank_free, 1)

            @block.scalar
            def _(act):
                for j in range(len(jobs)):
                    prep.take_hi(act, j)
                act.wait_ge(var_ready, 1)
                act.activation(mv[:, 2, :], mv[:, 1, :], ACT.Sqrt).then_inc(std_ready, 1)
                for t in range(T):
                    act.wait_ge(turned, t + 1)
                    act.activation(st.xT_hi[:, :, t * P:(t + 1) * P], bank[t % R][:], ACT.Copy).then_inc(hi_done, 1)

            @block.tensor
            def _(pe):
                for j in range(len(jobs)):
                    prep.turn(pe, j)
                for t in range(T):
                    pe.wait_ge(xn_ready, t + 1)
                    if t >= R:
                        pe.wait_ge(bank_free, t - R + 1)
                    for c in range(KC):
                        last = pe.transpose(bank[t % R][:, c, :], xn[t % R][:, c * P:(c + 1) * P], st.ident[:])
                    last.then_inc(turned, 1)


def project(st, name, wT_hi, wT_lo, bias, kinds, q_dram, k_dram, v, vh):
    nc = st.nc
    NT = len(kinds)
    NV = kinds.count("v")
    NQK = NT - NV
    assert NT % 2 == 0 and all(k == "v" for k in kinds[NQK:])
    in_slot = [len(range(s, NQK, 2)) for s in range(2)]
    rows = vh * HD
    V_LAG = min(NV, 2)
    projected, hi_done, lo_done, vT_ready, v_turned, v_read = st.sems(
        "projected", "hi_done", "lo_done", "vT_ready", "v_turned", "v_read")
    stored = st.sems("stored_0", "stored_1")
    with ExitStack() as stack:
        sb, ps = tensors(nc, stack)
        hi = [sb(f"{name}_hi{s}", [P, S], F32R) for s in range(2)]
        lo = [sb(f"{name}_lo{s}", [P, S], F32R) for s in range(2)]
        vT = [sb(f"{name}_vT{s}", [P, S], F32) for s in range(2)]
        bank = [ps(f"{name}_bank{s}", [P, S]) for s in range(2)]
        v_bank = ps(f"{name}_v_bank", [P, QT, P])

        with nc.Block() as block:

            @block.tensor
            def _(pe):
                pe.sem_inc(v_turned, 2)
                with pe.Fori(0, B) as b:
                    def turn_v(n):
                        pe.wait_ge(vT_ready, b * NV + n + 3)
                        pe.wait_ge(v_read, b * NV + n + 1)
                        for q in range(QT):
                            last = pe.transpose(v_bank[:, q, :], vT[n % 2][:, q * P:(q + 1) * P], st.ident[:])
                        last.then_inc(v_turned, 1)

                    for f in range(NT):
                        g = (f - 2) % NT
                        back = 1 if f < 2 else 0
                        if g < NQK:
                            pe.wait_ge(lo_done, (b - back + 1) * NQK + g + 1)
                        else:
                            pe.wait_ge(vT_ready, (b - back) * NV + g - NQK + 3)
                        n = 0
                        for c in range(KC):
                            for w, m in ((wT_hi, st.xT_hi), (wT_hi, st.xT_lo), (wT_lo, st.xT_hi)):
                                last = pe.matmul(bank[f % 2][:], w[:, c, f * P:(f + 1) * P],
                                                 m[:, c, bass.ds(b * S, S)], start=(n == 0), stop=(n == 3 * KC - 1))
                                n += 1
                        last.then_inc(projected, 1)
                        if f > NQK:
                            turn_v(f - 1 - NQK)
                    turn_v(NV - 1)

            @block.scalar
            def _(act):
                act.sem_inc(vT_ready, 2)
                with act.Fori(0, B) as b:
                    for f in range(NT):
                        act.wait_ge(projected, b * NT + f + 1)
                        if f >= NQK:
                            n = f - NQK
                            act.wait_ge(v_turned, b * NV + n + 3 - V_LAG)
                            act.activation(vT[n % 2][:], bank[f % 2][:], ACT.Identity,
                                           bias=bias[:, f:f + 1]).then_inc(vT_ready, 1)
                        else:
                            act.wait_ge(stored[f % 2], 32 * (b * in_slot[f % 2] + f // 2) + 32)
                            act.activation(hi[f % 2][:], bank[f % 2][:], ACT.Identity,
                                           bias=bias[:, f:f + 1]).then_inc(hi_done, 1)

            @block.vector
            def _(dve):
                dve.sem_inc(lo_done, NQK)
                dve.sem_inc(v_read, 1)
                with dve.Fori(0, B) as b:
                    for f in range(NT):
                        if f >= NQK:
                            n = f - NQK
                            dve.wait_ge(v_turned, b * NV + n + 3)
                            for q in range(QT):
                                last = dve.tensor_copy(v[:, b * QT + q, n * vh:(n + 1) * vh, 0:HD],
                                                       v_bank[:, q, 0:rows].rearrange("p (h d) -> p h d", h=vh))
                            last.then_inc(v_read, 1)
                        else:
                            dve.wait_ge(hi_done, b * NQK + f + 1)
                            dve.scalar_tensor_tensor(lo[f % 2][:], bank[f % 2][:], bias[:, f:f + 1],
                                                     hi[f % 2][:].bitcast(F32), ALU.add, ALU.subtract)\
                                .then_inc(lo_done, 1)

            @block.sync
            def _(sp):
                for s in range(2):
                    sp.sem_inc(stored[s], 32)
                with sp.Fori(0, B) as b:
                    for f in range(NQK):
                        dram, f0 = (q_dram, f) if kinds[f] == "q" else (k_dram, f - kinds.index("k"))
                        n = min(P, dram.shape[1])
                        sp.wait_ge(lo_done, b * NQK + f + 1 + NQK)
                        for part, tile in enumerate((hi, lo)):
                            sp.dma_start(dram[part, f0 * P:f0 * P + n, bass.ds(b * S, S)], tile[f % 2][0:n, :].bitcast(F32))\
                                .then_inc(stored[f % 2], 16)
                for s in range(2):
                    sp.wait_ge(stored[s], 32 * (B * in_slot[s] + 1))


def attend(st, name, q_dram, k_dram, v, per_head, out):
    nc = st.nc
    N = B * NH
    scale = HD ** -0.5
    STK = 3 * HD
    maxed, max_read, mrow_in, mrow_turned, mrow_ready, scored, exp_done, weighed, o_read = st.sems(
        "maxed", "max_read", "mrow_in", "mrow_turned", "mrow_ready", "scored", "exp_done", "weighed", "o_read")
    turned, oT_ready = st.sems("turned", "oT_ready")
    max_hi_done, rden_done, on_done, made, v_staged, v_hi_done, split_next, pT_hi_done, pT_lo_done, cleared, \
        last_lo_done, ks_made, vs_cleared, vs_made = st.sems(
        "max_hi_done", "rden_done", "on_done", "made", "v_staged", "v_hi_done", "split_next", "pT_hi_done",
        "pT_lo_done", "cleared", "last_lo_done", "ks_made", "vs_cleared", "vs_made")
    R = 4
    loaded = st.sems(*(f"qk_loaded_{s}" for s in range(R)))
    add = out is st.x
    with ExitStack() as stack:
        sb, ps = tensors(nc, stack)
        qs, ks = ([st.xT_hi[:, row, s * S:(s + 1) * S] for s in range(R)] for row in (2, 3))
        pT_hi, pT_lo = ([w[:, s, :].rearrange("p (k q) -> p k q", k=QT) for s in range(2)]
                        for w in (st.xT_hi, st.xT_lo))
        pT = [sb(f"{name}_pT{s}", [P, QT, S], F32) for s in range(2)]
        mx = sb(f"{name}_mx", [P, QT, 1], F32)
        ms = sb(f"{name}_ms", [P, QT, P], F32R)
        rden = sb(f"{name}_rden", [P, QT, 1], F32)
        warm = sb(f"{name}_warm", [P, 1], F32)
        on = sb(f"{name}_on", [P, QT, HD], F32)
        vs = [sb(f"{name}_vs{s}", [P, QT, P], F32R) for s in range(2)]
        OUTS = 2 * HD + 1
        fold = sb(f"{name}_fold", [OUTS, HD + 1], F32)
        max_bank = ps(f"{name}_max_bank", [P, 2, S])
        score_bank = ps(f"{name}_score_bank", [P, QT, S])
        o_bank = ps(f"{name}_o_bank", [P, 512])
        m_bank = ps(f"{name}_m_bank", [P, QT, P])
        oT = sb(f"{name}_oT", [OUTS, S], F32)
        o4 = o_bank[:, 0:QT * (HD + 1)].rearrange("p (q d) -> p q d", q=QT)

        def rounds(eng, body):
            for s in range(R):
                body(s, s)
            with eng.Fori(1, N // R - 1) as j:
                for s in range(R):
                    body(R * j + s, s)
            for s in range(R):
                body(N - R + s, s)

        with nc.Block() as block:

            @block.sync
            def _(sp):
                def load(i, s):
                    b, h = i // NH, i % NH
                    cols, rows = bass.ds(b * S, S), bass.ds(h * HD, HD)
                    krows = rows if per_head else slice(0, HD)
                    sp.dma_start(qs[s][0:HD, :].bitcast(F32), q_dram[0, rows, cols]).then_inc(loaded[s], 16)
                    sp.dma_start(qs[s][HD:3 * HD, :].bitcast(F32), q_dram[:, rows, cols]).then_inc(loaded[s], 16)
                    sp.dma_start(ks[s][0:2 * HD, :].bitcast(F32), k_dram[:, krows, cols]).then_inc(loaded[s], 16)
                    sp.dma_start(ks[s][2 * HD:3 * HD, :].bitcast(F32), k_dram[0, krows, cols]).then_inc(loaded[s], 16)

                for s in range(R):
                    load(s, s)
                with sp.Fori(1, N // R) as j:
                    for s in range(R):
                        i = R * j + s
                        sp.wait_ge(scored, 2 * (i - R + 1))
                        load(i, s)

            @block.tensor
            def _(pe):
                def maxes(i, s, half):
                    if half == 0:
                        pe.wait_ge(loaded[s], 64 // R * (i - s) + 64)
                    pe.wait_ge(max_read, 2 * i + half + 1)
                    for q in range(2):
                        c = (2 * half + q) * P
                        last = pe.matmul(max_bank[:, q, :], qs[s][0:STK, c:c + P], ks[s][0:STK, :],
                                         start=True, stop=True)
                    last.then_inc(maxed, 1)

                def max_rows(i):
                    pe.wait_ge(mrow_in, i + 1)
                    pe.wait_ge(mrow_ready, i + 1)
                    for q in range(QT):
                        last = pe.matmul(m_bank[:, q, :], ms[:, q, :], st.ident_r[:], start=True, stop=True)
                    last.then_inc(mrow_turned, 1)

                def scores(i, s, half):
                    pe.wait_ge(mrow_ready, i + 2)
                    pe.wait_ge(exp_done, 2 * i + half + 1)
                    for kt in (2 * half, 2 * half + 1):
                        last = pe.matmul(score_bank[:, kt, :], ks[s][0:STK + 2, kt * P:(kt + 1) * P],
                                         qs[s][0:STK + 2, :], start=True, stop=True)
                    last.then_inc(scored, 1)

                def weigh(i, s, half):
                    if half == 0:
                        pe.wait_ge(v_staged, i + 1)
                        pe.wait_ge(o_read, i + 1)
                    pe.wait_ge(pT_lo_done, 2 * i + half + 5)
                    if half:
                        pe.wait_ge(last_lo_done, i + 3)
                    for kt in (2 * half, 2 * half + 1):
                        for m, part in enumerate((pT_hi, pT_lo)):
                            last = pe.matmul(o_bank[:], vs[s % 2][:, kt, :], part[s % 2][:, kt, :],
                                             start=(kt == 0 and m == 0), stop=(kt == QT - 1 and m == 1))
                    if half:
                        last.then_inc(weighed, 1)

                def turn(i):
                    pe.wait_ge(oT_ready, i + 1)
                    for q in range(QT):
                        last = pe.matmul(o4[:, q, :], oT[:, q * P:(q + 1) * P], fold[:],
                                         start=True, stop=True)
                    last.then_inc(turned, 1)

                def step(i, s):
                    first, final = isinstance(i, int) and i == 0, isinstance(i, int) and i == N - 1
                    scores(i, s, 0)
                    scores(i, s, 1)
                    if not final:
                        maxes(i + 1, (s + 1) % R, 1)
                    if not first:
                        weigh(i - 1, s - 1, 0)
                        weigh(i - 1, s - 1, 1)
                    if not (isinstance(i, int) and i >= N - 2):
                        maxes(i + 2, (s + 2) % R, 0)
                    if not final:
                        max_rows(i + 1)
                    if not first:
                        turn(i - 1)

                pe.sem_inc(mrow_turned, 1)
                pe.sem_inc(weighed, 2)
                maxes(0, 0, 0)
                maxes(0, 0, 1)
                pe.wait_ge(made, 1)
                pe.wait_ge(ks_made, 1)
                max_rows(0)
                maxes(1, 1, 0)
                rounds(pe, step)
                weigh(N - 1, 1, 0)
                weigh(N - 1, 1, 1)
                turn(N - 1)

            @block.gpsimd
            def _(pool):
                pool.sem_inc(last_lo_done, 2)
                for s in range(R):
                    last = pool.memset(ks[s][STK:STK + 2, :].bitcast(F32), 1.0)
                last.then_inc(ks_made, 1)
                pool.wait_ge(ks_made, 1)
                for w in vs:
                    last = pool.memset(w[:].bitcast(F32), 0.0)
                last.then_inc(vs_cleared, 1)
                pool.wait_ge(vs_cleared, 1)
                for w in vs:
                    last = pool.memset(w[:, :, 2 * HD:OUTS].bitcast(F32), 1.0)
                last.then_inc(vs_made, 1)
                pool.wait_ge(vs_made, 1)
                with pool.Fori(0, N // 2) as j:
                    for s in range(2):
                        i = 2 * j + s
                        pool.wait_ge(weighed, i + 1)
                        values = v[:, bass.ds(i // NH * QT, QT), i % NH if per_head else 0, :]
                        pool.tensor_copy(vs[s][:, :, 0:HD], values).then_inc(v_hi_done, 1)
                        pool.wait_ge(v_hi_done, i + 1)
                        pool.sem_inc(split_next, 1)
                        pool.tensor_tensor(vs[s][:, :, HD:2 * HD], values, vs[s][:, :, 0:HD].bitcast(F32),
                                           ALU.subtract).then_inc(v_staged, 1)
                        pool.wait_ge(pT_hi_done, 2 * i + 2)
                        pool.tensor_tensor(pT_lo[s][:, QT - 1, :], pT[s][:, QT - 1, :],
                                           pT_hi[s][:, QT - 1, :].bitcast(F32), ALU.subtract)\
                            .then_inc(last_lo_done, 1)

            @block.scalar
            def _(act):
                act.sem_inc(exp_done, 2)
                act.sem_inc(mrow_ready, 1)

                def rows(i, s):
                    act.wait_ge(mrow_turned, i + 2)
                    act.activation(qs[s][STK:STK + 2, :], m_bank[STK:STK + 2, :, :].rearrange("p q c -> p (q c)"),
                                   ACT.Copy).then_inc(mrow_ready, 1)

                def take_oT(i):
                    act.wait_ge(weighed, i + 3)
                    act.activation(oT[:], o_bank[0:OUTS, :], ACT.Copy).then_inc(oT_ready, 1)

                def step(i, s):
                    def take_hi(half):
                        tiles = slice(2 * half, 2 * half + 2)
                        act.wait_ge(exp_done, 2 * i + half + 3)
                        act.wait_ge(weighed, i + 1)
                        act.activation(pT_hi[s % 2][:, tiles, :], pT[s % 2][:, tiles, :], ACT.Copy)\
                            .then_inc(pT_hi_done, 1)

                    for half in range(2):
                        tiles = slice(2 * half, 2 * half + 2)
                        act.wait_ge(scored, 2 * i + half + 1)
                        act.wait_ge(pT_lo_done, 2 * i + half + 1)
                        if half:
                            act.wait_ge(last_lo_done, i + 1)
                        act.activation(pT[s % 2][:, tiles, :], score_bank[:, tiles, :], ACT.Exp, scale=scale)\
                            .then_inc(exp_done, 1)
                    take_hi(0)
                    if not isinstance(i, int) or i >= 1:
                        take_oT(i - 1)
                    if not isinstance(i, int) or i < N - 1:
                        rows(i + 1, (s + 1) % R)
                    take_hi(1)

                act.activation(warm[:], st.ident[:, 0:1], ACT.Exp)
                rows(0, 0)
                rounds(act, step)
                take_oT(N - 1)

            @block.vector
            def _(dve):
                def reduce(i, half):
                    if half == 0:
                        reached(dve, mrow_in, i)
                    dve.wait_ge(maxed, 2 * i + half + 1)
                    dve.tensor_reduce(mx[:, 2 * half:2 * half + 2, 0], max_bank[:], AX.X, ALU.max)\
                        .then_inc(max_read, 1)

                def split_max(i):
                    dve.wait_ge(max_read, 2 * i + 3)
                    dve.wait_ge(mrow_turned, i + 1)
                    dve.tensor_scalar(ms[:, :, STK:STK + 1], mx[:], -1.0, None, ALU.mult).then_inc(max_hi_done, 1)
                    dve.wait_ge(max_hi_done, i + 1)
                    dve.scalar_tensor_tensor(ms[:, :, STK + 1:STK + 2], mx[:], -1.0,
                                             ms[:, :, STK:STK + 1].bitcast(F32), ALU.mult, ALU.subtract)\
                        .then_inc(mrow_in, 1)

                def invert(i):
                    dve.wait_ge(turned, i + 1)
                    dve.reciprocal(rden[:], o4[:, :, HD:HD + 1]).then_inc(rden_done, 1)

                def dest(i):
                    return out[:, bass.ds(i // NH * QT, QT), bass.ds(i % NH * HD, HD)]

                def normalise(i):
                    dve.wait_ge(rden_done, i + 1)
                    dve.tensor_tensor(on[:] if add else dest(i), o4[:, :, 0:HD], rden[:].to_broadcast([P, QT, HD]),
                                      ALU.mult).then_inc(o_read, 1)

                def add_out(i):
                    if add:
                        dve.wait_ge(o_read, i + 2)
                        dve.tensor_tensor(dest(i), dest(i), on[:], ALU.add).then_inc(on_done, 1)

                def take_lo(i, s, half):
                    tiles = slice(2, 3) if half else slice(0, 2)
                    dve.wait_ge(pT_hi_done, 2 * i + half + 1)
                    dve.tensor_tensor(pT_lo[s % 2][:, tiles, :], pT[s % 2][:, tiles, :],
                                      pT_hi[s % 2][:, tiles, :].bitcast(F32), ALU.subtract).then_inc(pT_lo_done, 1)

                def step(i, s):
                    first, final = isinstance(i, int) and i == 0, isinstance(i, int) and i == N - 1
                    earlier = not (isinstance(i, int) and i < 2)
                    if not final:
                        reduce(i + 1, 0)
                    if earlier:
                        invert(i - 2)
                        normalise(i - 2)
                    if not first:
                        take_lo(i - 1, s - 1, 1)
                    if earlier:
                        add_out(i - 2)
                    if not final:
                        reduce(i + 1, 1)
                        split_max(i + 1)
                    take_lo(i, s, 0)

                dve.sem_inc(pT_lo_done, 4)
                dve.sem_inc(max_read, 1)
                dve.sem_inc(o_read, 1)
                dve.memset(ms[:].bitcast(F32), 0.0)
                dve.memset(fold[:], 0.0).then_inc(cleared, 1)
                dve.wait_ge(cleared, 1)
                dve.tensor_copy(fold[0:HD, 0:HD], st.ident[0:HD, 0:HD])
                dve.tensor_copy(fold[HD:2 * HD, 0:HD], st.ident[HD:2 * HD, HD:2 * HD])
                dve.tensor_copy(fold[2 * HD:OUTS, HD:HD + 1], st.ident[2 * HD:OUTS, 2 * HD:OUTS]).then_inc(made, 1)
                reduce(0, 0)
                reduce(0, 1)
                split_max(0)
                rounds(dve, step)
                for i in (N - 2, N - 1):
                    invert(i)
                    normalise(i)
                    add_out(i)
                    if i == N - 2:
                        take_lo(N - 1, 1, 1)


def persistent(st):
    sb, _ = tensors(st.nc, st.ctx)
    st.x = sb("x_res", [P, T, D], F32)
    st.ident = sb("ident", [P, P], F32)
    st.ident_r = sb("ident_r", [P, P], F32R)
    st.xT_hi = sb("xT_hi", [P, KC, TOK], F32R)
    st.xT_lo = sb("xT_lo", [P, KC, TOK], F32R)


def column(v):
    return v.rearrange("(p a) -> p a", a=1)


def layer0_attention(st, Wq_w, Wq_b, Wk_w, Wk_b, Wv_w, Wv_b):
    nc = st.nc
    kinds = ["q"] * KC + ["k", "v"]
    q_dram = nc.dram_tensor("l0_q", (2, D, TOK), F32).ap()
    k_dram = nc.dram_tensor("l0_k", (2, HD, TOK), F32).ap()
    with ExitStack() as outer:
        sb, _ = tensors(nc, outer)
        v = sb("l0_v", [P, T, 1, HD], F32)
        with ExitStack() as stack:
            sb, _ = tensors(nc, stack)
            wT_hi = sb("l0_wT_hi", [P, KC, len(kinds) * P], F32R)
            wT_lo = sb("l0_wT_lo", [P, KC, len(kinds) * P], F32R)
            bias = sb("l0_bias", [P, len(kinds)], F32)
            with ExitStack() as loading:
                sb, _ = tensors(nc, loading)
                wq = sb("l0_wq", [P, KC, D], F32)
                wkv = sb("l0_wkv", [HD, 2, D], F32)
                loads = [(wq[:], Wq_w.rearrange("(f p) d -> p f d", p=P)),
                         (wkv[:, 0, :], Wk_w), (wkv[:, 1, :], Wv_w),
                         (bias[:, 0:KC], Wq_b.rearrange("(f p) -> p f", p=P)),
                         (bias[0:HD, KC:KC + 1], column(Wk_b)), (bias[0:HD, KC + 1:KC + 2], column(Wv_b))]
                jobs = [([wq[:, f, c * P:(c + 1) * P] for f in range(KC)],
                         wT_hi[:, c, 0:D], wT_lo[:, c, 0:D]) for c in range(KC)]
                jobs += [([wkv[:, n, c * P:(c + 1) * P]], wT_hi[:, c, D + n * P:D + n * P + HD],
                          wT_lo[:, c, D + n * P:D + n * P + HD]) for c in range(KC) for n in range(2)]
                fills = [w[:, :, D:].bitcast(F32) for w in (wT_hi, wT_lo)] + [bias[:, KC:]]
                norm_to_features(st, "l0a", loads, jobs, fills)
            project(st, "l0p", wT_hi, wT_lo, bias, kinds, q_dram, k_dram, v, 1)
        attend(st, "l0s", q_dram, k_dram, v, False, st.x)


def load_context(st, ctx_in, ctxT_hi, ctxT_lo, more_loads, more_jobs, name):
    with ExitStack() as stack:
        sb, _ = tensors(st.nc, stack)
        raw = sb(f"{name}_ctx", [P, T, C], F32)
        loads = [(raw[:], ctx_in.rearrange("b (q p) c -> p (b q) c", p=P))] + more_loads
        jobs = [([raw[:, b * QT + q, c * P:(c + 1) * P] for q in range(QT)],
                 ctxT_hi[:, c, b * S:(b + 1) * S], ctxT_lo[:, c, b * S:(b + 1) * S])
                for b in range(B) for c in range(CC)]
        norm_to_features(st, name, loads, jobs + more_jobs)


def feature_attention(st, ctx_in, Wq, bq, Wk, bk):
    nc = st.nc
    assert S == D
    with ExitStack() as stack:
        sb, ps = tensors(nc, stack)
        ctxT_hi = sb("fa_ctxT_hi", [P, CC, TOK], F32R)
        ctxT_lo = sb("fa_ctxT_lo", [P, CC, TOK], F32R)
        wT_hi = sb("fa_wT_hi", [P, CC, 2 * P], F32R)
        wT_lo = sb("fa_wT_lo", [P, CC, 2 * P], F32R)
        bias = sb("fa_bias", [P, 2], F32)
        with ExitStack() as loading:
            sb2, _ = tensors(nc, loading)
            raw = sb2("fa_w", [P, 2, C], F32)
            loads = [(raw[:, 0, :], Wq), (raw[:, 1, :], Wk), (bias[:, 0:1], column(bq)), (bias[:, 1:2], column(bk))]
            jobs = [([raw[:, n, c * P:(c + 1) * P] for n in range(2)], wT_hi[:, c, :], wT_lo[:, c, :])
                    for c in range(CC)]
            load_context(st, ctx_in, ctxT_hi, ctxT_lo, loads, jobs, "fa_prep")

        hi = [sb(f"fa_hi{n}", [P, S], F32R) for n in range(2)]
        lo = [sb(f"fa_lo{n}", [P, S], F32R) for n in range(2)]
        prob = sb("fa_prob", [P, QT, S], F32)
        nmax = sb("fa_nmax", [P, QT], F32)
        den = sb("fa_den", [P, QT], F32)
        rden = sb("fa_rden", [P, QT], F32)
        attT_hi = sb("fa_attT_hi", [P, QT, S], F32R)
        attT_lo = sb("fa_attT_lo", [P, QT, S], F32R)
        work = [ps(f"fa_work{n}", [P, 512]) for n in range(2)]
        energy = ps("fa_energy", [P, QT, S])
        turn = [ps(f"fa_turn{n}", [P, 512]) for n in range(2)]
        worked, work_read, hi_done, scored, nmax_ready, exp_done, rden_done, prob_ready, turned, att_hi, turn_read = \
            st.sems("worked", "work_read", "hi_done", "scored", "nmax_ready", "exp_done", "rden_done", "prob_ready",
                    "turned", "att_hi", "turn_read")

        def qk_use(b, n):
            return n if b == 0 else (2 + QT) * (b - 1) + 2 + n

        def out_use(b, t):
            return (2 + QT) * b + (4 if b < B - 1 else 2) + t

        with nc.Block() as block:

            @block.tensor
            def _(pe):
                def project_qk(b):
                    for n in range(2):
                        if b:
                            pe.wait_ge(work_read, qk_use(b, n) - 1)
                        m = 0
                        for c in range(CC):
                            for w, x in ((wT_hi, ctxT_hi), (wT_hi, ctxT_lo), (wT_lo, ctxT_hi)):
                                last = pe.matmul(work[n][:], w[:, c, n * P:(n + 1) * P], x[:, c, b * S:(b + 1) * S],
                                                 start=(m == 0), stop=(m == 3 * CC - 1))
                                m += 1
                        last.then_inc(worked, 1)

                def energies(b):
                    pe.wait_ge(work_read, qk_use(b, 1) + 1)
                    for q in range(QT):
                        for m, (qq, kk) in enumerate(((hi[0], hi[1]), (hi[0], lo[1]), (lo[0], hi[1]))):
                            last = pe.matmul(energy[:, q, :], qq[:, q * P:(q + 1) * P], kk[:], start=(m == 0),
                                             stop=(m == 2))
                        last.then_inc(scored, 1)

                def turn_attention(b):
                    pe.wait_ge(prob_ready, b + 1)
                    for k in range(QT):
                        if QT * b + k >= 2:
                            pe.wait_ge(turn_read, QT * b + k - 1)
                        for q in range(QT):
                            last = pe.transpose(turn[k % 2][:, q * P:(q + 1) * P], prob[:, q, k * P:(k + 1) * P],
                                                st.ident[:])
                        last.then_inc(turned, 1)

                def mix(b, t):
                    pe.wait_ge(turn_read, QT * b + QT)
                    pe.wait_ge(work_read, out_use(b, t) - 1)
                    tile = slice(b * S + t * P, b * S + (t + 1) * P)
                    m = 0
                    for k in range(QT):
                        for x, a in ((st.xT_hi, attT_hi), (st.xT_hi, attT_lo), (st.xT_lo, attT_hi)):
                            last = pe.matmul(work[t % 2][:], x[:, k, tile], a[:, k, :], start=(m == 0),
                                             stop=(m == 3 * QT - 1))
                            m += 1
                    last.then_inc(worked, 1)

                project_qk(0)
                energies(0)
                for b in range(B):
                    turn_attention(b)
                    if b < B - 1:
                        project_qk(b + 1)
                        energies(b + 1)
                    for t in range(QT):
                        mix(b, t)

            @block.scalar
            def _(act):
                def take_qk(b):
                    for n in range(2):
                        act.wait_ge(worked, qk_use(b, n) + 1)
                        act.activation(hi[n][:], work[n][:], ACT.Identity, bias=bias[:, n:n + 1]).then_inc(hi_done, 1)

                def exponentials(b):
                    for q in range(QT):
                        act.wait_ge(nmax_ready, QT * b + q + 1)
                        act.activation(prob[:, q, :], energy[:, q, :], ACT.Exp, bias=nmax[:, q:q + 1],
                                       accum_out=den[:, q:q + 1]).then_inc(exp_done, 1)

                take_qk(0)
                exponentials(0)
                for b in range(B):
                    for k in range(QT):
                        act.wait_ge(turned, QT * b + k + 1)
                        act.activation(attT_hi[:, k, :], turn[k % 2][:], ACT.Copy).then_inc(att_hi, 1)
                    if b < B - 1:
                        take_qk(b + 1)
                        exponentials(b + 1)

            @block.vector
            def _(dve):
                def take_qk(b):
                    for n in range(2):
                        dve.wait_ge(hi_done, 2 * b + n + 1)
                        dve.scalar_tensor_tensor(lo[n][:], work[n][:], bias[:, n:n + 1], hi[n][:].bitcast(F32),
                                                 ALU.add, ALU.subtract).then_inc(work_read, 1)

                def maxima(b):
                    if b:
                        dve.wait_ge(exp_done, QT * b)
                    for q in range(QT):
                        dve.wait_ge(scored, QT * b + q + 1)
                        dve.tensor_reduce(nmax[:, q:q + 1], energy[:, q, :], AX.X, ALU.max, negate=True)\
                            .then_inc(nmax_ready, 1)

                def normalise(b):
                    dve.wait_ge(exp_done, QT * b + QT)
                    if b:
                        dve.wait_ge(prob_ready, b)
                    dve.reciprocal(rden[:], den[:]).then_inc(rden_done, 1)
                    dve.wait_ge(rden_done, b + 1)
                    for q in range(QT):
                        last = dve.tensor_scalar(prob[:, q, :], prob[:, q, :], rden[:, q:q + 1], None, ALU.mult)
                    last.then_inc(prob_ready, 1)

                def add(b, t):
                    dve.wait_ge(worked, out_use(b, t) + 1)
                    xt = st.x[:, b * QT + t, :]
                    dve.tensor_tensor(xt, work[t % 2][:], xt, ALU.add).then_inc(work_read, 1)

                take_qk(0)
                maxima(0)
                normalise(0)
                for b in range(B):
                    for k in range(QT):
                        dve.wait_ge(att_hi, QT * b + k + 1)
                        dve.tensor_tensor(attT_lo[:, k, :], turn[k % 2][:], attT_hi[:, k, :].bitcast(F32),
                                          ALU.subtract).then_inc(turn_read, 1)
                    if b < B - 1:
                        take_qk(b + 1)
                        maxima(b + 1)
                    add(b, 0)
                    if b < B - 1:
                        normalise(b + 1)
                    for t in range(1, QT):
                        add(b, t)


def turn_scales(nc, st, scale, gate_up_scales, down_scales, weights):
    NC = scale.shape[2]
    with ExitStack() as stack:
        sb, ps = tensors(nc, stack)
        s16 = sb("ffn_s16", [KC, 2 * NC * P], F16)
        d16 = sb("ffn_d16", [NC, D], F16)
        s32 = sb("ffn_s32", [KC, 2 * NC * P], F32)
        d32 = sb("ffn_d32", [NC, D], F32)
        norm_to_features(st, "ffn", [(s16[:], gate_up_scales), (d16[:], down_scales)] + weights)
        gu_bank, dn_bank = ps("ffn_gu_scales", [P, 512]), ps("ffn_dn_scales", [P, 512])
        s32_ready, s_turned = st.sems("s32_ready", "s_turned")
        with nc.Block() as block:

            @block.tensor
            def _(pe):
                pe.wait_ge(s32_ready, 2)
                for f in range(2 * NC):
                    pe.matmul(gu_bank[:, f * KC:(f + 1) * KC], s32[:, f * P:(f + 1) * P], st.ident[0:KC, 0:KC],
                              start=True, stop=True)
                for o in range(KC):
                    last = pe.matmul(dn_bank[:, o * NC:(o + 1) * NC], d32[:, o * P:(o + 1) * P], st.ident[0:NC, 0:NC],
                                     start=True, stop=True)
                last.then_inc(s_turned, 1)

            @block.vector
            def _(dve):
                dve.tensor_copy(s32[:], s16[:]).then_inc(s32_ready, 1)
                dve.tensor_copy(d32[:], d16[:]).then_inc(s32_ready, 1)
                dve.wait_ge(s_turned, 1)
                gu = gu_bank[:, 0:2 * NC * KC].rearrange("p (n c k) -> p c n k", n=2, k=KC)
                dn = dn_bank[:, 0:KC * NC].rearrange("p (o c) -> p c o", o=KC)
                for row, by in enumerate((4.0, -1.0)):
                    dve.tensor_scalar(scale[:, row, :, 0:2, :], gu, by, None, ALU.mult)
                    dve.tensor_scalar(scale[:, row, :, 2, :], dn, by, None, ALU.mult)


def packed_ffn(st, gate_up_packed, gate_up_scales, down_packed, down_scales):
    nc = st.nc
    I = gate_up_packed.shape[0] // 2
    NC = I // P
    WORDS = D // 8
    MAG, SIGN, BASE = 7 << 22, 1 << 31, 124 << 23
    with ExitStack() as stack:
        sb, ps = tensors(nc, stack)
        packed = sb("ffn_packed", [P, 2 * NC, WORDS], I32)
        dpacked = sb("ffn_dpacked", [P, KC, I // 8], I32)
        scale = sb("ffn_scale", [P, 2, NC, 3, KC], F32)
        csc = sb("ffn_csc", [P, 2, 3 * KC], F32)
        turn_scales(nc, st, scale, gate_up_scales, down_scales,
                    [(packed[:], gate_up_packed.rearrange("(f p) w -> p f w", p=P)),
                     (dpacked[:], down_packed.rearrange("(o p) w -> p o w", p=P))])
        mag = sb("ffn_mag", [P, 3, D], I32)
        sgn = sb("ffn_sgn", [P, 3, D], I32)
        w32 = sb("ffn_w32", [P, 3, D], F32)
        gu_hi = [sb(f"ffn_gu_hi{s}", [P, 2, KC, P], F32R) for s in range(2)]
        gu_lo = [sb(f"ffn_gu_lo{s}", [P, 2, KC, P], F32R) for s in range(2)]
        dn_hi = [sb(f"ffn_dn_hi{s}", [P, D], F32R) for s in range(2)]
        dn_lo = [sb(f"ffn_dn_lo{s}", [P, D], F32R) for s in range(2)]
        sl = [sb(f"ffn_sl{s}", [P, S], F32) for s in range(2)]
        h32 = [sb(f"ffn_h32{s}", [P, S], F32) for s in range(2)]
        h_hi = [sb(f"ffn_h_hi{s}", [P, S], F32R) for s in range(2)]
        h_lo = [sb(f"ffn_h_lo{s}", [P, S], F32R) for s in range(2)]
        y = sb("ffn_y", [P, T, D], F32)
        ss = sb("ffn_ss", [P, 4, T], F32)
        turn = [ps(f"ffn_turn{s}", [P, 512]) for s in range(2)]
        g_bank = [ps(f"ffn_g{s}", [P, S]) for s in range(2)]
        u_bank = [ps(f"ffn_u{s}", [P, S]) for s in range(2)]
        y_bank = [ps(f"ffn_y{s}", [P, D]) for s in range(2)]
        mag_in, mag_ready, sgn_ready, csc_ready, f_ready, scaled, w_ready, turned, w_hi, turn_read = st.sems(
            "mag_in", "mag_ready", "sgn_ready", "csc_ready", "f_ready", "scaled", "w_ready", "turned",
            "w_hi", "turn_read")
        gu_done, silu_done, h_ready, h_hi_done, h_lo_done, y_done, y_read, y_zero, sq_done, ms_ready, rms_ready = \
            st.sems("gu_done", "silu_done", "h_ready", "h_hi_done", "h_lo_done", "y_done", "y_read", "y_zero",
                    "sq_done", "ms_ready", "rms_ready")

        def chunks(eng, body):
            with eng.Fori(0, NC // 2) as j:
                for s in range(2):
                    body(2 * j + s, s)
            for c in range(NC // 2 * 2, NC):
                body(c, c % 2)

        with nc.Block() as block:

            @block.gpsimd
            def _(pool):
                pool.memset(y[:], 0.0).then_inc(y_zero, 1)

            @block.tensor
            def _(pe):
                def turn_weights(c, n):
                    pe.wait_ge(w_ready, c + 1)
                    pe.wait_ge(turn_read, 3 * c + n + (1 if n else 2))
                    for k in range(KC):
                        last = pe.transpose(turn_of(c, n)[:, k * P:(k + 1) * P], w32[:, n, k * P:(k + 1) * P],
                                            st.ident[:])
                    last.then_inc(turned, 1)

                def gate_up(c, s, b, n, m0, m1):
                    bank = (g_bank, u_bank)[n][b % 2]
                    if m0 == 0:
                        pe.wait_ge(h_ready if n else silu_done, B * c + b + 1)
                    passes = [(w[s][:, n, k, :], x[:, k, b * S:(b + 1) * S]) for k in range(KC)
                              for w, x in ((gu_hi, st.xT_hi), (gu_hi, st.xT_lo), (gu_lo, st.xT_hi))]
                    for m in range(m0, m1):
                        last = pe.matmul(bank[:], *passes[m], start=(m == 0), stop=(m == 3 * KC - 1))
                    if m1 == 3 * KC:
                        last.then_inc(gu_done, 1)

                def down(c, s, b, t):
                    u = B * c + b
                    if t == 0:
                        pe.wait_ge(h_lo_done, u + 1)
                        pe.wait_ge(turn_read, 3 * c + 5)
                    pe.wait_ge(y_read, QT * u + t + 1)
                    for m, (h, w) in enumerate(((h_hi, dn_hi), (h_hi, dn_lo), (h_lo, dn_hi))):
                        last = pe.matmul(y_bank[t % 2][:], h[b % 2][:, t * P:(t + 1) * P], w[s][:],
                                         start=(m == 0), stop=(m == 2))
                    last.then_inc(y_done, 1)

                def turn_of(c, n):
                    return turn[n % 2]

                def chunk(c, s):
                    known = isinstance(c, int)
                    more = not (known and c == NC - 1)
                    pe.wait_ge(turn_read, 3 * c + 4)
                    for b in range(B):
                        def down_before(t):
                            if b:
                                down(c, s, b - 1, t)
                            elif not (known and c == 0):
                                down(c - 1, 1 - s, B - 1, t)

                        gate_up(c, s, b, 0, 0, 8)
                        down_before(0)
                        gate_up(c, s, b, 0, 8, 12)
                        down_before(1)
                        if b == 3 and more:
                            turn_weights(c + 1, 1)
                        gate_up(c, s, b, 1, 0, 6)
                        down_before(2)
                        gate_up(c, s, b, 1, 6, 12)
                        down_before(3)
                        if b >= 2 and more:
                            turn_weights(c + 1, (b - 2) * 2)

                for n in range(3):
                    turn_weights(0, n)
                chunk(0, 0)
                with pe.Fori(0, (NC - 2) // 2) as j:
                    chunk(2 * j + 1, 1)
                    chunk(2 * j + 2, 0)
                for c in range((NC - 2) // 2 * 2 + 1, NC):
                    chunk(c, c % 2)
                for t in range(QT):
                    down(NC - 1, (NC - 1) % 2, B - 1, t)

            @block.scalar
            def _(act):
                act.sem_inc(silu_done, 2)

                def scale_weights(c):
                    act.wait_ge(csc_ready, c + 1)
                    act.wait_ge(f_ready, c + 1)
                    for n in range(3):
                        for k in range(KC):
                            col = n * KC + k
                            last = act.activation(w32[:, n, k * P:(k + 1) * P], w32[:, n, k * P:(k + 1) * P],
                                                  ACT.Identity, bias=csc[:, 1, col:col + 1],
                                                  scale=csc[:, 0, col:col + 1])
                    last.then_inc(scaled, 1)

                def take_hi(c, s, n):
                    act.wait_ge(turned, 3 * c + n + 1)
                    dst = dn_hi[s][:] if n == 2 else gu_hi[s][:, n, :, :].rearrange("p k f -> p (k f)")
                    act.activation(dst, turn[n % 2][:], ACT.Copy).then_inc(w_hi, 1)

                def silu(c, b):
                    u = B * c + b
                    act.wait_ge(gu_done, 2 * u + 1)
                    act.wait_ge(h_ready, u + 1)
                    act.activation(sl[b % 2][:], g_bank[b % 2][:], ACT.Silu).then_inc(silu_done, 1)

                def take_h(c, b):
                    u = B * c + b
                    act.wait_ge(h_ready, u + 3)
                    act.activation(h_hi[b % 2][:], h32[b % 2][:], ACT.Copy).then_inc(h_hi_done, 1)

                def chunk(c, s):
                    more = not (isinstance(c, int) and c == NC - 1)
                    for b in range(B):
                        silu(c, b)
                        if b == 3 and more:
                            take_hi(c + 1, 1 - s, 1)
                        take_h(c, b)
                        if b == 0 and more:
                            scale_weights(c + 1)
                        if b >= 2 and more:
                            take_hi(c + 1, 1 - s, (b - 2) * 2)
                        elif b >= 2:
                            squares(b - 2)

                def squares(b):
                    act.wait_ge(y_read, QT * (B * (NC - 1) + b + 1) + 2)
                    for t in range(b * QT, (b + 1) * QT):
                        if t >= 2:
                            act.wait_ge(sq_done, t - 1)
                        act.activation(w32[:, t % 2, :], y[:, t, :], ACT.Square, accum_out=ss[:, 0, t:t + 1])\
                            .then_inc(sq_done, 1)

                scale_weights(0)
                for n in range(3):
                    take_hi(0, 0, n)
                chunks(act, chunk)
                squares(B - 2)
                squares(B - 1)
                act.wait_ge(ms_ready, 1)
                act.activation(ss[:, 2, :], ss[:, 1, :], ACT.Sqrt).then_inc(rms_ready, 1)

            @block.vector
            def _(dve):
                dve.sem_inc(turn_read, 2)
                dve.sem_inc(h_ready, 2)
                dve.sem_inc(y_read, 2)

                def unpack(c, part):
                    dst, keep, at = ((mag, MAG, 22), (sgn, SIGN - (1 << 32), 28))[part]
                    for j in range(8):
                        shift = at - 4 * j
                        op = ALU.logical_shift_left if shift >= 0 else ALU.logical_shift_right
                        gu_words = packed[:].rearrange("p (n c) w -> p c n w", n=2)[:, bass.ds(c, 1), :, :]\
                            .rearrange("p a n w -> p (a n) w")
                        dn_words = dpacked[:, :, bass.ds(c * (P // 8), P // 8)]
                        dve.tensor_scalar(dst[:, 0:2, :].rearrange("p n (w e) -> p n w e", e=8)[:, :, :, j],
                                          gu_words, abs(shift), keep, op, ALU.bitwise_and)
                        last = dve.tensor_scalar(
                            dst[:, 2, :].rearrange("p (o w e) -> p o w e", o=KC, e=8)[:, :, :, j],
                            dn_words, abs(shift), keep, op, ALU.bitwise_and)
                    return last

                def magnitudes(c):
                    reached(dve, f_ready, c)
                    unpack(c, 0).then_inc(mag_in, 1)

                def exponents(c):
                    dve.wait_ge(mag_in, c + 1)
                    dve.tensor_scalar(mag[:], mag[:], BASE, None, ALU.bitwise_or).then_inc(mag_ready, 1)

                def values(c):
                    reached(dve, scaled, c)
                    dve.tensor_copy(csc[:].rearrange("p r (n k) -> p r n k", n=3),
                                    scale[:, :, bass.ds(c, 1), :, :].rearrange("p r a n k -> p r (a n) k"))\
                        .then_inc(csc_ready, 1)
                    g = mag[:].bitcast(F32)
                    dve.wait_ge(mag_ready, c + 1)
                    reached(dve, turned, 3 * c)
                    dve.scalar_tensor_tensor(w32[:], g, 0.25, g, ALU.min, ALU.add).then_inc(f_ready, 1)

                def signs(c):
                    reached(dve, w_ready, c)
                    unpack(c, 1).then_inc(sgn_ready, 1)

                def put_signs(c):
                    dve.wait_ge(scaled, c + 1)
                    dve.wait_ge(sgn_ready, c + 1)
                    wi = w32[:].bitcast(I32)
                    dve.tensor_tensor(wi, wi, sgn[:], ALU.bitwise_xor).then_inc(w_ready, 1)

                def take_lo(c, s, n):
                    dve.wait_ge(w_hi, 3 * c + n + 1)
                    hi, lo = (dn_hi[s][:], dn_lo[s][:]) if n == 2 else \
                        (x[s][:, n, :, :].rearrange("p k f -> p (k f)") for x in (gu_hi, gu_lo))
                    dve.tensor_tensor(lo, turn[n % 2][:], hi.bitcast(F32), ALU.subtract).then_inc(turn_read, 1)

                def hidden(c, b, part):
                    u = B * c + b
                    if part == 0:
                        dve.wait_ge(silu_done, u + 3)
                        dve.wait_ge(gu_done, 2 * u + 2)
                        dve.tensor_tensor(h32[b % 2][:], u_bank[b % 2][:], sl[b % 2][:], ALU.mult).then_inc(h_ready, 1)
                    else:
                        dve.wait_ge(h_hi_done, u + 1)
                        dve.tensor_tensor(h_lo[b % 2][:], h32[b % 2][:], h_hi[b % 2][:].bitcast(F32), ALU.subtract)\
                            .then_inc(h_lo_done, 1)

                def add_y(c, b, t):
                    v = QT * (B * c + b) + t
                    dve.wait_ge(y_done, v + 1)
                    yt = y[:, b * QT + t, :]
                    dve.tensor_tensor(yt, y_bank[t % 2][:], yt, ALU.add).then_inc(y_read, 1)

                def chunk(c, s):
                    known = isinstance(c, int)
                    more = not (known and c == NC - 1)
                    for b in range(B):
                        def add_before(t):
                            if b:
                                add_y(c, b - 1, t)
                            elif not (known and c == 0):
                                add_y(c - 1, B - 1, t)

                        if b == 0:
                            take_lo(c, s, 2)
                        if b == 3 and more:
                            take_lo(c + 1, 1 - s, 0)
                        add_before(0)
                        add_before(1)
                        if b == 3 and more:
                            take_lo(c + 1, 1 - s, 1)
                        add_before(2)
                        hidden(c, b, 0)
                        add_before(3)
                        hidden(c, b, 1)
                        if b == 0 and more:
                            values(c + 1)
                            signs(c + 1)
                        if b == 1 and more:
                            put_signs(c + 1)
                        if b >= 2 and not (known and c >= NC - 2):
                            (magnitudes, exponents)[b - 2](c + 2)

                magnitudes(0)
                exponents(0)
                values(0)
                signs(0)
                put_signs(0)
                for n in range(2):
                    take_lo(0, 0, n)
                magnitudes(1)
                exponents(1)
                dve.wait_ge(y_zero, 1)
                chunk(0, 0)
                with dve.Fori(0, (NC - 2) // 2) as j:
                    chunk(2 * j + 1, 1)
                    chunk(2 * j + 2, 0)
                for c in range((NC - 2) // 2 * 2 + 1, NC):
                    chunk(c, c % 2)
                for t in range(QT):
                    add_y(NC - 1, B - 1, t)
                dve.wait_ge(sq_done, T)
                dve.tensor_scalar(ss[:, 1, :], ss[:, 0, :], 1.0 / D, 1e-6, ALU.mult, ALU.add).then_inc(ms_ready, 1)
                dve.wait_ge(rms_ready, 1)
                dve.reciprocal(ss[:, 3, :], ss[:, 2, :]).then_inc(ms_ready, 1)
                dve.wait_ge(ms_ready, 2)
                for t in range(T):
                    dve.scalar_tensor_tensor(st.x[:, t, :], y[:, t, :], ss[:, 3, t:t + 1], st.x[:, t, :], ALU.mult,
                                             ALU.add)


def turn_tile(eng_pe, bank, source, ident):
    for c in range(KC):
        last = eng_pe.transpose(bank[:, c * P:(c + 1) * P], source[:, c * P:(c + 1) * P], ident)
    return last


def layer1_attention(st, Wqkv_w, Wqkv_b, out_w, out_b):
    nc = st.nc
    kinds = ["q"] * KC + ["k"] * KC + ["v"] * KC
    q_dram = nc.dram_tensor("l1_q", (2, D, TOK), F32).ap()
    k_dram = nc.dram_tensor("l1_k", (2, D, TOK), F32).ap()
    with ExitStack() as outer:
        sb, _ = tensors(nc, outer)
        v = sb("l1_v", [P, T, NH, HD], F32)
        ow_hi = sb("l1_ow_hi", [P, KC, D], F32R)
        ow_lo = sb("l1_ow_lo", [P, KC, D], F32R)
        out_bias = sb("l1_out_bias", [P, D], F32)
        with ExitStack() as stack:
            sb, _ = tensors(nc, stack)
            wT_hi = sb("l1_wT_hi", [P, KC, 3 * D], F32R)
            wT_lo = sb("l1_wT_lo", [P, KC, 3 * D], F32R)
            bias = sb("l1_bias", [P, 3 * KC], F32)
            raw = v[:].rearrange("p t h d -> p (t h d)").rearrange("p (f d) -> p f d", d=D)
            sources = [Wqkv_w[n * D:(n + 1) * D, :] for n in range(3)] + [out_w]
            loads = [(raw[:, n * KC:(n + 1) * KC, :], w.rearrange("(f p) d -> p f d", p=P))
                     for n, w in enumerate(sources)]
            loads.append((bias[:], Wqkv_b.rearrange("(f p) -> p f", p=P)))
            loads.append((out_bias[:], out_b.rearrange("(a d) -> a d", a=1).to_broadcast([P, D])))
            parts = [[w[:, :, n * D:(n + 1) * D] for w in (wT_hi, wT_lo)] for n in range(3)] + [(ow_hi, ow_lo)]
            jobs = [([raw[:, n * KC + f, c * P:(c + 1) * P] for f in range(KC)], hi[:, c, :], lo[:, c, :])
                    for n, (hi, lo) in enumerate(parts) for c in range(KC)]
            norm_to_features(st, "l1a", loads, jobs)
            project(st, "l1p", wT_hi, wT_lo, bias, kinds, q_dram, k_dram, v, P // HD)
        ao = sb_tensor(nc, outer, "l1_ao", [P, T, D])
        attend(st, "l1s", q_dram, k_dram, v, True, ao)
        output_projection(st, ao, ow_hi, ow_lo, out_bias)


def sb_tensor(nc, stack, name, shape, dt=F32):
    return stack.enter_context(nc.sbuf_tensor(name, shape, dt))


def output_projection(st, ao, w_hi, w_lo, bias):
    nc = st.nc
    with ExitStack() as stack:
        sb, ps = tensors(nc, stack)
        a32 = [sb(f"op_a32{s}", [P, D], F32) for s in range(2)]
        a_hi = [sb(f"op_a_hi{s}", [P, D], F32R) for s in range(2)]
        a_lo = [sb(f"op_a_lo{s}", [P, D], F32R) for s in range(2)]
        turn = [ps(f"op_turn{s}", [P, D]) for s in range(2)]
        bank = [ps(f"op_bank{s}", [P, D]) for s in range(2)]
        copied, turned, hi_done, lo_done, done, read, biased = st.sems(
            "op_copied", "op_turned", "op_hi", "op_lo", "op_done", "op_read", "op_biased")
        with nc.Block() as block:

            @block.gpsimd
            def _(pool):
                with pool.Fori(0, T) as t:
                    xt = st.x[:, bass.ds(t, 1), :].rearrange("p a d -> p (a d)")
                    pool.tensor_tensor(xt, xt, bias[:], ALU.add).then_inc(biased, 1)

            @block.tensor
            def _(pe):
                def turn_a(t, s):
                    pe.wait_ge(copied, t + 1)
                    pe.wait_ge(lo_done, t + 1)
                    turn_tile(pe, turn[s], a32[s], st.ident[:]).then_inc(turned, 1)

                def product(t, s):
                    pe.wait_ge(lo_done, t + 3)
                    pe.wait_ge(read, t + 1)
                    m = 0
                    for c in range(KC):
                        for a, w in ((a_hi, w_hi), (a_hi, w_lo), (a_lo, w_hi)):
                            last = pe.matmul(bank[s][:], a[s][:, c * P:(c + 1) * P], w[:, c, :], start=(m == 0),
                                             stop=(m == 3 * KC - 1))
                            m += 1
                    last.then_inc(done, 1)

                turn_a(0, 0)
                with pe.Fori(0, T // 2 - 1) as j:
                    for s in range(2):
                        turn_a(2 * j + s + 1, 1 - s)
                        product(2 * j + s, s)
                turn_a(T - 1, 1)
                product(T - 2, 0)
                product(T - 1, 1)

            @block.scalar
            def _(act):
                act.sem_inc(done, 2)
                with act.Fori(0, T // 2) as j:
                    for s in range(2):
                        t = 2 * j + s
                        act.wait_ge(turned, t + 1)
                        act.wait_ge(done, t + 1)
                        act.activation(a_hi[s][:], turn[s][:], ACT.Copy).then_inc(hi_done, 1)

            @block.vector
            def _(dve):
                dve.sem_inc(lo_done, 2)
                dve.sem_inc(read, 2)

                def copy(t, s):
                    dve.wait_ge(lo_done, t + 1)
                    dve.tensor_copy(a32[s][:], ao[:, bass.ds(t, 1), :].rearrange("p a d -> p (a d)"))\
                        .then_inc(copied, 1)

                def take_lo(t, s):
                    dve.wait_ge(hi_done, t + 1)
                    dve.tensor_tensor(a_lo[s][:], turn[s][:], a_hi[s][:].bitcast(F32), ALU.subtract)\
                        .then_inc(lo_done, 1)

                def add(t, s):
                    dve.wait_ge(biased, t + 1)
                    dve.wait_ge(done, t + 3)
                    xt = st.x[:, bass.ds(t, 1), :].rearrange("p a d -> p (a d)")
                    dve.tensor_tensor(xt, bank[s][:], xt, ALU.add).then_inc(read, 1)

                copy(0, 0)
                copy(1, 1)
                take_lo(0, 0)
                with dve.Fori(0, T // 2 - 1) as j:
                    for s in range(2):
                        t = 2 * j + s
                        copy(t + 2, s)
                        take_lo(t + 1, 1 - s)
                        add(t, s)
                take_lo(T - 1, 1)
                add(T - 2, 0)
                add(T - 1, 1)


def routed_mixture(st, Wr, U, V, attr, Wa, out):
    nc = st.nc
    NS, R = Wr.shape[0], U.shape[2]
    F = NS * R
    FC = F // P
    AD = attr.shape[1]
    with ExitStack() as stack:
        sb, ps = tensors(nc, stack)
        wr_hi = sb("mix_wr_hi", [P, KC, P], F32R)
        wr_lo = sb("mix_wr_lo", [P, KC, P], F32R)
        u_hi = sb("mix_u_hi", [P, KC, F], F32R)
        u_lo = sb("mix_u_lo", [P, KC, F], F32R)
        v32 = sb("mix_v32", [P, FC, D], F32)
        v_hi = sb("mix_v_hi", [P, FC, D], F32R)
        v_lo = sb("mix_v_lo", [P, FC, D], F32R)
        attr_b = sb("mix_attr", [P, NS, AD], F32)
        wa_b = sb("mix_wa", [P, 1, AD], F32)
        with ExitStack() as loading:
            sb2, _ = tensors(nc, loading)
            wr = sb2("mix_wr", [NS, D], F32)
            u = sb2("mix_u", [P, P, R], F32)
            loads = [(wr[:], Wr), (u[:], U.rearrange("s (c h) r -> (s c) h r", c=KC)),
                     (attr_b[:].rearrange("p s a -> p (s a)"),
                      attr.rearrange("s a -> (s a)").rearrange("(o a) -> o a", o=1).to_broadcast([P, NS * AD])),
                     (wa_b[:, 0, :], Wa.to_broadcast([P, AD])),
                     (v32[:], V.rearrange("s r d -> (s r) d").rearrange("(c p) d -> p c d", p=P))]
            jobs = [([wr[:, c * P:(c + 1) * P]], wr_hi[:, c, 0:NS], wr_lo[:, c, 0:NS]) for c in range(KC)]
            for r in range(0, R, 4):
                hi, lo = (w[:].rearrange("p c (s r) -> p r s c", r=R)[:, r:r + 4] for w in (u_hi, u_lo))
                jobs.append(([u[:, :, r + k] for k in range(4)], hi, lo))
            norm_to_features(st, "mix_prep", loads, jobs, [w[:].bitcast(F32) for w in (wr_hi, wr_lo)])

        scT = sb("mix_scT", [NS, S], F32)
        sc = sb("mix_sc", [P, T, NS], F32)
        top = sb("mix_top", [P, T, 8], F32)
        idx = sb("mix_idx", [P, T, 8], U32)
        idx_f = sb("mix_idx_f", [P, T, 2], F32)
        number = sb("mix_number", [P, 1, NS], F32)
        first = sc
        g = sb("mix_g", [P, T, NS], F32)
        e = sb("mix_e", [P, T, NS], F32)
        den = sb("mix_den", [P, 4, T], F32)
        aw = sb("mix_aw", [P, 3, NS], F32)
        spread = sb("mix_spread", [P, F], F32)
        spread_r = sb("mix_spread_r", [P, F], F32R)
        gT_hi = sb("mix_gT_hi", [P, TOK], F32R)
        gT_lo = sb("mix_gT_lo", [P, TOK], F32R)
        hu, z = ([v32[:, 2 * m + n, :] for n in range(2)] for m in range(2))
        z_hi = [sb(f"mix_z_hi{n}", [P, FC, S], F32R) for n in range(2)]
        z_lo = [sb(f"mix_z_lo{n}", [P, FC, S], F32R) for n in range(2)]
        hu_bank = [ps(f"mix_hu_bank{n}", [P, S]) for n in range(2)]
        g_bank = [ps(f"mix_g_bank{n}", [P, S]) for n in range(2)]
        out_bank = [ps(f"mix_out_bank{n}", [P, D]) for n in range(2)]
        sc_bank = ps("mix_sc_bank", [P, S])
        turn_bank = ps("mix_turn_bank", [P, S])
        v_hi_done, made, scored, sc_read, sc_turned, sc_taken, chain, e_in, e_out, aw_in, aw_out, g_ready, g_turned, \
            gT_hi_done, gT_done = st.sems(
                "v_hi_done", "made", "scored", "sc_read", "sc_turned", "sc_taken", "mix_chain", "e_in", "e_out",
                "aw_in", "aw_out", "g_ready", "g_turned", "gT_hi_done", "gT_done")
        hu_done, hu_copied, spread_done, z_made, z_hi_done, z_lo_done, out_done, x_ready, stored = st.sems(
            "hu_done", "hu_copied", "spread_done", "z_made", "z_hi_done", "z_lo_done", "out_done", "x_ready",
            "stored")
        with nc.Block() as block:

            @block.gpsimd
            def _(pool):
                pool.iota(number[:, 0, :], pattern=[[1, NS]], base=0, channel_multiplier=0,
                          allow_small_or_imprecise_dtypes=True).then_inc(made, 1)
                pool.memset(spread[:], 1.0).then_inc(made, 1)
                pool.wait_ge(made, 2)
                pool.affine_select(out=spread[:], in_=spread[:], compare_op=ALU.is_ge, fill=0.0, base=0,
                                   pattern=[[1, F]], channel_multiplier=-R).then_inc(made, 1)
                pool.wait_ge(made, 3)
                pool.affine_select(out=spread[:], in_=spread[:], compare_op=ALU.is_ge, fill=0.0, base=R - 1,
                                   pattern=[[-1, F]], channel_multiplier=R).then_inc(made, 1)
                for w in (gT_hi, gT_lo):
                    pool.memset(w[:].bitcast(F32), 0.0).then_inc(made, 1)

            @block.tensor
            def _(pe):
                def turn_scores(b):
                    pe.wait_ge(sc_read, b + 1)
                    if b:
                        pe.wait_ge(sc_taken, b)
                    for q in range(QT):
                        last = pe.matmul(turn_bank[:, q * NS:(q + 1) * NS], scT[:, q * P:(q + 1) * P],
                                         st.ident[0:NS, 0:NS], start=True, stop=True)
                    last.then_inc(sc_turned, 1)

                for b in range(B):
                    if b:
                        pe.wait_ge(sc_read, b)
                    m = 0
                    for c in range(KC):
                        for w, x in ((wr_hi, st.xT_hi), (wr_hi, st.xT_lo), (wr_lo, st.xT_hi)):
                            last = pe.matmul(sc_bank[:], w[:, c, :], x[:, c, b * S:(b + 1) * S], start=(m == 0),
                                             stop=(m == 3 * KC - 1))
                            m += 1
                    last.then_inc(scored, 1)
                    turn_scores(b)

                def hidden(b, c):
                    i = b * FC + c
                    pe.wait_ge(hu_copied, i + 1)
                    m = 0
                    for k in range(KC):
                        for w, x in ((u_hi, st.xT_hi), (u_hi, st.xT_lo), (u_lo, st.xT_hi)):
                            last = pe.matmul(hu_bank[c % 2][:], w[:, k, c * P:(c + 1) * P],
                                             x[:, k, bass.ds(b * S, S)], start=(m == 0), stop=(m == 3 * KC - 1))
                            m += 1
                    last.then_inc(hu_done, 1)

                def spread_weights(b, c):
                    pe.wait_ge(z_made, b * FC + c + 1)
                    for m, part in enumerate((gT_hi, gT_lo)):
                        last = pe.matmul(g_bank[c % 2][:], spread_r[:, c * P:(c + 1) * P],
                                         part[:, bass.ds(b * S, S)], start=(m == 0), stop=(m == 1))
                    last.then_inc(spread_done, 1)

                def mix(b, s, q):
                    pe.wait_ge(z_lo_done, FC * (b + 1))
                    pe.wait_ge(x_ready, b * QT + q + 1)
                    m = 0
                    for c in range(FC):
                        for a, w in ((z_hi, v_hi), (z_hi, v_lo), (z_lo, v_hi)):
                            last = pe.matmul(out_bank[q % 2][:], a[s][:, c, q * P:(q + 1) * P], w[:, c, :],
                                             start=(m == 0), stop=(m == 3 * FC - 1))
                            m += 1
                    last.then_inc(out_done, 1)

                def batch(b, s, first):
                    for c in range(FC):
                        if not (first and c < 2):
                            hidden(b, c)
                        spread_weights(b, c)
                        if not first:
                            mix(b - 1, 1 - s, c)

                hidden(0, 0)
                hidden(0, 1)
                pe.wait_ge(g_ready, 1)
                for b in range(B):
                    if b:
                        pe.wait_ge(gT_done, b)
                    for q in range(QT):
                        last = pe.matmul(turn_bank[0:NS, q * P:(q + 1) * P], g[:, b * QT + q, :], st.ident[:],
                                         start=True, stop=True)
                    last.then_inc(g_turned, 1)
                pe.wait_ge(gT_done, B)
                pe.wait_ge(v_hi_done, 2 * FC)
                batch(0, 0, True)
                with pe.Fori(0, (B - 2) // 2) as j:
                    batch(2 * j + 1, 1, False)
                    batch(2 * j + 2, 0, False)
                batch(B - 1, 1, False)
                for q in range(QT):
                    mix(B - 1, 1, q)

            @block.scalar
            def _(act):
                act.sem_inc(hu_copied, 2)
                for c in range(FC):
                    act.activation(v_hi[:, c, :], v32[:, c, :], ACT.Copy).then_inc(v_hi_done, 1)
                for b in range(B):
                    act.wait_ge(scored, b + 1)
                    if b:
                        act.wait_ge(sc_turned, b)
                    act.activation(scT[:], sc_bank[0:NS, :], ACT.Copy).then_inc(sc_read, 1)
                act.wait_ge(aw_in, 1)
                act.activation(aw[:, 1, :], aw[:, 0, :], ACT.Exp, scale=-1.0).then_inc(aw_out, 1)
                act.wait_ge(e_in, 1)
                act.activation(e[:], e[:], ACT.Exp).then_inc(e_out, 1)
                for b in range(B):
                    act.wait_ge(g_turned, b + 1)
                    act.wait_ge(made, 6)
                    act.activation(gT_hi[0:NS, b * S:(b + 1) * S], turn_bank[0:NS, :], ACT.Copy).then_inc(gT_hi_done, 1)

                def copy_hidden(i, c):
                    act.wait_ge(hu_done, i + 1)
                    act.wait_ge(z_made, i + 1)
                    act.activation(hu[c % 2], hu_bank[c % 2][:], ACT.Copy).then_inc(hu_copied, 1)

                def two_batches(start):
                    for n in range(2 * FC):
                        i, s, c = start + n, n // FC, n % FC
                        act.wait_ge(z_made, i + 3)
                        act.activation(z_hi[s][:, c, :], z[c % 2], ACT.Copy).then_inc(z_hi_done, 1)
                        if not (isinstance(i, int) and i == B * FC - 1):
                            copy_hidden(i + 1, (c + 1) % FC)

                act.wait_ge(v_hi_done, 2 * FC)
                copy_hidden(0, 0)
                with act.Fori(0, B // 2 - 1) as j:
                    two_batches(2 * FC * j)
                two_batches((B - 2) * FC)

            @block.vector
            def _(dve):
                n_chain = [0]

                def link(ins):
                    n_chain[0] += 1
                    ins.then_inc(chain, 1)
                    dve.wait_ge(chain, n_chain[0])

                dve.sem_inc(z_made, 2)
                dve.sem_inc(x_ready, 2)
                link(dve.tensor_tensor(attr_b[:], attr_b[:], wa_b[:].to_broadcast([P, NS, AD]), ALU.mult))
                dve.tensor_reduce(aw[:, 0, :], attr_b[:], AX.X, ALU.add).then_inc(aw_in, 1)
                for c in range(FC):
                    dve.wait_ge(v_hi_done, FC)
                    dve.tensor_tensor(v_lo[:, c, :], v32[:, c, :], v_hi[:, c, :].bitcast(F32), ALU.subtract)\
                        .then_inc(v_hi_done, 1)
                for b in range(B):
                    dve.wait_ge(sc_turned, b + 1)
                    dve.tensor_copy(sc[:, b * QT:(b + 1) * QT, :],
                                    turn_bank[:, 0:QT * NS].rearrange("p (q s) -> p q s", q=QT)).then_inc(sc_taken, 1)
                dve.wait_ge(sc_taken, B)
                for t in range(T):
                    last = dve.max(top[:, t, :], sc[:, t, :])
                link(last)
                for t in range(T):
                    last = dve.max_index(idx[:, t, :], top[:, t, :], sc[:, t, :])
                link(last)
                full = [P, T, NS]
                dve.tensor_tensor(e[:], sc[:], top[:, :, 0:1].to_broadcast(full), ALU.subtract).then_inc(e_in, 1)
                link(dve.tensor_copy(idx_f[:], idx[:, :, 0:2]))
                dve.wait_ge(made, 6)
                dve.tensor_copy(spread_r[:], spread[:])
                dve.wait_ge(e_in, 1)
                numbers = number[:].to_broadcast(full)
                link(dve.tensor_tensor(first[:], numbers, idx_f[:, :, 0:1].to_broadcast(full), ALU.is_equal))
                link(dve.tensor_tensor(g[:], numbers, idx_f[:, :, 1:2].to_broadcast(full), ALU.is_equal))
                link(dve.tensor_tensor(g[:], g[:], first[:], ALU.add))
                dve.wait_ge(aw_out, 1)
                link(dve.tensor_scalar(aw[:, 1, :], aw[:, 1, :], 1.0, None, ALU.add))
                link(dve.reciprocal(aw[:, 2, :], aw[:, 1, :]))
                dve.wait_ge(e_out, 1)
                link(dve.tensor_reduce(den[:, 0, :], e[:], AX.X, ALU.add))
                link(dve.reciprocal(den[:, 1, :], den[:, 0, :]))
                link(dve.tensor_tensor(e[:], e[:], over(den, 1, full), ALU.mult))
                link(dve.tensor_tensor(g[:], g[:], e[:], ALU.mult))
                link(dve.tensor_reduce(den[:, 0, :], g[:], AX.X, ALU.add))
                link(dve.tensor_scalar(den[:, 0, :], den[:, 0, :], 1e-8, None, ALU.add))
                link(dve.reciprocal(den[:, 1, :], den[:, 0, :]))
                link(dve.tensor_tensor(g[:], g[:], over(den, 1, full), ALU.mult))
                link(dve.tensor_tensor(e[:], g[:], aw[:, 2:3, :].to_broadcast(full), ALU.mult))
                link(dve.tensor_reduce(den[:, 2, :], e[:], AX.X, ALU.add))
                link(dve.tensor_scalar(den[:, 3, :], den[:, 2, :], 0.2, 0.9, ALU.mult, ALU.add))
                dve.tensor_tensor(g[:], g[:], over(den, 3, full), ALU.mult).then_inc(g_ready, 1)
                for b in range(B):
                    dve.wait_ge(gT_hi_done, b + 1)
                    cols = slice(b * S, (b + 1) * S)
                    dve.tensor_tensor(gT_lo[0:NS, cols], turn_bank[0:NS, :], gT_hi[0:NS, cols].bitcast(F32), ALU.subtract)\
                        .then_inc(gT_done, 1)
                def batch(b, s, first):
                    for c in range(FC):
                        i = b * FC + c
                        dve.wait_ge(hu_copied, i + 3)
                        dve.wait_ge(spread_done, i + 1)
                        dve.tensor_tensor(z[c % 2], g_bank[c % 2][:], hu[c % 2], ALU.mult).then_inc(z_made, 1)
                        dve.wait_ge(z_hi_done, i + 1)
                        dve.tensor_tensor(z_lo[s][:, c, :], z[c % 2], z_hi[s][:, c, :].bitcast(F32), ALU.subtract)\
                            .then_inc(z_lo_done, 1)
                        if not first:
                            add(b - 1, c)

                def add(b, q):
                    dve.wait_ge(out_done, b * QT + q + 1)
                    xt = st.x[:, bass.ds(b * QT + q, 1), :].rearrange("p a d -> p (a d)")
                    dve.tensor_tensor(xt, out_bank[q % 2][:], xt, ALU.add).then_inc(x_ready, 1)

                batch(0, 0, True)
                with dve.Fori(0, (B - 2) // 2) as j:
                    batch(2 * j + 1, 1, False)
                    batch(2 * j + 2, 0, False)
                batch(B - 1, 1, False)
                for q in range(QT):
                    add(B - 1, q)

            @block.sync
            def _(sp):
                for b in range(B):
                    sp.wait_ge(x_ready, QT * (b + 1) + 2)
                    sp.dma_start(out[b].rearrange("(q p) d -> p q d", p=P), st.x[:, b * QT:(b + 1) * QT, :])\
                        .then_inc(stored, 16)
                sp.wait_ge(stored, 16 * B)


def over(rows, n, shape):
    return rows[:, n, :].rearrange("p (t a) -> p t a", a=1).to_broadcast(shape)


def cross_attention(st, ctx_in, mask, Wq, Wk, Wv, Wo):
    nc = st.nc
    HX = 128
    G = Wk.shape[1] // HX
    NR = Wq.shape[1] // HX // G
    NU = G * B
    LOW = -1e30
    scale = HX ** -0.5
    with ExitStack() as stack:
        sb, ps = tensors(nc, stack)
        ctxT_hi = sb("xa_ctxT_hi", [P, CC, TOK], F32R)
        ctxT_lo = sb("xa_ctxT_lo", [P, CC, TOK], F32R)
        load_context(st, ctx_in, ctxT_hi, ctxT_lo, [], [], "xa_prep")
        mask8 = sb("xa_mask8", [P, B, S], U8)
        mask_bias = sb("xa_mask_bias", [P, S], F32)
        PIECE = KC // 2 * NR * HX
        assert PIECE == 2 * CC * HX == D
        raw = [sb(f"xa_raw{n}", [P, PIECE], F32) for n in range(2)]
        kv_w = [sb(f"xa_kv_w{n}", [P, 2, CC, HX], F32R) for n in range(2)]
        q_w = [sb(f"xa_q_w{n}", [P, KC, NR * HX], F32R) for n in range(2)]
        o_w = [sb(f"xa_o_w{n}", [P, NR, D], F32R) for n in range(2)]
        k_hi = [sb(f"xa_k_hi{n}", [P, S], F32R) for n in range(2)]
        k_lo = [sb(f"xa_k_lo{n}", [P, S], F32R) for n in range(2)]
        vT = sb("xa_vT", [P, S], F32)
        v_hi = [sb(f"xa_v_hi{n}", [P, QT * HX], F32R) for n in range(2)]
        v_lo = [sb(f"xa_v_lo{n}", [P, QT * HX], F32R) for n in range(2)]
        q_hi = [sb(f"xa_q_hi{n}", [P, S], F32R) for n in range(NR)]
        q_lo = [sb(f"xa_q_lo{n}", [P, S], F32R) for n in range(NR)]
        nmax = sb("xa_nmax", [P, QT], F32)
        den = sb("xa_den", [P, NR, 3, QT], F32)
        prob = sb("xa_prob", [P, QT, S], F32)
        pT_hi = sb("xa_pT_hi", [P, QT - 1, S], F32R)
        pT_lo = sb("xa_pT_lo", [P, QT - 1, S], F32R)
        o_hi = sb("xa_o_hi", [P, S], F32R)
        o_lo = sb("xa_o_lo", [P, S], F32R)
        bank_a = ps("xa_bank_a", [P, 512])
        bank_b = ps("xa_bank_b", [P, 512])
        s_bank = [ps(f"xa_s_bank{n}", [P, S]) for n in range(2)]
        t_bank = [ps(f"xa_t_bank{n}", [P, S]) for n in range(2)]
        o_bank = ps("xa_o_bank", [P, S])
        out_bank = ps("xa_out_bank", [P, D])
        mask_in, mask_ready, maximum_next, rounding_next, raw_in_0, raw_in_1, split, weighed_first = st.sems(
            "mask_in", "mask_ready", "maximum_next", "rounding_next", "raw_in_0", "raw_in_1", "split", "weighed_first")
        k_done, k_hi_done, k_lo_done, vT_done, vT_copied, v_done, v_hi_done, v_lo_done, q_done, q_hi_done, \
            q_lo_done = st.sems("k_done", "k_hi_done", "k_lo_done", "vT_done", "vT_copied", "v_done", "v_hi_done",
                                "v_lo_done", "q_done", "q_hi_done", "q_lo_done")
        scored, maxed, exp_done, clamped, inverted, turned, pT_hi_done, pT_lo_done, weighed, o_hi_done, o_lo_done, \
            out_done, added = st.sems("scored", "maxed", "exp_done", "clamped", "inverted", "turned", "pT_hi_done",
                                      "pT_lo_done", "weighed", "o_hi_done", "o_lo_done", "out_done", "added")

        raw_in = (raw_in_0, raw_in_1)
        STAGING = (0, 1, 0, 1, 0)
        PIECES = len(STAGING)

        def products(pe, bank, pairs):
            for m, (w, x) in enumerate(pairs):
                last = pe.matmul(bank, w, x, start=(m == 0), stop=(m == len(pairs) - 1))
            return last

        def units(eng, unit):
            unit(0, 0)
            with eng.Fori(0, NU // 2 - 1) as j:
                unit(2 * j + 1, 1)
                unit(2 * j + 2, 0)
            unit(NU - 1, 1)

        def is_last(u):
            return isinstance(u, int) and u == NU - 1

        def is_first(u):
            return isinstance(u, int) and u == 0

        with nc.Block() as block:

            @block.sync
            def _(sp):
                def load(g):
                    for i, n in enumerate(STAGING):
                        before = g * PIECES + (-1, -2, 0, 1, 2)[i]
                        reached(sp, split, 2 * before + 2 if not (is_first(g) and i < 2) else 0)
                        if i == 0:
                            view = raw[n][:].rearrange("p (n c f) -> p n c f", n=2, c=CC)
                            for m, w in enumerate((Wk, Wv)):
                                sp.dma_start(view[:, m, :, :], w[:, bass.ds(g * HX, HX)]
                                             .rearrange("(c p) f -> p c f", p=P)).then_inc(raw_in[n], 16)
                        elif i < 3:
                            rows = slice((i - 1) * D // 2, i * D // 2)
                            sp.dma_start(raw[n][:].rearrange("p (c f) -> p c f", c=KC // 2),
                                         Wq[rows, bass.ds(g * NR * HX, NR * HX)].rearrange("(c p) f -> p c f", p=P))\
                                .then_inc(raw_in[n], 16)
                        else:
                            sp.dma_start(raw[n][:], Wo[bass.ds((g * NR + i - 3) * HX, HX), :]).then_inc(raw_in[n], 16)

                sp.dma_start(mask8[:].rearrange("p b s -> p (b s)"),
                             mask.rearrange("b s -> (b s)").rearrange("(o a) -> o a", o=1).to_broadcast([P, B * S]))\
                    .then_inc(mask_in, 16)
                load(0)
                with sp.Fori(1, G) as g:
                    load(g)

            @block.gpsimd
            def _(pool):
                def rounded(eng, hi, raw):
                    eng.sem_inc(rounding_next, 1)
                    return eng.tensor_copy(hi, raw)

                def split_weights(g):
                    loaded = ((64 * g + 32, 0), (32 * g + 16, 1), (64 * g + 48, 0), (32 * g + 32, 1), (64 * g + 64, 0))
                    for i, (count, n) in enumerate(loaded):
                        pool.wait_ge(raw_in[n], count)
                        if i == 0:
                            parts = [w[:].rearrange("p n c f -> p (n c f)") for w in kv_w]
                            reached(pool, k_done, B * g)
                            reached(pool, vT_done, B * g)
                        elif i < 3:
                            parts = [w[:, (i - 1) * KC // 2:i * KC // 2, :].rearrange("p c f -> p (c f)")
                                     for w in q_w]
                            reached(pool, q_done, NR * B * g)
                        else:
                            parts = [w[:, i - 3, :] for w in o_w]
                            reached(pool, out_done, QT * (NR * B * g - NR + i - 2) if not is_first(g) else 0)
                        rounded(pool, parts[0], raw[n][:]).then_inc(split, 1)
                        pool.wait_ge(split, 2 * (g * PIECES + i) + 1)
                        pool.tensor_tensor(parts[1], raw[n][:], parts[0].bitcast(F32), ALU.subtract)\
                            .then_inc(split, 1)

                split_weights(0)
                with pool.Fori(1, G) as g:
                    split_weights(g)

            @block.tensor
            def _(pe):
                def ctx_projection(u, bank, n):
                    cols = bass.ds(u % B * S, S)
                    return products(pe, bank[:], [(w[:, n, c, :], x[:, c, cols]) for c in range(CC)
                                                  for w, x in ((kv_w[0], ctxT_hi), (kv_w[0], ctxT_lo),
                                                               (kv_w[1], ctxT_hi))])

                def project_k(u):
                    pe.wait_ge(split, u // B * (2 * PIECES) + 2)
                    reached(pe, q_lo_done, 2 * u - 1)
                    ctx_projection(u, bank_a, 0).then_inc(k_done, 1)

                def project_vT(u):
                    pe.wait_ge(split, u // B * (2 * PIECES) + 2)
                    reached(pe, v_lo_done, u)
                    ctx_projection(u, bank_b, 1).then_inc(vT_done, 1)

                def turn_v(u):
                    pe.wait_ge(vT_copied, u + 1)
                    for q in range(QT):
                        last = pe.transpose(bank_b[:, q * HX:(q + 1) * HX], vT[:, q * P:(q + 1) * P], st.ident[:])
                    last.then_inc(v_done, 1)

                def project_q(u, r, part):
                    cols = bass.ds(u % B * S, S)
                    pairs = [(w[:, c, r * HX:(r + 1) * HX], x[:, c, cols]) for c in range(KC)
                             for w, x in ((q_w[0], st.xT_hi), (q_w[0], st.xT_lo), (q_w[1], st.xT_hi))]
                    if part:
                        for m in range(KC * part, KC * part + KC):
                            last = pe.matmul(bank_a[:], *pairs[m], start=False, stop=(m == 3 * KC - 1))
                        if part == 2:
                            last.then_inc(q_done, 1)
                        return
                    pe.wait_ge(split, u // B * (2 * PIECES) + 6)
                    if r == 0:
                        pe.wait_ge(k_lo_done, u + 1)
                        reached(pe, q_lo_done, 2 * u)
                    else:
                        pe.wait_ge(k_lo_done, NU if is_last(u) else u + 2)
                    for m in range(KC):
                        pe.matmul(bank_a[:], *pairs[m], start=(m == 0), stop=False)

                def score(u, s, r, q):
                    n = NR * u + r
                    if q == 0:
                        pe.wait_ge(q_lo_done, n + 1)
                    reached(pe, maxed, QT * n + q - 1)
                    tile = slice(q * P, (q + 1) * P)
                    products(pe, s_bank[q % 2][:], [(q_hi[r][:, tile], k_hi[s][:]), (q_hi[r][:, tile], k_lo[s][:]),
                                                    (q_lo[r][:, tile], k_hi[s][:])]).then_inc(scored, 1)

                def turn_probabilities(u, r, kt):
                    n = NR * u + r
                    pe.wait_ge(exp_done, QT * n + QT)
                    reached(pe, pT_lo_done, QT * n + kt - 1)
                    for q in range(QT):
                        last = pe.transpose(t_bank[kt % 2][:, q * P:(q + 1) * P], prob[:, q, kt * P:(kt + 1) * P],
                                            st.ident[:])
                    last.then_inc(turned, 1)

                def weigh(u, s, r, kt):
                    n = NR * u + r
                    pe.wait_ge(pT_lo_done, QT * n + kt + 1)
                    if kt == 0:
                        reached(pe, o_lo_done, n)
                        pe.wait_ge(v_lo_done, u + 1)
                    keys = slice(kt * HX, (kt + 1) * HX)
                    for m, (v, p_) in enumerate(((v_hi, pT_hi), (v_hi, pT_lo), (v_lo, pT_hi))):
                        last = pe.matmul(o_bank[:], v[s][:, keys], p_[:, kt % (QT - 1), :], start=(kt == 0 and m == 0),
                                         stop=(kt == QT - 1 and m == 2))
                    if kt == 0:
                        last.then_inc(weighed_first, 1)
                    if kt == QT - 1:
                        last.then_inc(weighed, 1)

                def project_out(n, r, q):
                    pe.wait_ge(o_lo_done, n + 1)
                    pe.wait_ge(split, n // (NR * B) * (2 * PIECES) + 8 + 2 * r)
                    reached(pe, added, QT * n + q)
                    tile = slice(q * P, (q + 1) * P)
                    products(pe, out_bank[:], [(o_hi[:, tile], o_w[0][:, r, :]), (o_hi[:, tile], o_w[1][:, r, :]),
                                               (o_lo[:, tile], o_w[0][:, r, :])]).then_inc(out_done, 1)

                def unit(u, s):
                    for r in range(NR):
                        n = NR * u + r

                        def out(q):
                            if not (is_first(u) and r == 0):
                                project_out(n - 1, 1 - r, q)

                        def next_q(part):
                            if r == 0:
                                project_q(u, 1, part)
                            elif not is_last(u):
                                project_q(u + 1, 0, part)

                        def next_score(q):
                            if r == 0:
                                score(u, s, 1, q)
                            elif not is_last(u):
                                score(u + 1, 1 - s, 0, q)

                        score(u, s, r, 2)
                        score(u, s, r, 3)
                        if r == 0:
                            if not is_last(u):
                                project_k(u + 1)
                            out(0)
                            if not is_last(u):
                                project_vT(u + 1)
                            out(1)
                            next_q(0)
                            next_q(1)
                            out(2)
                            next_q(2)
                            turn_probabilities(u, r, 0)
                            out(3)
                            turn_probabilities(u, r, 1)
                            next_score(0)
                            turn_probabilities(u, r, 2)
                            weigh(u, s, r, 0)
                            turn_probabilities(u, r, 3)
                            next_score(1)
                            weigh(u, s, r, 1)
                            weigh(u, s, r, 2)
                        else:
                            next_q(0)
                            out(0)
                            next_q(1)
                            out(1)
                            next_q(2)
                            if not is_last(u):
                                turn_v(u + 1)
                            out(2)
                            turn_probabilities(u, r, 0)
                            turn_probabilities(u, r, 1)
                            out(3)
                            turn_probabilities(u, r, 2)
                            weigh(u, s, r, 0)
                            turn_probabilities(u, r, 3)
                            weigh(u, s, r, 1)
                            next_score(0)
                            weigh(u, s, r, 2)
                            next_score(1)
                        weigh(u, s, r, 3)

                project_k(0)
                project_vT(0)
                turn_v(0)
                for part in range(3):
                    project_q(0, 0, part)
                score(0, 0, 0, 0)
                score(0, 0, 0, 1)
                units(pe, unit)
                for q in range(QT):
                    project_out(NR * NU - 1, 1, q)

            @block.scalar
            def _(act):
                def take_k(u, s):
                    act.wait_ge(k_done, u + 1)
                    reached(act, scored, NR * QT * (u - 1))
                    act.activation(k_hi[s][:], bank_a[:], ACT.Copy).then_inc(k_hi_done, 1)

                def take_vT(u):
                    act.wait_ge(vT_done, u + 1)
                    reached(act, v_done, u)
                    act.activation(vT[:], bank_b[:], ACT.Copy).then_inc(vT_copied, 1)

                def take_v(u, s):
                    act.wait_ge(v_done, u + 1)
                    reached(act, weighed, NR * (u - 1))
                    act.activation(v_hi[s][:], bank_b[:], ACT.Copy).then_inc(v_hi_done, 1)

                def take_q(u, r):
                    n = NR * u + r
                    act.wait_ge(q_done, n + 1)
                    reached(act, scored, QT * (n - 1))
                    act.activation(q_hi[r][:], bank_a[:], ACT.Copy).then_inc(q_hi_done, 1)

                def take_pT(u, r, kt):
                    n = NR * u + r
                    act.wait_ge(turned, QT * n + kt + 1)
                    reached(act, weighed, n)
                    if kt == QT - 1:
                        act.wait_ge(weighed_first, n + 1)
                    act.activation(pT_hi[:, kt % (QT - 1), :], t_bank[kt % 2][:], ACT.Copy).then_inc(pT_hi_done, 1)

                def take_o(n):
                    act.wait_ge(weighed, n + 1)
                    reached(act, out_done, QT * n)
                    act.activation(o_hi[:], o_bank[:], ACT.Copy).then_inc(o_hi_done, 1)

                def exponential(u, r, q):
                    n = NR * u + r
                    act.wait_ge(maxed, QT * n + q + 1)
                    reached(act, clamped, n - 1)
                    act.activation(prob[:, q, :], prob[:, q, :], ACT.Exp, bias=nmax[:, q:q + 1], scale=-1.0,
                                   accum_out=den[:, r, 0, q:q + 1]).then_inc(exp_done, 1)

                def unit(u, s):
                    for r in range(NR):
                        n = NR * u + r
                        if r == 0:
                            if not is_last(u):
                                take_k(u + 1, 1 - s)
                            exponential(u, r, 2)
                            exponential(u, r, 3)
                            if not is_last(u):
                                take_vT(u + 1)
                            take_q(u, 1)
                        else:
                            exponential(u, r, 2)
                            exponential(u, r, 3)
                            if not is_last(u):
                                take_q(u + 1, 0)
                                take_v(u + 1, 1 - s)
                        for kt in range(QT):
                            take_pT(u, r, kt)
                        if r == 0:
                            exponential(u, 1, 0)
                            take_o(n)
                            exponential(u, 1, 1)
                        else:
                            take_o(n)
                            if not is_last(u):
                                exponential(u + 1, 0, 0)
                                exponential(u + 1, 0, 1)

                take_k(0, 0)
                take_vT(0)
                take_v(0, 0)
                take_q(0, 0)
                exponential(0, 0, 0)
                exponential(0, 0, 1)
                units(act, unit)

            @block.vector
            def _(dve):
                def take_lo(hi_done, count, lo, bank, hi, lo_done):
                    dve.wait_ge(hi_done, count)
                    dve.tensor_tensor(lo, bank, hi.bitcast(F32), ALU.subtract).then_inc(lo_done, 1)

                def take_k(u, s):
                    take_lo(k_hi_done, u + 1, k_lo[s][:], bank_a[:], k_hi[s][:], k_lo_done)

                def take_v(u, s):
                    take_lo(v_hi_done, u + 1, v_lo[s][:], bank_b[:], v_hi[s][:], v_lo_done)

                def take_q(u, r):
                    take_lo(q_hi_done, NR * u + r + 1, q_lo[r][:], bank_a[:], q_hi[r][:], q_lo_done)

                def maximum(u, r, q):
                    n = NR * u + r
                    dve.wait_ge(scored, QT * n + q + 1)
                    reached(dve, turned, QT * n)
                    dve.wait_ge(mask_ready, u + 1)
                    dve.sem_inc(maximum_next, 1)
                    dve.tensor_tensor_reduce(prob[:, q, :], s_bank[q % 2][:], mask_bias[:], -scale, -LOW * 1e-5,
                                             ALU.add, ALU.min, nmax[:, q:q + 1]).then_inc(maxed, 1)

                def bias_of(u):
                    reached(dve, maxed, NR * QT * u)
                    dve.tensor_scalar(mask_bias[:], mask8[:, bass.ds(u % B, 1), :].rearrange("p a s -> p (a s)"),
                                      -LOW, LOW, ALU.mult, ALU.add).then_inc(mask_ready, 1)

                def take_pT(u, r, kt):
                    slot = kt % (QT - 1)
                    take_lo(pT_hi_done, QT * (NR * u + r) + kt + 1, pT_lo[:, slot, :], t_bank[kt % 2][:],
                            pT_hi[:, slot, :], pT_lo_done)

                def add(n, r, q):
                    dve.wait_ge(out_done, QT * n + q + 1)
                    xt = st.x[:, bass.ds(n // NR % B * QT + q, 1), :].rearrange("p a d -> p (a d)")
                    dve.scalar_tensor_tensor(xt, out_bank[:], den[:, r, 2, q:q + 1], xt, ALU.mult, ALU.add)\
                        .then_inc(added, 1)

                def unit(u, s):
                    for r in range(NR):
                        n = NR * u + r

                        def add_last(q):
                            if not (is_first(u) and r == 0):
                                add(n - 1, 1 - r, q)

                        maximum(u, r, 2)
                        maximum(u, r, 3)
                        add_last(0)
                        if r == 0 and not is_last(u):
                            take_k(u + 1, 1 - s)
                        invert_sum(n, r)
                        add_last(1)
                        if r == 0:
                            add_last(2)
                            take_q(u, 1)
                            take_pT(u, r, 0)
                            take_pT(u, r, 1)
                            add_last(3)
                            take_pT(u, r, 2)
                            maximum(u, 1, 0)
                            take_pT(u, r, 3)
                            maximum(u, 1, 1)
                        else:
                            if not is_last(u):
                                take_q(u + 1, 0)
                            add_last(2)
                            take_pT(u, r, 0)
                            if not is_last(u):
                                take_v(u + 1, 1 - s)
                            take_pT(u, r, 1)
                            take_pT(u, r, 2)
                            add_last(3)
                            take_pT(u, r, 3)
                            if not is_last(u):
                                bias_of(u + 1)
                                maximum(u + 1, 0, 0)
                                maximum(u + 1, 0, 1)
                        take_lo(o_hi_done, n + 1, o_lo[:], o_bank[:], o_hi[:], o_lo_done)
                        dve.wait_ge(inverted, n + 1)

                def invert_sum(n, r):
                    dve.wait_ge(exp_done, QT * n + QT)
                    dve.tensor_scalar(den[:, r, 1, :], den[:, r, 0, :], 1e-30, None, ALU.max).then_inc(clamped, 1)
                    dve.wait_ge(clamped, n + 1)
                    dve.reciprocal(den[:, r, 2, :], den[:, r, 1, :]).then_inc(inverted, 1)

                dve.wait_ge(mask_in, 16)
                take_k(0, 0)
                take_v(0, 0)
                take_q(0, 0)
                bias_of(0)
                maximum(0, 0, 0)
                maximum(0, 0, 1)
                units(dve, unit)
                for q in range(QT):
                    add(NR * NU - 1, 1, q)


_INS = ["x", "ctx_1024", "mask_BxS2_bf1", "L0_attn_Wq_w", "L0_attn_Wq_b", "L0_attn_Wk_w", "L0_attn_Wk_b",
        "L0_attn_Wv_w", "L0_attn_Wv_b", "L0_xattn_Wq", "L0_xattn_bq", "L0_xattn_Wk", "L0_xattn_bk",
        "L0_ffn_gate_up_packed", "L0_ffn_gate_up_scales", "L0_ffn_down_packed", "L0_ffn_down_scales",
        "L1_attn_Wqkv_w", "L1_attn_Wqkv_b", "L1_attn_out_w", "L1_attn_out_b", "L1_xattn_Wq", "L1_xattn_Wk",
        "L1_xattn_Wv", "L1_xattn_Wo", "L1_ffn_Wr", "L1_ffn_U", "L1_ffn_V", "L1_ffn_attr", "L1_ffn_Wa"]
_OUTS = [((B, S, D), "float32")]


def decoder(nc, x, ctx_in, mask, l0_Wq, l0_bq, l0_Wk, l0_bk, l0_Wv, l0_bv, x0_Wq, x0_bq, x0_Wk, x0_bk,
            gate_up_packed, gate_up_scales, down_packed, down_scales, Wqkv, bqkv, out_w, out_b, x1_Wq, x1_Wk,
            x1_Wv, x1_Wo, Wr, U, V, attr, Wa, out):
    with ExitStack() as ctx:
        st = State(nc, ctx)
        persistent(st)
        st.stage(setup, x)
        st.stage(layer0_attention, l0_Wq, l0_bq, l0_Wk, l0_bk, l0_Wv, l0_bv)
        st.stage(feature_attention, ctx_in, x0_Wq, x0_bq, x0_Wk, x0_bk)
        st.stage(packed_ffn, gate_up_packed, gate_up_scales, down_packed, down_scales)
        st.stage(layer1_attention, Wqkv, bqkv, out_w, out_b)
        st.stage(cross_attention, ctx_in, mask, x1_Wq, x1_Wk, x1_Wv, x1_Wo)
        st.stage(routed_mixture, Wr, U, V, attr, Wa, out)


def kernel(**inputs):
    import numpy as _np
    import concourse.bacc as _bacc
    from concourse import mybir as _mybir
    from concourse.bass_utils import run_bass_kernel_spmd as _run

    nc = _bacc.Bacc("TRN2", target_bir_lowering=False, num_devices=1)
    arrays, args = {}, []
    for name in _INS:
        a = _np.ascontiguousarray(inputs[name])
        arrays[f"in_{name}_dram"] = a
        args.append(nc.dram_tensor(f"in_{name}_dram", a.shape, _mybir.dt.from_np(a.dtype), kind="ExternalInput").ap())
    for i, (shape, dtype) in enumerate(_OUTS):
        dt = _mybir.dt.from_np(_np.dtype(dtype))
        args.append(nc.dram_tensor(f"out_{i}_dram", shape, dt, kind="ExternalOutput").ap())
    decoder(nc, *args)
    r = _run(nc, [arrays], core_ids=[0])
    return r.results[0]["out_0_dram"]
```
